# Optimizing a Trainium2 kernel written in Bass

```python
import numpy as np
import jax
import jax.numpy as jnp

def _softmax(x, axis=-1):
    return jax.nn.softmax(x, axis=axis)

def _gelu(x):
    return jax.nn.gelu(x, approximate=True)

def _silu(x):
    return jax.nn.silu(x)

def _sigmoid(x):
    return jax.nn.sigmoid(x)

def _layernorm(x, axis=-1, eps=1e-05):
    m = jnp.mean(x, axis=axis, keepdims=True)
    v = jnp.var(x, axis=axis, keepdims=True)
    return (x - m) / jnp.sqrt(v + eps)

def _scatter_add(tgt, idx, src, axis=0):
    return tgt.at[idx].add(src)

def _segment_sum(src, seg, n):
    return jax.ops.segment_sum(src, seg, n)
kernel_name = 'mk_early_fusion_embed_d2_tok_img512_r4_fa8ffd'

def setup_inputs(seed: int=0):
    np.random.seed(seed)
    _w = jnp.asarray

    def _rec_inputs():
        import jax
        import jax.numpy as jnp
        _rk = jax.random.key(seed)
        x = -0.000147625 + 0.999875 * jax.random.normal(jax.random.fold_in(_rk, 1), (64, 3, 224, 224), jnp.float32)
        x_txt = jax.random.randint(jax.random.fold_in(_rk, 51), (64, 128), 0, 125, jnp.int32)
        return (x, x_txt)
    x, x_txt = _rec_inputs()

    def _L0_tok_setup():
        import jax, jax.numpy as jnp
        import numpy as np
        N_PATCHES = 8
        PATCH = 28
        C = 3
        IN_D = C * PATCH * PATCH
        HID = 128
        SEQ = N_PATCHES * N_PATCHES + 1

        def _positional_embedding(seq_len, dim):
            i = np.arange(seq_len)[:, None].astype(np.float32)
            j = np.arange(dim)[None, :].astype(np.float32)
            ang = i / np.power(100000.0, j / dim)
            pe = np.where(j % 2 == 0, np.sin(ang), np.cos(ang))
            return jnp.asarray(pe, dtype=jnp.float32)
        key = jax.random.key(seed)
        k1, k2, k3, k4 = jax.random.split(key, 4)
        B = 64
        X = jax.random.normal(k1, (B, C, 224, 224), dtype=jnp.float32)
        bound = 1.0 / np.sqrt(IN_D)
        W = jax.random.uniform(k2, (HID, IN_D), minval=-bound, maxval=bound, dtype=jnp.float32)
        b = jax.random.uniform(k3, (HID,), minval=-bound, maxval=bound, dtype=jnp.float32)
        class_token = jax.random.uniform(k4, (1, HID), dtype=jnp.float32)
        pos_embed = _positional_embedding(SEQ, HID)
        return {'X': X, 'W': W, 'b': b, 'class_token': class_token, 'pos_embed': pos_embed}
    _L0_tok_all = _L0_tok_setup()
    _L0_tok_in = {k: v for k, v in _L0_tok_all.items() if k in ('W', 'b', 'class_token', 'pos_embed')}
    del _L0_tok_all

    def _L0_txt_setup():
        import jax, jax.numpy as jnp
        import numpy as np
        QMAX = 127.0
        CTX = 2

        def fake_quant(w):
            scale = jnp.max(jnp.abs(w)) / QMAX
            wq = jnp.round(w / scale) * scale
            return w + jax.lax.stop_gradient(wq - w)
        key = jax.random.key(seed)
        k1, k2, k3 = jax.random.split(key, 3)
        y = jax.random.randint(k1, (64, 512), 0, 125, dtype=jnp.int64)
        emb_weight = jax.random.normal(k2, (125, 128), dtype=jnp.float32)
        conv_weight = jax.random.normal(k3, (128, 1, 2), dtype=jnp.float32)
        return {'y': y, 'emb_weight': emb_weight, 'conv_weight': conv_weight}
    _L0_txt_all = _L0_txt_setup()
    _L0_txt_in = {k: v for k, v in _L0_txt_all.items() if k in ('emb_weight', 'conv_weight')}
    del _L0_txt_all

    def _L0_attn_setup():
        import jax, jax.numpy as jnp
        import numpy as np
        B, L, C = (2, 256, 128)
        H, P = (8, 4)
        D = C // H
        LN_EPS = 1e-05

        def _layernorm(x, g, b):
            mu = jnp.mean(x, axis=-1, keepdims=True)
            var = jnp.mean((x - mu) ** 2, axis=-1, keepdims=True)
            return (x - mu) * jax.lax.rsqrt(var + LN_EPS) * g + b
        key = jax.random.key(seed)
        ks = jax.random.split(key, 12)
        s = 0.02
        inp = {'features': jax.random.normal(ks[0], (B, L, C), jnp.float32), 'coords': jax.random.normal(ks[1], (B, L, 3), jnp.float32), 'ln_g': jnp.ones((C,), jnp.float32), 'ln_b': jnp.zeros((C,), jnp.float32), 'wq': jax.random.normal(ks[2], (C, C), jnp.float32) * s, 'bq': jnp.zeros((C,), jnp.float32), 'wk': jax.random.normal(ks[3], (C, C), jnp.float32) * s, 'bk': jnp.zeros((C,), jnp.float32), 'wv': jax.random.normal(ks[4], (C, C), jnp.float32) * s, 'bv': jnp.zeros((C,), jnp.float32), 'wqp': jax.random.normal(ks[5], (C, H * P * 3), jnp.float32) * s, 'bqp': jnp.zeros((H * P * 3,), jnp.float32), 'wkp': jax.random.normal(ks[6], (C, H * P * 3), jnp.float32) * s, 'bkp': jnp.zeros((H * P * 3,), jnp.float32), 'wvp': jax.random.normal(ks[7], (C, H * P * 3), jnp.float32) * s, 'bvp': jnp.zeros((H * P * 3,), jnp.float32), 'wo': jax.random.normal(ks[8], (C, C), jnp.float32) * s, 'bo': jnp.zeros((C,), jnp.float32), 'pscale': jnp.full((H,), 1.0 / np.sqrt(P), jnp.float32)}
        return inp
    _L0_attn_all = _L0_attn_setup()
    _L0_attn_in = {k: v for k, v in _L0_attn_all.items() if k in ('coords', 'ln_g', 'ln_b', 'wq', 'bq', 'wk', 'bk', 'wv', 'bv', 'wqp', 'bqp', 'wkp', 'bkp', 'wvp', 'bvp', 'wo', 'bo', 'pscale')}
    del _L0_attn_all

    def _L0_ffn_setup():
        import jax, jax.numpy as jnp
        import numpy as np
        E = 64
        K = 2
        D = 128
        H = 64
        NSH = 2
        ROUTE_SCALE = 2.5
        CAP = 256
        STD = 0.02
        key = jax.random.key(seed)
        ks = jax.random.split(key, 8)
        x = jax.random.normal(ks[0], (4, 512, D), dtype=jnp.float32)
        gate_w = jax.random.normal(ks[1], (E, D), dtype=jnp.float32) * STD
        w1 = jax.random.normal(ks[2], (E, D, H), dtype=jnp.float32) * STD
        w3 = jax.random.normal(ks[3], (E, D, H), dtype=jnp.float32) * STD
        w2 = jax.random.normal(ks[4], (E, H, D), dtype=jnp.float32) * STD
        sw1 = jax.random.normal(ks[5], (D, H * NSH), dtype=jnp.float32) * STD
        sw3 = jax.random.normal(ks[6], (D, H * NSH), dtype=jnp.float32) * STD
        sw2 = jax.random.normal(ks[7], (H * NSH, D), dtype=jnp.float32) * STD
        return {'x': x, 'gate_w': gate_w, 'w1': w1, 'w3': w3, 'w2': w2, 'sw1': sw1, 'sw3': sw3, 'sw2': sw2}
    _L0_ffn_all = _L0_ffn_setup()
    _L0_ffn_in = {k: v for k, v in _L0_ffn_all.items() if k in ('gate_w', 'w1', 'w3', 'w2', 'sw1', 'sw3', 'sw2')}
    del _L0_ffn_all

    def _L1_attn_setup():
        import jax, jax.numpy as jnp
        import numpy as np

        def _hippo_dplr(n):
            pr = np.sqrt(1.0 + 2.0 * np.arange(n))
            A = -(np.tril(pr[:, None] * pr[None, :]) - np.diag(np.arange(n)))
            p = np.sqrt(np.arange(n) + 0.5)
            b = np.sqrt(2.0 * np.arange(n) + 1.0)
            S = A + p[:, None] * p[None, :]
            lam_re = np.full(n, np.mean(np.diagonal(S)))
            lam_im, V = np.linalg.eigh(S * -1j)
            p_c = V.conj().T @ p.astype(np.complex128)
            b_c = V.conj().T @ b.astype(np.complex128)
            return (lam_re, lam_im, p_c, b_c)
        B, L, H, N = (4, 256, 128, 64)
        key = jax.random.key(seed)
        kx, kc, ks, k1, k2 = jax.random.split(key, 5)
        lam_re, lam_im, p_c, b_c = _hippo_dplr(N)
        c = jax.random.normal(kc, (N, 2)) * 0.5 ** 0.5
        f32 = lambda a: jnp.asarray(a, dtype=jnp.float32)
        return {'x': jax.random.normal(kx, (B, L, H), dtype=jnp.float32), 'norm_weight': jnp.ones((H,), jnp.float32), 'norm_bias': jnp.zeros((H,), jnp.float32), 'lambda_re': f32(lam_re), 'lambda_im': f32(lam_im), 'p_re': f32(p_c.real), 'p_im': f32(p_c.imag), 'b_re': f32(b_c.real), 'b_im': f32(b_c.imag), 'c_re': c[:, 0].astype(jnp.float32), 'c_im': c[:, 1].astype(jnp.float32), 'd': jnp.ones((), jnp.float32), 'log_step': jax.random.uniform(ks, (), jnp.float32, float(np.log(0.001)), float(np.log(0.1))), 'out_w': (jax.random.normal(k1, (H, H), jnp.float32) / np.sqrt(H)).astype(jnp.float32), 'out_b': jnp.zeros((H,), jnp.float32), 'out2_w': (jax.random.normal(k2, (H, H), jnp.float32) / np.sqrt(H)).astype(jnp.float32), 'out2_b': jnp.zeros((H,), jnp.float32)}
    _L1_attn_all = _L1_attn_setup()
    _L1_attn_in = {k: v for k, v in _L1_attn_all.items() if k in ('norm_weight', 'norm_bias', 'lambda_re', 'lambda_im', 'p_re', 'p_im', 'b_re', 'b_im', 'c_re', 'c_im', 'd', 'log_step', 'out_w', 'out_b', 'out2_w', 'out2_b')}
    del _L1_attn_all

    def _L1_ffn_setup():
        import jax, jax.numpy as jnp
        import numpy as np
        B, S, D, H, E, K = (2, 512, 128, 256, 8, 2)

        def _moe(x, router_w, w_gate, w_up, w_down):
            bsz, seq, d = x.shape
            flat = x.reshape(-1, d)
            logits = flat @ router_w.T
            topk_vals, topk_idx = jax.lax.top_k(logits, K)
            topk_w = jax.nn.softmax(topk_vals, axis=-1)
            s = flat.shape[0]
            dense_w = jnp.zeros((s, E), dtype=flat.dtype).at[jnp.arange(s)[:, None], topk_idx].add(topk_w)
            g = jnp.einsum('sd,edh->esh', flat, w_gate)
            u = jnp.einsum('sd,edh->esh', flat, w_up)
            y = jnp.einsum('esh,ehd->esd', jax.nn.silu(g) * u, w_down)
            out = jnp.einsum('esd,se->sd', y, dense_w)
            return out.reshape(bsz, seq, d)
        key = jax.random.key(seed)
        k1, k2, k3, k4, k5 = jax.random.split(key, 5)
        return {'x': jax.random.normal(k1, (B, S, D), dtype=jnp.float32), 'router_w': jax.random.normal(k2, (E, D), dtype=jnp.float32) * D ** (-0.5), 'w_gate': jax.random.normal(k3, (E, D, H), dtype=jnp.float32) * D ** (-0.5), 'w_up': jax.random.normal(k4, (E, D, H), dtype=jnp.float32) * D ** (-0.5), 'w_down': jax.random.normal(k5, (E, H, D), dtype=jnp.float32) * H ** (-0.5)}
    _L1_ffn_all = _L1_ffn_setup()
    _L1_ffn_in = {k: v for k, v in _L1_ffn_all.items() if k in ('router_w', 'w_gate', 'w_up', 'w_down')}
    del _L1_ffn_all
    return {'x': x, 'x_txt': x_txt, 'L0_tok_W': _L0_tok_in['W'], 'L0_tok_b': _L0_tok_in['b'], 'L0_tok_class_token': _L0_tok_in['class_token'], 'L0_tok_pos_embed': _L0_tok_in['pos_embed'], 'L0_txt_emb_weight': _L0_txt_in['emb_weight'], 'L0_txt_conv_weight': _L0_txt_in['conv_weight'], 'L0_attn_coords': _L0_attn_in['coords'], 'L0_attn_ln_g': _L0_attn_in['ln_g'], 'L0_attn_ln_b': _L0_attn_in['ln_b'], 'L0_attn_wq': _L0_attn_in['wq'], 'L0_attn_bq': _L0_attn_in['bq'], 'L0_attn_wk': _L0_attn_in['wk'], 'L0_attn_bk': _L0_attn_in['bk'], 'L0_attn_wv': _L0_attn_in['wv'], 'L0_attn_bv': _L0_attn_in['bv'], 'L0_attn_wqp': _L0_attn_in['wqp'], 'L0_attn_bqp': _L0_attn_in['bqp'], 'L0_attn_wkp': _L0_attn_in['wkp'], 'L0_attn_bkp': _L0_attn_in['bkp'], 'L0_attn_wvp': _L0_attn_in['wvp'], 'L0_attn_bvp': _L0_attn_in['bvp'], 'L0_attn_wo': _L0_attn_in['wo'], 'L0_attn_bo': _L0_attn_in['bo'], 'L0_attn_pscale': _L0_attn_in['pscale'], 'L0_ffn_gate_w': _L0_ffn_in['gate_w'], 'L0_ffn_w1': _L0_ffn_in['w1'], 'L0_ffn_w3': _L0_ffn_in['w3'], 'L0_ffn_w2': _L0_ffn_in['w2'], 'L0_ffn_sw1': _L0_ffn_in['sw1'], 'L0_ffn_sw3': _L0_ffn_in['sw3'], 'L0_ffn_sw2': _L0_ffn_in['sw2'], 'L1_attn_norm_weight': _L1_attn_in['norm_weight'], 'L1_attn_norm_bias': _L1_attn_in['norm_bias'], 'L1_attn_lambda_re': _L1_attn_in['lambda_re'], 'L1_attn_lambda_im': _L1_attn_in['lambda_im'], 'L1_attn_p_re': _L1_attn_in['p_re'], 'L1_attn_p_im': _L1_attn_in['p_im'], 'L1_attn_b_re': _L1_attn_in['b_re'], 'L1_attn_b_im': _L1_attn_in['b_im'], 'L1_attn_c_re': _L1_attn_in['c_re'], 'L1_attn_c_im': _L1_attn_in['c_im'], 'L1_attn_d': _L1_attn_in['d'], 'L1_attn_log_step': _L1_attn_in['log_step'], 'L1_attn_out_w': _L1_attn_in['out_w'], 'L1_attn_out_b': _L1_attn_in['out_b'], 'L1_attn_out2_w': _L1_attn_in['out2_w'], 'L1_attn_out2_b': _L1_attn_in['out2_b'], 'L1_ffn_router_w': _L1_ffn_in['router_w'], 'L1_ffn_w_gate': _L1_ffn_in['w_gate'], 'L1_ffn_w_up': _L1_ffn_in['w_up'], 'L1_ffn_w_down': _L1_ffn_in['w_down']}

def reference(x, x_txt, L0_tok_W, L0_tok_b, L0_tok_class_token, L0_tok_pos_embed, L0_txt_emb_weight, L0_txt_conv_weight, L0_attn_coords, L0_attn_ln_g, L0_attn_ln_b, L0_attn_wq, L0_attn_bq, L0_attn_wk, L0_attn_bk, L0_attn_wv, L0_attn_bv, L0_attn_wqp, L0_attn_bqp, L0_attn_wkp, L0_attn_bkp, L0_attn_wvp, L0_attn_bvp, L0_attn_wo, L0_attn_bo, L0_attn_pscale, L0_ffn_gate_w, L0_ffn_w1, L0_ffn_w3, L0_ffn_w2, L0_ffn_sw1, L0_ffn_sw3, L0_ffn_sw2, L1_attn_norm_weight, L1_attn_norm_bias, L1_attn_lambda_re, L1_attn_lambda_im, L1_attn_p_re, L1_attn_p_im, L1_attn_b_re, L1_attn_b_im, L1_attn_c_re, L1_attn_c_im, L1_attn_d, L1_attn_log_step, L1_attn_out_w, L1_attn_out_b, L1_attn_out2_w, L1_attn_out2_b, L1_ffn_router_w, L1_ffn_w_gate, L1_ffn_w_up, L1_ffn_w_down):
    import jax
    import jax.numpy as jnp

    def _L0_tok_ref(X, W, b, class_token, pos_embed):
        import jax, jax.numpy as jnp
        import numpy as np
        N_PATCHES = 8
        PATCH = 28
        C = 3
        IN_D = C * PATCH * PATCH
        HID = 128
        SEQ = N_PATCHES * N_PATCHES + 1

        def _positional_embedding(seq_len, dim):
            i = np.arange(seq_len)[:, None].astype(np.float32)
            j = np.arange(dim)[None, :].astype(np.float32)
            ang = i / np.power(100000.0, j / dim)
            pe = np.where(j % 2 == 0, np.sin(ang), np.cos(ang))
            return jnp.asarray(pe, dtype=jnp.float32)
        B = X.shape[0]
        patches = X.reshape(B, C, N_PATCHES, PATCH, N_PATCHES, PATCH)
        patches = patches.transpose(0, 2, 4, 1, 3, 5).reshape(B, N_PATCHES * N_PATCHES, IN_D)
        tokens = jnp.einsum('bpi,hi->bph', patches, W) + b
        cls = jnp.broadcast_to(class_token[None, :, :], (B, 1, HID))
        tokens = jnp.concatenate([cls, tokens], axis=1)
        return tokens * pos_embed[None, :, :]

    def _L0_txt_ref(y, emb_weight, conv_weight):
        import jax, jax.numpy as jnp
        import numpy as np
        QMAX = 127.0
        CTX = 2

        def fake_quant(w):
            scale = jnp.max(jnp.abs(w)) / QMAX
            wq = jnp.round(w / scale) * scale
            return w + jax.lax.stop_gradient(wq - w)
        w_emb = fake_quant(emb_weight)
        e = w_emb[jnp.clip(y, 0)]
        e = e * (y >= 0)[..., None].astype(e.dtype)
        x = jnp.pad(e, ((0, 0), (CTX - 1, 0), (0, 0)))
        D = conv_weight.shape[0]
        w = fake_quant(conv_weight).transpose(2, 1, 0)
        out = jax.lax.conv_general_dilated(x, w, window_strides=(1,), padding='VALID', feature_group_count=D, dimension_numbers=('NWC', 'WIO', 'NWC'))
        return jax.nn.relu(out)

    def _L0_attn_ref(features, coords, ln_g, ln_b, wq, bq, wk, bk, wv, bv, wqp, bqp, wkp, bkp, wvp, bvp, wo, bo, pscale):
        import jax, jax.numpy as jnp
        import numpy as np
        B, L, C = (2, 256, 128)
        H, P = (8, 4)
        D = C // H
        LN_EPS = 1e-05

        def _layernorm(x, g, b):
            mu = jnp.mean(x, axis=-1, keepdims=True)
            var = jnp.mean((x - mu) ** 2, axis=-1, keepdims=True)
            return (x - mu) * jax.lax.rsqrt(var + LN_EPS) * g + b
        b, l, c = features.shape
        h = pscale.shape[0]
        d = c // h
        p = wqp.shape[1] // (h * 3)
        x = _layernorm(features, ln_g, ln_b)
        q_s = (x @ wq + bq).reshape(b, l, h, d).transpose(0, 2, 1, 3)
        k_s = (x @ wk + bk).reshape(b, l, h, d).transpose(0, 2, 1, 3)
        v_s = (x @ wv + bv).reshape(b, l, h, d).transpose(0, 2, 1, 3)
        q_p = (x @ wqp + bqp).reshape(b, l, h, p, 3).transpose(0, 2, 1, 3, 4)
        k_p = (x @ wkp + bkp).reshape(b, l, h, p, 3).transpose(0, 2, 1, 3, 4)
        logits_s = jnp.einsum('bhid,bhjd->bhij', q_s, k_s) * d ** (-0.5)
        dot = jnp.einsum('bhipk,bhjpk->bhij', q_p, k_p)
        qsq = jnp.sum(q_p * q_p, axis=(-1, -2))
        ksq = jnp.sum(k_p * k_p, axis=(-1, -2))
        pdist2 = qsq[..., :, None] + ksq[..., None, :] - 2.0 * dot
        logits = logits_s - pdist2 * pscale[None, :, None, None]
        attn = jax.nn.softmax(logits, axis=-1)
        out_s = jnp.einsum('bhij,bhjd->bhid', attn, v_s)
        out_s = out_s.transpose(0, 2, 1, 3).reshape(b, l, c)
        out = out_s @ wo + bo
        return out

    def _L0_ffn_ref(x, gate_w, w1, w3, w2, sw1, sw3, sw2):
        import jax, jax.numpy as jnp
        import numpy as np
        E = 64
        K = 2
        D = 128
        H = 64
        NSH = 2
        ROUTE_SCALE = 2.5
        CAP = 256
        STD = 0.02
        bs, slen, d = x.shape
        xf = x.reshape(-1, d)
        logits = xf @ gate_w.T
        scores = jax.nn.sigmoid(logits.astype(jnp.float32))
        top_scores, top_idx = jax.lax.top_k(scores, K)
        top_scores = top_scores / (top_scores.sum(-1, keepdims=True) + 1e-20)
        top_scores = top_scores * ROUTE_SCALE
        flat_e = top_idx.reshape(-1)
        x_pairs = jnp.repeat(xf, K, axis=0)
        oh = jax.nn.one_hot(flat_e, E, dtype=jnp.int32)
        pos = jnp.take_along_axis(jnp.cumsum(oh, axis=0), flat_e[:, None], axis=1)[:, 0] - 1
        buf = jnp.zeros((E, CAP, d), dtype=xf.dtype).at[flat_e, pos].set(x_pairs, mode='drop')
        h = jax.nn.silu(jnp.einsum('ecd,edh->ech', buf, w1)) * jnp.einsum('ecd,edh->ech', buf, w3)
        y = jnp.einsum('ech,ehd->ecd', h, w2)
        valid = (pos < CAP)[:, None]
        y_pairs = jnp.where(valid, y[flat_e, jnp.minimum(pos, CAP - 1)], 0.0)
        routed = (y_pairs.reshape(-1, K, d) * top_scores[..., None].astype(xf.dtype)).sum(axis=1)
        shared = jax.nn.silu(xf @ sw1) * (xf @ sw3) @ sw2
        return (shared + routed).reshape(bs, slen, d)

    def _L1_attn_ref(x, norm_weight, norm_bias, lambda_re, lambda_im, p_re, p_im, b_re, b_im, c_re, c_im, d, log_step, out_w, out_b, out2_w, out2_b):
        import jax, jax.numpy as jnp
        import numpy as np

        def _hippo_dplr(n):
            pr = np.sqrt(1.0 + 2.0 * np.arange(n))
            A = -(np.tril(pr[:, None] * pr[None, :]) - np.diag(np.arange(n)))
            p = np.sqrt(np.arange(n) + 0.5)
            b = np.sqrt(2.0 * np.arange(n) + 1.0)
            S = A + p[:, None] * p[None, :]
            lam_re = np.full(n, np.mean(np.diagonal(S)))
            lam_im, V = np.linalg.eigh(S * -1j)
            p_c = V.conj().T @ p.astype(np.complex128)
            b_c = V.conj().T @ b.astype(np.complex128)
            return (lam_re, lam_im, p_c, b_c)
        Bsz, L, H = x.shape
        skip = x
        mu = jnp.mean(x, -1, keepdims=True)
        var = jnp.mean((x - mu) ** 2, -1, keepdims=True)
        xn = (x - mu) / jnp.sqrt(var + 1e-05) * norm_weight + norm_bias
        lam = (lambda_re + 1j * lambda_im).astype(jnp.complex64)
        p = (p_re + 1j * p_im).astype(jnp.complex64)
        b = (b_re + 1j * b_im).astype(jnp.complex64)
        c = (c_re + 1j * c_im).astype(jnp.complex64)
        step = jnp.exp(log_step).astype(jnp.complex64)
        N = lam.shape[0]
        I = jnp.eye(N, dtype=jnp.complex64)
        A = jnp.diag(lam) - p[:, None] * p[None, :].conj()
        A0 = 2.0 / step * I + A
        Dinv = jnp.diag(1.0 / (2.0 / step - lam))
        qcD = p.conj()[None, :] @ Dinv
        Dp = Dinv @ p[:, None]
        A1 = Dinv - Dp @ qcD / (1.0 + qcD @ p[:, None])
        Ab = A1 @ A0
        Bb = 2.0 * (A1 @ b[:, None])[:, 0]
        u = xn.astype(jnp.complex64)

        def step_fn(state, u_t):
            new = jnp.einsum('nm,bhm->bhn', Ab, state) + u_t[..., None] * Bb
            return (new, jnp.einsum('n,bhn->bh', c, new).real)
        init = jnp.zeros((Bsz, H, N), jnp.complex64)
        _, ys = jax.lax.scan(step_fn, init, jnp.moveaxis(u, 1, 0))
        y = jnp.moveaxis(ys, 0, 1) + d * xn
        y = jax.nn.gelu(y)
        gate = jax.nn.sigmoid(y @ out2_w.T + out2_b)
        return skip + (y @ out_w.T + out_b) * gate

    def _L1_ffn_ref(x, router_w, w_gate, w_up, w_down):
        import jax, jax.numpy as jnp
        import numpy as np
        B, S, D, H, E, K = (2, 512, 128, 256, 8, 2)

        def _moe(x, router_w, w_gate, w_up, w_down):
            bsz, seq, d = x.shape
            flat = x.reshape(-1, d)
            logits = flat @ router_w.T
            topk_vals, topk_idx = jax.lax.top_k(logits, K)
            topk_w = jax.nn.softmax(topk_vals, axis=-1)
            s = flat.shape[0]
            dense_w = jnp.zeros((s, E), dtype=flat.dtype).at[jnp.arange(s)[:, None], topk_idx].add(topk_w)
            g = jnp.einsum('sd,edh->esh', flat, w_gate)
            u = jnp.einsum('sd,edh->esh', flat, w_up)
            y = jnp.einsum('esh,ehd->esd', jax.nn.silu(g) * u, w_down)
            out = jnp.einsum('esd,se->sd', y, dense_w)
            return out.reshape(bsz, seq, d)
        return _moe(x, router_w, w_gate, w_up, w_down)
    h = _L0_tok_ref(x, L0_tok_W, L0_tok_b, L0_tok_class_token, L0_tok_pos_embed)
    h = jnp.concatenate([h, _L0_txt_ref(x_txt, L0_txt_emb_weight, L0_txt_conv_weight)], axis=1)
    h = h + _L0_attn_ref(_layernorm(h, axis=-1), L0_attn_coords, L0_attn_ln_g, L0_attn_ln_b, L0_attn_wq, L0_attn_bq, L0_attn_wk, L0_attn_bk, L0_attn_wv, L0_attn_bv, L0_attn_wqp, L0_attn_bqp, L0_attn_wkp, L0_attn_bkp, L0_attn_wvp, L0_attn_bvp, L0_attn_wo, L0_attn_bo, L0_attn_pscale)
    h = h + _L0_ffn_ref(_layernorm(h, axis=-1), L0_ffn_gate_w, L0_ffn_w1, L0_ffn_w3, L0_ffn_w2, L0_ffn_sw1, L0_ffn_sw3, L0_ffn_sw2)
    h = h + _L1_attn_ref(_layernorm(h, axis=-1), L1_attn_norm_weight, L1_attn_norm_bias, L1_attn_lambda_re, L1_attn_lambda_im, L1_attn_p_re, L1_attn_p_im, L1_attn_b_re, L1_attn_b_im, L1_attn_c_re, L1_attn_c_im, L1_attn_d, L1_attn_log_step, L1_attn_out_w, L1_attn_out_b, L1_attn_out2_w, L1_attn_out2_b)
    h = h + _L1_ffn_ref(_layernorm(h, axis=-1), L1_ffn_router_w, L1_ffn_w_gate, L1_ffn_w_up, L1_ffn_w_down)
    return h

_drawn_inputs = setup_inputs


def setup_inputs(seed=0):
    import zlib

    import numpy as np

    out = dict(_drawn_inputs(seed))
    spreads = {'L0_attn_ln_g': (1.0, 0.6),
     'L0_attn_ln_b': (0.0, 0.424),
     'L0_attn_bq': (0.0, 0.8),
     'L0_attn_bk': (0.0, 0.8),
     'L0_attn_bv': (0.0, 0.1),
     'L0_attn_bqp': (0.0, 0.8),
     'L0_attn_bkp': (0.0, 0.8),
     'L0_attn_bvp': (0.0, 0.1),
     'L0_attn_bo': (0.0, 0.1),
     'L0_attn_pscale': (0.5, 0.6),
     'L1_attn_norm_weight': (1.0, 0.2),
     'L1_attn_norm_bias': (0.0, 0.279),
     'L1_attn_lambda_re': (-0.5, 0.591),
     'L1_attn_out_b': (0.0, 0.1),
     'L1_attn_out2_b': (0.0, 0.351)}
    factors = {'L0_tok_b': 3.136,
     'L0_attn_wq': 8.0,
     'L0_attn_wk': 8.0,
     'L0_attn_wqp': 6.454,
     'L0_attn_wkp': 5.697,
     'L0_ffn_gate_w': 3.236,
     'L0_ffn_w1': 3.417,
     'L0_ffn_w3': 3.417,
     'L0_ffn_w2': 3.401,
     'L0_ffn_sw1': 3.097,
     'L0_ffn_sw3': 3.011,
     'L0_ffn_sw2': 3.099}
    for name, (base, spread) in spreads.items():
        noise = np.random.default_rng([zlib.crc32(name.encode()), seed]).standard_normal(out[name].shape)
        drawn = base * np.exp(spread * noise) if base else spread * noise
        out[name] = jnp.asarray(drawn.astype(out[name].dtype))
    for name, factor in factors.items():
        out[name] = (out[name] * factor).astype(out[name].dtype)
    return out
```

```python
from contextlib import ExitStack

import numpy as np
import concourse.bass as bass
from concourse import mybir

F32 = mybir.dt.float32
BF16 = mybir.dt.bfloat16
I32 = mybir.dt.int32
U32 = mybir.dt.uint32
ALU = mybir.AluOpType
ACT = mybir.ActivationFunctionType
AX_X = mybir.AxisListType.X

BATCH, CHANS, IMG, PATCH = 64, 3, 224, 28
GRID = IMG // PATCH
NPATCH = GRID * GRID
PDIM = CHANS * PATCH * PATCH
HID = 128
NTEXT = 128
SEQ = 1 + NPATCH + NTEXT
SEQP = SEQ + 1
ROWS = SEQP // 2
PAIRS = BATCH // 2
TILES = 4
COLS = 2 * SEQP
KCH = -(-PDIM // 128)
GROUPS, GB = 8, 8
VOCAB = 125
HEADS, HD, NPT = 8, 16, 12
EPS = 1e-5
E1, CAP, EH = 64, 256, 64
SLOTS1 = E1 * CAP
E2, EH2 = 8, 256
REG2 = BATCH * SEQ + 128
SLOTS2 = E2 * REG2
MT2 = (2 * BATCH * SEQ) // 128 + E2
MT2 += -MT2 % 4
ROUTE_SCALE = 2.5
NST = 64
ROUND = 1.5 * 2.0 ** 23

CONST_COLS = {}


def constants():
    parts = {}
    p = np.arange(128)
    parts["ident"] = np.eye(128)
    parts["ones"] = np.ones((128, 128))
    tri = np.zeros((128, ROWS))
    tri[:ROWS] = (np.arange(ROWS)[:, None] < np.arange(ROWS)[None, :])
    parts["tri"] = tri
    rev = np.zeros((128, ROWS))
    rev[:ROWS] = np.eye(ROWS)[::-1]
    parts["rev"] = rev
    jm = np.zeros((128, 128))
    for n in range(NST):
        jm[n, n + NST] = -1.0
        jm[n + NST, n] = 1.0
    parts["jmat"] = jm
    hsel = np.zeros((128, 2, 128))
    for h in range(HEADS):
        hsel[h, h // 4, 32 * (h % 4):32 * (h % 4) + 32] = 1.0
    parts["hsel"] = hsel.reshape(128, 256)
    q = p % 32
    parts["row0"] = (q == 0)[:, None]
    parts["row1"] = (q == 1)[:, None]
    parts["rows_s"] = ((q >= 2) & (q < 2 + HD))[:, None]
    parts["rows_p"] = ((q >= 2 + HD) & (q < 2 + HD + NPT))[:, None]
    sel = np.zeros((128, 2, 128))
    for a in p:
        if 2 + HD <= a % 32 < 2 + HD + NPT:
            sel[a, 0, 32 * (a // 32)] = 1.0
            sel[a, 1, 32 * (a // 32) + 1] = 1.0
    parts["psel"] = sel.reshape(128, 256)
    parts["vocab"] = p[:, None]
    parts["iota64"] = np.tile(np.arange(E1), (128, 1))
    parts["eoff1"] = np.tile(CAP * np.arange(E1) - SLOTS1, (128, 1))
    parts["eoff2"] = np.tile(REG2 * np.arange(E2) - SLOTS2, (128, 1))
    pad = np.zeros((128, 2, TILES))
    pad[ROWS - 1, :, 1::2] = 1000.0
    parts["padbig"] = pad.reshape(128, 2 * TILES)
    half = (np.arange(128) >= NST).astype(float)
    ma = np.zeros((128, 128)); ma[0] = 1 - half; ma[1] = half
    mb = np.zeros((128, 128)); mb[0] = half; mb[1] = half - 1
    parts["mask_a"], parts["mask_b"] = ma, mb
    parts["csign"] = (1.0 - 2.0 * (p >= NST))[:, None]
    tix = np.zeros((128, MT2)); tix[:] = np.arange(MT2)
    parts["tile_index"] = tix
    parts["lower8"] = np.zeros((128, 64))
    parts["lower8"][0] = (np.arange(8)[None, :] < np.arange(8)[:, None]).reshape(64)
    at, cols = 0, {}
    for k, v in parts.items():
        cols[k] = (at, v.shape[1])
        at += v.shape[1]
    return np.concatenate([np.asarray(v, np.float32) for v in parts.values()], axis=1), cols


CONSTS, CONST_COLS = constants()
NCONST = CONSTS.shape[1]


class Memory:
    pass


class Steps:

    def __init__(self, eng, own, base=0, start=0):
        self.eng, self.own, self.base, self.n = eng, own, base, start

    def __call__(self, ins, signal=None, value=None):
        if signal is None:
            self.n += 1
            signal, value = self.own, self.base + self.n
        ins.then_inc(signal, 1)
        self.eng.wait_ge(signal, value)


def memory(nc, ctx):
    m = Memory()

    def sb(name, shape, dt=F32):
        return ctx.enter_context(nc.sbuf_tensor(name, shape, dt))

    m.cst = sb("cst", [128, NCONST])
    m.tok = sb("tok", [128, BATCH * NPATCH])
    m.hres = sb("hres", [ROWS, PAIRS, TILES, HID])
    m.slots1 = sb("slots1", [ROWS, PAIRS, 2 * TILES], I32)
    m.wts1 = sb("wts1", [ROWS, PAIRS, 2 * TILES])
    m.slots2 = sb("slots2", [ROWS, PAIRS, 2 * TILES], I32)
    m.wts2 = sb("wts2", [ROWS, PAIRS, 2 * TILES])
    m.wq = sb("wq", [128, 2, 128]); m.wk = sb("wk", [128, 2, 128]); m.wv = sb("wv", [128, 128]); m.wo = sb("wo", [128, 128])
    m.bo_row = sb("bo_row", [1, 128]); m.biasq = sb("biasq", [128, 2]); m.biask = sb("biask", [128, 2])
    m.rawq = sb("rawq", [128, 2]); m.rawk = sb("rawk", [128, 2]); m.scaleq = sb("scaleq", [128, 2])
    m.esq = sb("esq", [128, 2, 128]); m.esk = sb("esk", [128, 2, 128])
    m.embt = sb("embt", [VOCAB, 128]); m.convq = sb("convq", [128, 2])
    m.posT = sb("posT", [128, 1 + NPATCH]); m.tokb = sb("tokb", [128, 1])
    m.gatew = sb("gatew", [128, E1]); m.sw13 = sb("sw13", [128, 256]); m.sw2 = sb("sw2", [128, 128])
    m.outw = sb("outw", [128, 256]); m.outb = sb("outb", [1, 256])
    m.normw = sb("normw", [ROWS, 128]); m.normb = sb("normb", [ROWS, 128])
    m.toep = sb("toep", [ROWS, 2, SEQP])
    m.rtw = sb("rtw", [128, E2])
    m.wgu = sb("wgu", [128, E2, 2 * EH2]); m.wd = sb("wd", [128, E2, 2, 128])
    m.tri_bf = sb("tri_bf", [ROWS, ROWS], BF16); m.ones_bf = sb("ones_bf", [ROWS, ROWS], BF16)
    m.carry = sb("carry", [1, E1]); m.carry2 = sb("carry2", [1, E2])
    m.hT0, m.hT1 = (sb(f"hT{n}", [128, 2, SEQP]) for n in range(2))
    return m


def cview(m, name, rows=128):
    a, n = CONST_COLS[name]
    return m.cst[0:rows, a:a + n]


def setup_phase(nc, m, d, ctx):
    with ExitStack() as own:
        def sb(name, shape, dt=F32):
            return own.enter_context(nc.sbuf_tensor(name, shape, dt))

        sems = []

        def sem(name):
            sems.append(nc.alloc_semaphore(name))
            return sems[-1]

        ps = [own.enter_context(nc.psum_tensor(f"setup_ps{n}", [128, 512], F32)) for n in range(4)]
        emb = sb("emb", [VOCAB, 128]); cw = sb("cw", [128, 2])
        lng = sb("lng", [128, 1]); lnb = sb("lnb", [128, 1])
        brow = sb("brow", [1, 512]); bvrow = sb("bvrow", [1, 128]); borow = sb("borow", [1, 128])
        psc = sb("psc", [HEADS, 1]); psr = sb("psr", [128, 2]); npsr = sb("npsr", [128, 2])
        clsc = sb("clsc", [128, 1])
        ssm = sb("ssm", [2, 4, 128])
        bc = sb("bc", [128, 2])
        ls = sb("ls", [128, 1]); dsc = sb("dsc", [1, 1])
        tq = sb("tq", [128, 8]); tqe = sb("tqe", [128, 128]); tqc = sb("tqc", [128, 2])
        zrow = sb("zrow", [128, 2048])
        z = sb("ssm_z", [2, 20, 128]); z1 = sb("ssm_z1", [2, 12]); zc = sb("ssm_cols", [128, 6])
        a0 = sb("a0", [128, 128]); a0t = sb("a0t", [128, 128])
        a1 = sb("a1", [128, 128]); a1t = sb("a1t", [128, 128])
        pw = sb("pw", [128, 2, 128]); qw = sb("qw", [128, 2, 128])
        vm = sb("vm", [128, 256]); krow = sb("krow", [1, SEQP]); hank = sb("hank", [ROWS, 2, SEQP])
        bvc = sb("bvc", [128, 1])

        ld = sem("setup_loaded"); zs = sem("scratch_zeroed"); kst = sem("kernel_stored")
        hk = sem("hankel_loaded"); zz = sem("zero_row_set"); own_step = sem("setup_dve_step")
        exp_done = sem("step_size_ready")
        scale_mm, bias_mm, bv_mm, bo_mm = sem("scale_mm"), sem("bias_mm"), sem("bv_mm"), sem("bo_mm")
        amax_t, qscale_mm, ssm_mm, ab_mm = sem("amax_t"), sem("qscale_mm"), sem("ssm_mm"), sem("ab_mm")
        power_mm, kern_mm, toep_mm = sem("power_mm"), sem("kern_mm"), sem("toep_mm")
        bv_ready, amax_ready, qscale_ready = sem("bv_ready"), sem("amax_ready"), sem("qscale_ready")
        rank2_ready, a_ready, v0_ready = sem("rank2_ready"), sem("a_ready"), sem("v0_ready")
        power_ready, kern_ready = sem("power_ready"), sem("kern_ready")

        loads = [(m.cst[:, :], d["cst"]), (m.wq[:, :, :], d["wq"]), (m.wk[:, :, :], d["wk"]),
                 (m.wv[:, :], d["wv"]), (m.wo[:, :], d["wo"]), (brow[:, :], d["brow"]),
                 (bvrow[:, :], d["bv"]), (borow[:, :], d["bo"]), (psc[:, :], d["pscale"]),
                 (emb[:, :], d["emb"]), (cw[:, :], d["cw"]), (lng[:, :], d["lng"]), (lnb[:, :], d["lnb"]),
                 (m.posT[:, :], d["posT"]), (m.tokb[:, :], d["tokb"]), (clsc[:, :], d["cls"]),
                 (m.gatew[:, :], d["gatew"]), (m.sw13[:, :], d["sw13"]), (m.sw2[:, :], d["sw2"]),
                 (m.outw[:, :], d["outw"]), (m.outb[:, :], d["outb"]),
                 (m.normw[:, :], d["normw"].broadcast_to([ROWS, 128])),
                 (m.normb[:, :], d["normb"].broadcast_to([ROWS, 128])),
                 (m.rtw[:, :], d["rtw"]), (m.wgu[:, :, :], d["wgu"]), (m.wd[:, :, :, :], d["wd"]),
                 (ssm[:, :, :], d["ssm"].broadcast_to([2, 4, 128])), (bc[:, :], d["bc"]),
                 (ls[:, :], d["logstep"].broadcast_to([128, 1])), (dsc[:, :], d["dsc"])]

        ident, ones = cview(m, "ident"), cview(m, "ones")
        row0, row1 = cview(m, "row0"), cview(m, "row1")
        block = own.enter_context(nc.Block())

        @block.sync
        def _(sp):
            for dst, src in loads:
                sp.dma_start(dst, src, allow_slow_non_contiguous=True).then_inc(ld, 16)
            sp.wait_ge(zz, 1)
            for n in range(SLOTS1 // 2048):
                sp.dma_start(d["buf1"][2048 * n:2048 * n + 2048, :].rearrange("(p a) c -> p (a c)", p=128),
                             zrow[:, :]).then_inc(zs, 16)
            sp.dma_start(d["y1"][SLOTS1:SLOTS1 + 128, :], zrow[:, 0:128]).then_inc(zs, 16)
            sp.dma_start(d["buf2"][SLOTS2:SLOTS2 + 128, :], zrow[:, 0:128]).then_inc(zs, 16)
            sp.dma_start(d["y2"][128 * MT2:128 * MT2 + 128, :], zrow[:, 0:128]).then_inc(zs, 16)
            sp.dma_start(d["kpad"][0:1, 0:SEQ], zrow[0:1, 0:SEQ]).then_inc(kst, 16)
            sp.wait_ge(kern_ready, 1)
            sp.dma_start(d["kpad"][0:1, SEQ:SEQ + SEQP], krow[:, :]).then_inc(kst, 16)
            sp.wait_ge(kst, 32)
            for a in range(2):
                src = bass.AP(tensor=d["kpad"].tensor, offset=ROWS * (1 - a), ap=[[1, ROWS], [1, SEQP]])
                sp.dma_start(hank[:, a, :], src).then_inc(hk, 16)
            sp.wait_ge(zs, 16 * (SLOTS1 // 2048 + 3))

        @block.gpsimd
        def _(pool):
            nc.gpsimd.memset(zrow[:, :], 0.0).then_inc(zz, 1)
        @block.scalar
        def _(act):
            act.wait_ge(ld, 16 * len(loads))
            nc.scalar.activation(zc[:, 0:1], ls[:, :], ACT.Exp).then_inc(exp_done, 1)

        doublings = []
        n = 1
        while n < SEQP:
            doublings.append((n, min(n, SEQP - n)))
            n *= 2

        @block.tensor
        def _(pe):
            T = nc.tensor
            pe.wait_ge(ld, 16 * len(loads))
            for g in range(2):
                last = T.matmul(ps[0][:, g:g + 1], lhsT=cview(m, "hsel")[0:HEADS, 128 * g:128 * g + 128],
                                rhs=psc[:, :], start=True, stop=True)
            last.then_inc(scale_mm, 1)
            for n, w in ((0, m.wq), (2, m.wk)):
                for g in range(2):
                    T.matmul(ps[1][:, n + g:n + g + 1], lhsT=w[:, g, :], rhs=lnb[:, :], start=True, stop=False)
                    last = T.matmul(ps[1][:, n + g:n + g + 1], lhsT=brow[:, 128 * (n + g):128 * (n + g) + 128],
                                    rhs=ones[0:1, 0:1], start=False, stop=True)
            last.then_inc(bias_mm, 1)
            T.matmul(ps[2][:, 0:1], lhsT=m.wv[:, :], rhs=lnb[:, :], start=True, stop=False)
            T.matmul(ps[2][:, 0:1], lhsT=bvrow[:, :], rhs=ones[0:1, 0:1], start=False, stop=True).then_inc(bv_mm, 1)
            pe.wait_ge(bv_ready, 1)
            T.matmul(ps[2][0:1, 0:128], lhsT=bvc[:, :], rhs=m.wo[:, :], start=True, stop=True).then_inc(bo_mm, 1)
            for n, rows in enumerate((VOCAB, 128)):
                pe.wait_ge(amax_ready, n + 1)
                T.transpose(ps[3][0:1, 0:rows], tq[0:rows, 0:1], ident[0:rows, 0:rows]).then_inc(amax_t, 1)
                pe.wait_ge(qscale_ready, n + 1)
                T.matmul(ps[3][:, 256:257], lhsT=ones[0:1, :], rhs=tq[0:1, 2:3],
                         start=True, stop=True).then_inc(qscale_mm, 1)
            pe.wait_ge(rank2_ready, 1)
            for n, row in enumerate((z[0:1, 3, :], z[0:1, 4, :], ssm[0:1, 0, :], ssm[0:1, 1, :])):
                T.matmul(ps[0][:, 8 + n:9 + n], lhsT=row, rhs=ones[0:1, 0:1], start=True, stop=True)
            for n, (a, b) in enumerate(((12, 13), (13, 12), (14, 14))):
                last = T.matmul(ps[1][:, 128 * n:128 * n + 128], lhsT=z[:, a, :], rhs=z[:, b, :], start=True, stop=True)
            last.then_inc(ssm_mm, 1)
            pe.wait_ge(a_ready, 1)
            T.matmul(ps[2][:, 0:128], lhsT=a1t[:, :], rhs=a0[:, :], start=True, stop=True)
            T.matmul(ps[2][:, 128:256], lhsT=a0[:, :], rhs=a1t[:, :], start=True, stop=True)
            T.matmul(ps[2][:, 256:257], lhsT=a1t[:, :], rhs=bc[:, 0:1], start=True, stop=True).then_inc(ab_mm, 1)
            pe.wait_ge(v0_ready, 1)
            for k, (n, c) in enumerate(doublings):
                pe.wait_ge(power_ready, k)
                last = T.matmul(ps[k % 2][:, 0:c], lhsT=qw[:, k % 2, :], rhs=vm[:, 0:c], start=True, stop=True)
                if k < len(doublings) - 1:
                    T.matmul(ps[k % 2][:, 128:256], lhsT=qw[:, k % 2, :], rhs=pw[:, k % 2, :], start=True, stop=True)
                    last = T.matmul(ps[k % 2][:, 256:384], lhsT=pw[:, k % 2, :], rhs=qw[:, k % 2, :],
                                    start=True, stop=True)
                last.then_inc(power_mm, 1)
            pe.wait_ge(power_ready, len(doublings))
            T.matmul(ps[2][0:1, 0:SEQP], lhsT=bc[:, 1:2], rhs=vm[:, 0:SEQP], start=True, stop=True).then_inc(kern_mm, 1)
            pe.wait_ge(hk, 32)
            for a in range(2):
                last = T.matmul(ps[3][0:ROWS, SEQP * a:SEQP * a + SEQP], lhsT=cview(m, "rev", ROWS),
                                rhs=hank[:, a, :], start=True, stop=True)
            last.then_inc(toep_mm, 1)

        @block.vector
        def _(dve):
            V = nc.vector
            step = Steps(dve, own_step)
            dve.wait_ge(ld, 16 * len(loads))
            dve.wait_ge(scale_mm, 1)
            step(V.tensor_copy(psr[:, :], ps[0][:, 0:2]))
            step(V.tensor_scalar(npsr[:, :], psr[:, :], -1.0, None, ALU.mult))
            for g in range(2):
                sc = m.scaleq[:, g:g + 1]
                step(V.tensor_scalar(sc, psr[:, g:g + 1], 2.0, cview(m, "rows_p"), ALU.mult, ALU.mult))
                step(V.scalar_tensor_tensor(out=sc, in0=cview(m, "rows_s"), scalar=float(HD) ** -0.5, in1=sc,
                                            op0=ALU.mult, op1=ALU.add))
                step(V.tensor_tensor(sc, sc, row0, ALU.add))
                for k, es in ((0, m.esq), (1, m.esk)):
                    step(V.tensor_scalar(es[:, g, :], cview(m, "psel")[:, 128 * k:128 * k + 128],
                                         npsr[:, g:g + 1], None, ALU.mult))
            dve.wait_ge(bias_mm, 1)
            step(V.tensor_copy(m.rawq[:, :], ps[1][:, 0:2]))
            step(V.tensor_copy(m.rawk[:, :], ps[1][:, 2:4]))
            step(V.tensor_tensor(m.biasq[:, :], m.rawq[:, :], m.scaleq[:, :], ALU.mult))
            step(V.tensor_scalar(m.biasq[:, :], m.biasq[:, :], row1, None, ALU.add))
            step(V.tensor_scalar(m.biask[:, :], m.rawk[:, :], row0, None, ALU.add))
            dve.wait_ge(bv_mm, 1)
            step(V.tensor_copy(bvc[:, :], ps[2][:, 0:1]), bv_ready, 1)
            dve.wait_ge(bo_mm, 1)
            step(V.tensor_tensor(m.bo_row[:, :], borow[:, :], ps[2][0:1, 0:128], ALU.add))
            step(V.tensor_scalar(m.wq[:, :, :], m.wq[:, :, :], lng[:, 0:1], None, ALU.mult))
            step(V.tensor_scalar(m.wk[:, :, :], m.wk[:, :, :], lng[:, 0:1], None, ALU.mult))
            step(V.tensor_scalar(m.wv[:, :], m.wv[:, :], lng[:, 0:1], None, ALU.mult))
            step(V.tensor_scalar(m.sw2[:, :], m.sw2[:, :], 0.5, None, ALU.mult))
            step(V.tensor_scalar(m.wd[:, :, :, :], m.wd[:, :, :, :], 0.5, None, ALU.mult))
            step(V.tensor_scalar(m.outw[:, :], m.outw[:, :], 0.5, None, ALU.mult))
            step(V.tensor_copy(m.tri_bf[:, :], cview(m, "tri", ROWS)))
            step(V.memset(m.ones_bf[:, :], 1.0))
            step(V.memset(m.carry[:, :], 0.0))
            step(V.memset(m.carry2[:, :], 0.0))
            for h in (m.hT0, m.hT1):
                step(V.memset(h[:, :, SEQ:SEQP], 0.0))
                for b in range(2):
                    step(V.tensor_tensor(h[:, b, 0:1], clsc[:, :], m.posT[:, 0:1], ALU.mult))
            for n, (w, rows, out, t) in enumerate(((emb, VOCAB, m.embt, tqe), (cw, 128, m.convq, tqc))):
                t = t[0:rows, :]
                step(V.tensor_reduce(tq[0:rows, 0:1], w[:, :], AX_X, ALU.max, apply_absolute_value=True),
                     amax_ready, n + 1)
                dve.wait_ge(amax_t, n + 1)
                step(V.tensor_reduce(tq[0:1, 1:2], ps[3][0:1, 0:rows], AX_X, ALU.max))
                step(V.tensor_scalar(tq[0:1, 2:3], tq[0:1, 1:2], 1.0 / 127.0, None, ALU.mult), qscale_ready, n + 1)
                dve.wait_ge(qscale_mm, n + 1)
                step(V.tensor_copy(tq[:, 3:4], ps[3][:, 256:257]))
                step(V.reciprocal(tq[:, 4:5], tq[:, 3:4]))
                step(V.tensor_scalar(t, w[:, :], tq[0:rows, 4:5], None, ALU.mult))
                step(V.tensor_scalar(t, t, ROUND, None, ALU.add))
                step(V.tensor_scalar(t, t, ROUND, None, ALU.subtract))
                step(V.scalar_tensor_tensor(out=t, in0=t, scalar=tq[0:rows, 3:4], in1=w[:, :],
                                            op0=ALU.mult, op1=ALU.subtract))
                step(V.tensor_tensor(out[:, :], w[:, :], t, ALU.add))

            def Z(n):
                return z[:, n, :]

            def S(n):
                return z1[:, n:n + 1]

            def tt(o, a, b, op):
                step(V.tensor_tensor(o, a, b, op))

            lr, li, pr, pi = (ssm[:, n, :] for n in range(4))
            dve.wait_ge(exp_done, 1)
            step(V.reciprocal(zc[:, 1:2], zc[:, 0:1]))
            step(V.tensor_scalar(zc[:, 1:2], zc[:, 1:2], 2.0, None, ALU.mult))
            step(V.tensor_scalar(Z(0), lr, -1.0, zc[0:2, 1:2], ALU.mult, ALU.add))
            tt(Z(1), Z(0), Z(0), ALU.mult)
            tt(Z(2), li, li, ALU.mult)
            tt(Z(1), Z(1), Z(2), ALU.add)
            step(V.reciprocal(Z(2), Z(1)))
            tt(Z(3), Z(0), Z(2), ALU.mult)
            tt(Z(4), li, Z(2), ALU.mult)
            dr, di = Z(3), Z(4)
            tt(Z(9), dr, pr, ALU.mult)
            tt(Z(10), di, pi, ALU.mult)
            tt(Z(5), Z(9), Z(10), ALU.subtract)
            tt(Z(7), Z(9), Z(10), ALU.add)
            tt(Z(9), dr, pi, ALU.mult)
            tt(Z(10), di, pr, ALU.mult)
            tt(Z(6), Z(9), Z(10), ALU.add)
            tt(Z(8), Z(10), Z(9), ALU.subtract)
            tt(Z(9), Z(7), pr, ALU.mult)
            tt(Z(10), Z(8), pi, ALU.mult)
            tt(Z(9), Z(9), Z(10), ALU.subtract)
            step(V.tensor_reduce(S(0), z[:, 9, 0:NST], AX_X, ALU.add))
            step(V.tensor_scalar(S(0), S(0), 1.0, None, ALU.add))
            tt(Z(9), Z(7), pi, ALU.mult)
            tt(Z(10), Z(8), pr, ALU.mult)
            tt(Z(9), Z(9), Z(10), ALU.add)
            step(V.tensor_reduce(S(1), z[:, 9, 0:NST], AX_X, ALU.add))
            tt(S(2), S(0), S(0), ALU.mult)
            tt(S(3), S(1), S(1), ALU.mult)
            tt(S(2), S(2), S(3), ALU.add)
            step(V.reciprocal(S(3), S(2)))
            tt(S(4), S(0), S(3), ALU.mult)
            step(V.scalar_tensor_tensor(out=S(5), in0=S(1), scalar=-1.0, in1=S(3), op0=ALU.mult, op1=ALU.mult))
            step(V.tensor_scalar(Z(11), Z(6), S(5), None, ALU.mult))
            step(V.scalar_tensor_tensor(out=Z(9), in0=Z(5), scalar=S(4), in1=Z(11), op0=ALU.mult, op1=ALU.subtract))
            step(V.tensor_scalar(Z(11), Z(6), S(4), None, ALU.mult))
            step(V.scalar_tensor_tensor(out=Z(10), in0=Z(5), scalar=S(5), in1=Z(11), op0=ALU.mult, op1=ALU.add))
            for o, re, im, sign in ((12, Z(9), Z(10), ALU.add), (13, Z(7), Z(8), ALU.subtract), (14, pr, pi, ALU.add)):
                tt(Z(15), cview(m, "mask_a", 2), re, ALU.mult)
                tt(Z(16), cview(m, "mask_b", 2), im, ALU.mult)
                if o < 14:
                    tt(Z(o), Z(15), Z(16), sign)
            step(V.tensor_tensor(Z(14), Z(15), Z(16), ALU.add), rank2_ready, 1)
            dve.wait_ge(ssm_mm, 1)
            step(V.tensor_copy(zc[:, 2:6], ps[0][:, 8:12]))
            tt(zc[:, 1:2], zc[:, 1:2], zc[:, 4:5], ALU.add)
            for n, (mat, re, im, off, sign) in enumerate((
                    (a1, 2, 3, 0, ALU.add), (a1t, 2, 3, 128, ALU.subtract),
                    (a0t, 1, 5, 256, ALU.subtract), (a0, 1, 5, 256, ALU.add))):
                step(V.tensor_scalar(tqe[:, :], cview(m, "jmat"), zc[:, im:im + 1], None, ALU.mult))
                step(V.scalar_tensor_tensor(out=mat[:, :], in0=ident, scalar=zc[:, re:re + 1], in1=tqe[:, :],
                                            op0=ALU.mult, op1=sign))
                if n < 3:
                    tt(mat[:, :], mat[:, :], ps[1][:, off:off + 128], ALU.subtract)
            step(V.tensor_tensor(a0[:, :], a0[:, :], ps[1][:, 256:384], ALU.subtract), a_ready, 1)
            dve.wait_ge(ab_mm, 1)
            step(V.tensor_copy(pw[:, 0, :], ps[2][:, 0:128]))
            step(V.tensor_copy(qw[:, 0, :], ps[2][:, 128:256]))
            step(V.tensor_scalar(bc[:, 1:2], bc[:, 1:2], cview(m, "csign"), None, ALU.mult))
            step(V.tensor_scalar(vm[:, 0:1], ps[2][:, 256:257], 2.0, None, ALU.mult), v0_ready, 1)
            for k, (n, c) in enumerate(doublings):
                dve.wait_ge(power_mm, k + 1)
                if k < len(doublings) - 1:
                    step(V.tensor_copy(pw[:, (k + 1) % 2, :], ps[k % 2][:, 128:256]))
                    step(V.tensor_copy(qw[:, (k + 1) % 2, :], ps[k % 2][:, 256:384]))
                step(V.tensor_copy(vm[:, n:n + c], ps[k % 2][:, 0:c]), power_ready, k + 1)
            dve.wait_ge(kern_mm, 1)
            step(V.tensor_copy(krow[:, :], ps[2][0:1, 0:SEQP]))
            step(V.tensor_tensor(krow[:, 0:1], krow[:, 0:1], dsc[:, :], ALU.add), kern_ready, 1)
            dve.wait_ge(toep_mm, 1)
            step(V.tensor_copy(m.toep[:, :, :].rearrange("p a n -> p (a n)"), ps[3][0:ROWS, 0:2 * SEQP]))
    nc.clear_and_free_semaphores(sems)
    nc.all_engine_barrier()


def patch_phase(nc, m, d, ctx):
    with ExitStack() as own:
        def sb(name, shape, dt=F32):
            return own.enter_context(nc.sbuf_tensor(name, shape, dt))

        def sem(name):
            return ctx.enter_context(nc.semaphore(name))

        NT = GB * NPATCH
        wtok = sb("wtok", [128, KCH, 128])
        pat = [sb(f"patches{n}", [128, KCH, NT // 2]) for n in range(2)]
        ps = [own.enter_context(nc.psum_tensor(f"tok_ps{n}", [128, NT // 2], F32)) for n in range(2)]
        wl = sem("wtok_loaded")
        loaded = [sem(f"patches_loaded{n}") for n in range(2)]
        mm = [sem(f"patches_mm{n}") for n in range(2)]
        out_ready = [sem(f"tokens_ready{n}") for n in range(2)]
        block = own.enter_context(nc.Block())

        @block.sync
        def _(sp):
            sp.dma_start(wtok[:, :, :], d["wtok"]).then_inc(wl, 16)
            for n in range(2):
                sp.sem_inc(loaded[n], 16)
                sp.sem_inc(mm[n], 1)
                sp.sem_inc(out_ready[n], 1)
            with sp.Fori(1, GROUPS + 1) as i:
                for n in range(2):
                    sp.wait_ge(mm[n], i)
                    sp.dma_start(pat[n][:, :, :], d["xpat"][2 * i + (n - 2)]).then_inc(loaded[n], 16)

        @block.tensor
        def _(pe):
            pe.wait_ge(wl, 16)
            with pe.Fori(1, GROUPS + 1) as i:
                for n in range(2):
                    pe.wait_ge(loaded[n], 16 * i + 16)
                    pe.wait_ge(out_ready[n], i)
                    for k in range(KCH):
                        last = nc.tensor.matmul(ps[n][:, :], lhsT=wtok[:, k, :], rhs=pat[n][:, k, :],
                                                start=(k == 0), stop=(k == KCH - 1))
                    last.then_inc(mm[n], 1)

        @block.vector
        def _(dve):
            pos = m.posT[:, None, 1:1 + NPATCH].broadcast_to([128, GB // 2, NPATCH])
            with dve.Fori(1, GROUPS + 1) as i:
                for n in range(2):
                    dve.wait_ge(mm[n], i + 1)
                    dst = m.tok[:, bass.ds(i * NT + (n * (NT // 2) - NT), NT // 2)].rearrange("p (b t) -> p b t", b=GB // 2)
                    nc.vector.scalar_tensor_tensor(
                        out=dst, in0=ps[n][:, :].rearrange("p (b t) -> p b t", b=GB // 2),
                        scalar=m.tokb[:, 0:1], in1=pos, op0=ALU.add, op1=ALU.mult).then_inc(out_ready[n], 1)


def token_phase(nc, m, d, ctx):
    with ExitStack() as own:
        def sb(name, shape, dt=F32):
            return own.enter_context(nc.sbuf_tensor(name, shape, dt))

        def sem(name):
            return ctx.enter_context(nc.semaphore(name))

        ident, ones = cview(m, "ident"), cview(m, "ones")
        HALF = SEQP
        at = own.enter_context(nc.psum_tensor("scores", [128, 4, 512], F32))
        xb = own.enter_context(nc.psum_tensor("heads_out", [128, 512], F32))
        pb = own.enter_context(nc.psum_tensor("work", [128, 3, 512], F32))

        ybuf = sb("ybuf", [VOCAB, 2, NTEXT], I32)
        oh = sb("onehot", [VOCAB, 2, NTEXT + 1])
        cv = sb("conv", [128, 2, NTEXT])
        hT = m.hT0
        h_sb = sb("h_sb", [ROWS, TILES, HID])
        st, mv = sb("stats", [ROWS, TILES, 6]), sb("meanvar", [ROWS, TILES, 2])
        vv, rs = sb("var_eps", [ROWS, TILES]), sb("rstd", [ROWS, TILES])
        st2, mv2 = sb("stats2", [ROWS, TILES, 6]), sb("meanvar2", [ROWS, TILES, 2])
        vv2, rs2 = sb("var_eps2", [ROWS, TILES]), sb("rstd2", [ROWS, TILES])
        nhalf = sb("nhalf", [ROWS, TILES])
        xh = sb("xh", [ROWS, TILES, HID]); xT = sb("xT", [128, COLS])
        sq = sb("squares", [128, 2, COLS])
        qk = sb("qk", [128, 4, COLS])
        vx = sb("v_ext", [ROWS, TILES, HEADS, 32])
        mx = sb("maxima", [ROWS, 4, 2]); mp = sb("max_placed", [ROWS, 2, 128])
        q2 = sb("q_shifted", [128, HALF]); pt = sb("probs", [ROWS, 4, 2 * HALF])
        osb = sb("heads_sb", [128, 2, COLS])
        rsum = sb("recip_sums", [ROWS, TILES, HEADS]); on = sb("heads_norm", [ROWS, TILES, HEADS, HD])
        oT = sb("oT", [128, COLS]); h1 = sb("h1", [ROWS, TILES, HID])
        xf = sb("xf", [ROWS, TILES, HID]); xfT = sb("xfT", [128, COLS])
        th = sb("tanh_g", [128, COLS]); hm = sb("hidden", [128, COLS])
        er = sb("router_exp", [ROWS, TILES, E1]); nu = sb("neg_inv_score", [ROWS, TILES, E1])
        tv, ti = sb("top_vals", [ROWS, TILES, 8]), sb("top_idx", [ROWS, TILES, 8], U32)
        sc, den = sb("top_scores", [ROWS, TILES, 2]), sb("score_sum", [ROWS, TILES])
        idf = sb("top_idx_f", [ROWS, 2, TILES])
        ohk = sb("chosen", [ROWS, 2, TILES, E1]); mk = sb("mask", [ROWS, TILES, E1], BF16)
        ap_, apb = sb("slot_of", [ROWS, TILES, E1]), sb("slot_in_cap", [ROWS, TILES, E1])
        slf = sb("slot_f", [ROWS, 2 * TILES]); sli = sb("slot_i", [ROWS, 2 * TILES], I32)

        y_loaded, oh_ready, emb_mm, cv_ready = sem("y_loaded"), sem("oh_ready"), sem("emb_mm"), sem("cv_ready")
        text_in, patches_in, h_mm, h_sb_ready = sem("text_in"), sem("patches_in"), sem("h_mm"), sem("h_sb_ready")
        var_ready, rs_ready, xh_ready, xT_mm = sem("var_ready"), sem("rs_ready"), sem("xh_ready"), sem("xT_mm")
        xT_ready, proj_mm, sq_ready, esum_mm = sem("xT_ready"), sem("proj_mm"), sem("sq_ready"), sem("esum_mm")
        q_ready, k_ready, v_mm, v_ready = sem("q_ready"), sem("k_ready"), sem("v_mm"), sem("v_ready")
        s_mm, m_ready, mT_mm, q2_ready = sem("s_mm"), sem("m_ready"), sem("mT_mm"), sem("q2_ready")
        st_mm, exp_ready, pv_mm, o_ready = sem("st_mm"), sem("exp_ready"), sem("pv_mm"), sem("o_ready")
        otm_mm, on_ready, oT_mm, oT_ready = sem("otm_mm"), sem("on_ready"), sem("oT_mm"), sem("oT_ready")
        ao_mm, h1_ready, var2_ready, rs2_ready = sem("ao_mm"), sem("h1_ready"), sem("var2_ready"), sem("rs2_ready")
        xf_ready, xfT_mm, xfT_ready, rt_mm = sem("xf_ready"), sem("xfT_mm"), sem("xfT_ready"), sem("rt_mm")
        gu_mm, er_ready, th_ready, hm_ready = sem("gu_mm"), sem("er_ready"), sem("th_ready"), sem("hm_ready")
        sh_mm, hres_ready, mk_ready, pos_mm = sem("sh_mm"), sem("hres_ready"), sem("mk_ready"), sem("pos_mm")
        slot_ready, scattered, rows_sent = sem("slot_ready"), sem("scattered"), sem("rows_sent")
        own_f, own_a, own_b, preset = sem("dve_front"), sem("dve_att"), sem("dve_back"), sem("preset")
        block = own.enter_context(nc.Block())
        STEPS_F, STEPS_A, STEPS_B = 15, 1, 39

        @block.sync
        def _(sp):
            for s in (oh_ready, emb_mm, cv_ready, text_in, patches_in, h_mm, h_sb_ready, var_ready, rs_ready,
                      xh_ready, xT_mm, xT_ready, v_mm, v_ready, otm_mm, on_ready, oT_mm, oT_ready, ao_mm,
                      h1_ready, var2_ready, rs2_ready, xf_ready, xfT_mm, xfT_ready, rt_mm, gu_mm, er_ready,
                      th_ready, hm_ready, sh_mm, hres_ready, mk_ready, pos_mm, slot_ready, rows_sent):
                sp.sem_inc(s, 1)
            for s in (q_ready, k_ready):
                sp.sem_inc(s, 2)
            for s in (proj_mm, sq_ready, esum_mm, s_mm, m_ready, mT_mm, q2_ready, st_mm, exp_ready, pv_mm, o_ready):
                sp.sem_inc(s, 4)
            sp.sem_inc(y_loaded, 16)
            sp.sem_inc(own_f, STEPS_F)
            sp.sem_inc(own_a, 4 * STEPS_A)
            sp.sem_inc(own_b, STEPS_B)
            with sp.Fori(1, PAIRS + 1) as i:
                sp.wait_ge(oh_ready, i)
                src = d["ytxt"][bass.ds(i - 1, 1), :].broadcast_to([VOCAB, 2 * NTEXT])
                sp.dma_start(ybuf[:, :, :].rearrange("p b t -> p (b t)"), src).then_inc(y_loaded, 16)

        @block.gpsimd
        def _(pool):
            nc.gpsimd.memset(oh[:, :, :], 0.0).then_inc(preset, 1)
            nc.gpsimd.memset(vx[:, :, :, :], 0.0).then_inc(preset, 1)
            nc.gpsimd.memset(mp[:, :, :], 0.0).then_inc(preset, 1)
            nc.gpsimd.memset(nhalf[:, :], -0.5).then_inc(preset, 1)
            pool.wait_ge(preset, 4)
            nc.gpsimd.memset(vx[:, :, :, HD:HD + 1], 1.0).then_inc(preset, 1)
            pool.wait_ge(preset, 5)
            with pool.Fori(1, PAIRS + 1) as i:
                pool.wait_ge(h_mm, i)
                nc.gpsimd.tensor_copy(
                    hT[:, :, 1:1 + NPATCH],
                    m.tok[:, bass.ds(i * 2 * NPATCH - 2 * NPATCH, 2 * NPATCH)].rearrange("p (b t) -> p b t", b=2)
                ).then_inc(patches_in, 1)
                pool.wait_ge(var_ready, i + 1)
                nc.gpsimd.tensor_tensor(rs[:, :], vv[:, :], nhalf[:, :], ALU.pow).then_inc(rs_ready, 1)
                pool.wait_ge(var2_ready, i + 1)
                nc.gpsimd.tensor_tensor(rs2[:, :], vv2[:, :], nhalf[:, :], ALU.pow).then_inc(rs2_ready, 1)
                pool.wait_ge(slot_ready, i + 1)
                pool.nop(nofuse=True)
                for n in range(2 * TILES):
                    nc.gpsimd.indirect_dma_start(
                        out=d["buf1"], out_offset=bass.IndirectOffsetOnAxis(ap=sli[:, n:n + 1], axis=0),
                        in_=xf[:, n % TILES, :], in_offset=None,
                        bounds_check=SLOTS1 - 1, oob_is_err=False).then_inc(scattered, 16)
                pool.wait_ge(scattered, i * (16 * 2 * TILES))
                pool.sem_inc(rows_sent, 1)

        @block.tensor
        def _(pe):
            T = nc.tensor
            pe.wait_ge(preset, 5)
            with pe.Fori(1, PAIRS + 1) as i:
                pe.wait_ge(oh_ready, i + 1)
                pe.wait_ge(hres_ready, i)
                T.matmul(pb[:, 0, 0:2 * (NTEXT + 1)], lhsT=m.embt[:, :],
                         rhs=oh[:, :, :].rearrange("p b t -> p (b t)"), start=True, stop=True).then_inc(emb_mm, 1)
                pe.wait_ge(patches_in, i + 1)
                pe.wait_ge(text_in, i + 1)
                pe.wait_ge(slot_ready, i)
                for j in range(TILES):
                    last = T.transpose(pb[0:ROWS, 1, HID * j:HID * j + HID],
                                       hT[:, j // 2, ROWS * (j % 2):ROWS * (j % 2) + ROWS], ident)
                last.then_inc(h_mm, 1)
                pe.wait_ge(xh_ready, i + 1)
                pe.wait_ge(er_ready, i)
                for j in range(TILES):
                    last = T.transpose(pb[:, 2, ROWS * j:ROWS * j + ROWS], xh[:, j, :], ident[0:ROWS, 0:ROWS])
                last.then_inc(xT_mm, 1)
                pe.wait_ge(xT_ready, i + 1)
                pe.wait_ge(h_sb_ready, i + 1)

                def project(n, bank):
                    w = (m.wq if n < 2 else m.wk)[:, n % 2, :]
                    T.matmul(pb[:, bank, 0:COLS], lhsT=w, rhs=xT[:, :], start=True, stop=True).then_inc(proj_mm, 1)

                def add_squares(n, bank):
                    es = (m.esq if n < 2 else m.esk)[:, n % 2, :]
                    pe.wait_ge(sq_ready, 4 * i + (n + 1))
                    T.matmul(pb[:, bank, 0:COLS], lhsT=es, rhs=sq[:, n % 2, :],
                             start=False, stop=True, skip_group_check=True).then_inc(esum_mm, 1)

                project(0, 0)
                project(1, 1)
                project(2, 2)
                add_squares(0, 0)
                add_squares(1, 1)
                pe.wait_ge(q_ready, 2 * i + 1)
                project(3, 0)
                add_squares(2, 2)
                pe.wait_ge(q_ready, 2 * i + 2)
                for j in range(TILES):
                    last = T.matmul(pb[0:ROWS, 1, HID * j:HID * j + HID], lhsT=xT[:, ROWS * j:ROWS * j + ROWS],
                                    rhs=m.wv[:, :], start=True, stop=True)
                last.then_inc(v_mm, 1)
                add_squares(3, 0)
                pe.wait_ge(k_ready, 2 * i + 2)
                pe.wait_ge(v_ready, i + 1)

                for u in range(4):
                    b, g = u // 2, u % 2
                    pe.wait_ge(exp_ready, 4 * i + u)
                    for hh in range(4):
                        r = slice(32 * hh, 32 * hh + 32)
                        for qt in range(2):
                            c = HALF * b + ROWS * qt
                            last = T.matmul(at[0:ROWS, hh, HALF * qt:HALF * qt + SEQ], lhsT=qk[r, g, c:c + ROWS],
                                            rhs=qk[r, 2 + g, HALF * b:HALF * b + SEQ], start=True, stop=True)
                    last.then_inc(s_mm, 1)
                    pe.wait_ge(m_ready, 4 * i + u + 1)
                    for qt in range(2):
                        last = T.matmul(pb[:, 1, ROWS * qt:ROWS * qt + ROWS], lhsT=mp[:, qt, :],
                                        rhs=ident[0:ROWS, 0:ROWS], start=True, stop=True)
                    last.then_inc(mT_mm, 1)
                    pe.wait_ge(q2_ready, 4 * i + u + 1)
                    for hh in range(4):
                        r = slice(32 * hh, 32 * hh + 32)
                        for kt in range(2):
                            c = HALF * b + ROWS * kt
                            last = T.matmul(at[0:ROWS, hh, HALF * kt:HALF * kt + HALF],
                                            lhsT=qk[r, 2 + g, c:c + ROWS], rhs=q2[r, :], start=True, stop=True)
                    last.then_inc(st_mm, 1)
                    pe.wait_ge(exp_ready, 4 * i + u + 1)
                    pe.wait_ge(o_ready, 4 * i + u)
                    for hh in range(4):
                        for kt in range(2):
                            n = ROWS - kt
                            last = T.matmul(xb[32 * hh:32 * hh + 32, 0:HALF],
                                            lhsT=vx[0:n, 2 * b + kt, 4 * g + hh, :],
                                            rhs=pt[0:n, hh, HALF * kt:HALF * kt + HALF],
                                            start=(kt == 0), stop=(kt == 1))
                    last.then_inc(pv_mm, 1)

                pe.wait_ge(o_ready, 4 * i + 4)
                for j in range(TILES):
                    for g in range(2):
                        c = 256 * j + 128 * g
                        last = T.transpose(pb[0:ROWS, c // 512, c % 512:c % 512 + 128],
                                           osb[:, g, ROWS * j:ROWS * j + ROWS], ident)
                last.then_inc(otm_mm, 1)
                pe.wait_ge(on_ready, i + 1)
                for j in range(TILES):
                    last = T.transpose(pb[:, 2, ROWS * j:ROWS * j + ROWS],
                                       on[:, j, :, :].rearrange("p h d -> p (h d)"), ident[0:ROWS, 0:ROWS])
                last.then_inc(oT_mm, 1)
                pe.wait_ge(oT_ready, i + 1)
                for j in range(TILES):
                    T.matmul(pb[0:ROWS, 0, HID * j:HID * j + HID], lhsT=oT[:, ROWS * j:ROWS * j + ROWS],
                             rhs=m.wo[:, :], start=True, stop=False)
                    last = T.matmul(pb[0:ROWS, 0, HID * j:HID * j + HID], lhsT=ones[0:1, 0:ROWS],
                                    rhs=m.bo_row[:, :], start=False, stop=True)
                last.then_inc(ao_mm, 1)
                pe.wait_ge(xf_ready, i + 1)
                for j in range(TILES):
                    last = T.transpose(pb[:, 1, ROWS * j:ROWS * j + ROWS], xf[:, j, :], ident[0:ROWS, 0:ROWS])
                last.then_inc(xfT_mm, 1)
                pe.wait_ge(xfT_ready, i + 1)
                for j in range(TILES):
                    last = T.matmul(pb[0:ROWS, 2, E1 * j:E1 * j + E1], lhsT=xfT[:, ROWS * j:ROWS * j + ROWS],
                                    rhs=m.gatew[:, :], start=True, stop=True)
                last.then_inc(rt_mm, 1)
                for n in range(2):
                    last = T.matmul(pb[:, n, 0:COLS], lhsT=m.sw13[:, 128 * n:128 * n + 128], rhs=xfT[:, :],
                                    start=True, stop=True)
                last.then_inc(gu_mm, 1)
                pe.wait_ge(hm_ready, i + 1)
                for j in range(TILES):
                    last = T.matmul(pb[0:ROWS, 0, HID * j:HID * j + HID], lhsT=hm[:, ROWS * j:ROWS * j + ROWS],
                                    rhs=m.sw2[:, :], start=True, stop=True)
                last.then_inc(sh_mm, 1)
                pe.wait_ge(mk_ready, i + 1)
                out = pb[0:ROWS, 1, 0:TILES * E1].rearrange("p (j e) -> p j e", j=TILES)
                T.matmul(out, lhsT=m.tri_bf[:, :], rhs=mk[:, :, :], start=True, stop=False)
                for j in range(TILES - 1):
                    T.matmul(out[:, j + 1:, :], lhsT=m.ones_bf[:, :],
                             rhs=mk[:, j:j + 1, :].broadcast_to([ROWS, TILES - 1 - j, E1]), start=False, stop=False)
                T.matmul(out, lhsT=ones[0:1, 0:ROWS],
                         rhs=m.carry[:, None, :].broadcast_to([1, TILES, E1]), start=False, stop=True)
                tot = pb[0:1, 1, TILES * E1:TILES * E1 + E1]
                for j in range(TILES):
                    T.matmul(tot, lhsT=m.ones_bf[:, 0:1], rhs=mk[:, j, :], start=(j == 0), stop=False)
                T.matmul(tot, lhsT=ones[0:1, 0:1], rhs=m.carry[:, :], start=False, stop=True).then_inc(pos_mm, 1)

        @block.scalar
        def _(act):
            A = nc.scalar
            act.wait_ge(preset, 5)
            with act.Fori(1, PAIRS + 1) as i:
                act.wait_ge(emb_mm, i + 1)
                emb = pb[:, 0, 0:2 * (NTEXT + 1)].rearrange("p (b t) -> p b t", b=2)
                A.activation(cv[:, :, :], emb[:, :, 0:NTEXT], ACT.Copy, scale=m.convq[:, 0:1]).then_inc(cv_ready, 1)
                act.wait_ge(h_mm, i + 1)
                act.wait_ge(h1_ready, i)
                A.activation(h_sb[:, :, :].rearrange("p j c -> p (j c)"), pb[0:ROWS, 1, :], ACT.Copy).then_inc(h_sb_ready, 1)
                act.wait_ge(xT_mm, i + 1)
                A.activation(xT[:, :], pb[:, 2, 0:COLS], ACT.Copy).then_inc(xT_ready, 1)
                for n, bank in enumerate((0, 1, 2, 0)):
                    raw = (m.rawq if n < 2 else m.rawk)[:, n % 2:n % 2 + 1]
                    act.wait_ge(proj_mm, 4 * i + (n + 1))
                    if n >= 2:
                        act.wait_ge(esum_mm, 4 * i + (n - 1))
                    A.activation(sq[:, n % 2, :], pb[:, bank, 0:COLS], ACT.Square, bias=raw).then_inc(sq_ready, 1)
                    if n == 1:
                        for k in range(2):
                            act.wait_ge(esum_mm, 4 * i + (k + 1))
                            A.activation(qk[:, k, :], pb[:, k, 0:COLS], ACT.Identity, bias=m.biasq[:, k:k + 1],
                                         scale=m.scaleq[:, k:k + 1]).then_inc(q_ready, 1)
                act.wait_ge(v_mm, i + 1)
                A.activation(vx[:, :, :, 0:HD].rearrange("p j h d -> p (j h) d"),
                             pb[0:ROWS, 1, :].rearrange("p (n d) -> p n d", d=HD), ACT.Copy).then_inc(v_ready, 1)
                for u in range(4):
                    b, g = u // 2, u % 2
                    act.wait_ge(st_mm, 4 * i + u + 1)
                    A.activation(pt[:, :, :], at[0:ROWS, :, 0:2 * HALF], ACT.Exp).then_inc(exp_ready, 1)
                    act.wait_ge(pv_mm, 4 * i + u + 1)
                    A.activation(osb[:, g, HALF * b:HALF * b + HALF], xb[:, 0:HALF], ACT.Copy).then_inc(o_ready, 1)
                act.wait_ge(oT_mm, i + 1)
                A.activation(oT[:, :], pb[:, 2, 0:COLS], ACT.Copy).then_inc(oT_ready, 1)
                act.wait_ge(xfT_mm, i + 1)
                A.activation(xfT[:, :], pb[:, 1, 0:COLS], ACT.Copy).then_inc(xfT_ready, 1)
                act.wait_ge(rt_mm, i + 1)
                A.activation(er[:, :, :].rearrange("p j e -> p (j e)"), pb[0:ROWS, 2, 0:TILES * E1], ACT.Exp,
                             scale=-1.0).then_inc(er_ready, 1)
                act.wait_ge(gu_mm, i + 1)
                A.activation(th[:, :], pb[:, 0, 0:COLS], ACT.Tanh, scale=0.5).then_inc(th_ready, 1)

        @block.vector
        def _(dve):
            V = nc.vector

            def variance(step, st, mv):
                step(V.tensor_tensor(mv[:, :, 0], st[:, :, 1], st[:, :, 4], ALU.add))
                step(V.tensor_tensor(mv[:, :, 1], st[:, :, 1], st[:, :, 4], ALU.subtract))
                step(V.scalar_tensor_tensor(out=mv[:, :, 1], in0=mv[:, :, 1], scalar=HID / 4.0, in1=mv[:, :, 1],
                                            op0=ALU.mult, op1=ALU.mult))
                step(V.tensor_tensor(mv[:, :, 1], mv[:, :, 1], st[:, :, 2], ALU.add))
                step(V.tensor_tensor(mv[:, :, 1], mv[:, :, 1], st[:, :, 5], ALU.add))
                step(V.tensor_scalar(mv[:, :, 1], mv[:, :, 1], 1.0 / HID, None, ALU.mult))
                step(V.tensor_scalar(mv[:, :, 0], mv[:, :, 0], 0.5, None, ALU.mult))

            dve.wait_ge(preset, 5)
            with dve.Fori(1, PAIRS + 1) as i:
                step = Steps(dve, own_f, i * STEPS_F)
                dve.wait_ge(y_loaded, 16 * i + 16)
                dve.wait_ge(emb_mm, i)
                step(V.tensor_scalar(oh[:, :, 1:], ybuf[:, :, :], float(VOCAB - 1), cview(m, "vocab", VOCAB),
                                     ALU.min, ALU.is_equal), oh_ready, i + 1)
                dve.wait_ge(cv_ready, i + 1)
                emb = pb[:, 0, 0:2 * (NTEXT + 1)].rearrange("p (b t) -> p b t", b=2)
                step(V.scalar_tensor_tensor(out=cv[:, :, :], in0=emb[:, :, 1:], scalar=m.convq[:, 1:2],
                                            in1=cv[:, :, :], op0=ALU.mult, op1=ALU.add))
                dve.wait_ge(h_mm, i)
                step(V.tensor_scalar(hT[:, :, 1 + NPATCH:SEQ], cv[:, :, :], 0.0, None, ALU.max), text_in, i + 1)
                dve.wait_ge(h_sb_ready, i + 1)
                for j in range(TILES):
                    step(V.bn_stats(st[:, j, :], h_sb[:, j, :]))
                variance(step, st, mv)
                step(V.tensor_scalar(vv[:, :], mv[:, :, 1], 1.0 + EPS, EPS * EPS, ALU.mult, ALU.add), var_ready, i + 1)
                dve.wait_ge(rs_ready, i + 1)
                dve.wait_ge(xT_mm, i)
                for j in range(TILES):
                    x = V.tensor_scalar(xh[:, j, :], h_sb[:, j, :], mv[:, j, 0:1],
                                        rs[:, j:j + 1], ALU.subtract, ALU.mult)
                    if j < TILES - 1:
                        step(x)
                    else:
                        step(x, xh_ready, i + 1)
                for k in range(2):
                    dve.wait_ge(esum_mm, 4 * i + (3 + k))
                    step(V.tensor_scalar(qk[:, 2 + k, :], pb[:, 2 - 2 * k, 0:COLS], m.biask[:, k:k + 1], None, ALU.add),
                         k_ready, 2 * i + (k + 1))
                assert step.n == STEPS_F, step.n

                for u in range(4):
                    b, g = u // 2, u % 2
                    step = Steps(dve, own_a, (4 * i + u) * STEPS_A)
                    dve.wait_ge(s_mm, 4 * i + u + 1)
                    sview = at[0:ROWS, :, 0:2 * HALF].rearrange("p h (t k) -> p h t k", t=2)[:, :, :, 0:SEQ]
                    step(V.tensor_reduce(mx[:, :, :], sview, AX_X, ALU.max))
                    dve.wait_ge(mT_mm, 4 * i + u)
                    step(V.tensor_scalar(mp[:, :, :].rearrange("p t (h r) -> p h t r", r=32)[:, :, :, 0],
                                         mx[:, :, :], -1.0, None, ALU.mult), m_ready, 4 * i + u + 1)
                    dve.wait_ge(mT_mm, 4 * i + u + 1)
                    step(V.tensor_tensor(q2[:, :], qk[:, g, HALF * b:HALF * b + HALF], pb[:, 1, 0:HALF], ALU.add),
                         q2_ready, 4 * i + u + 1)
                    assert step.n == STEPS_A, step.n

                step = Steps(dve, own_b, i * STEPS_B)
                dve.wait_ge(otm_mm, i + 1)
                heads = pb[0:ROWS, 0:2, :].rearrange("p a c -> p (a c)").rearrange("p (n r) -> p n r", r=32)
                step(V.reciprocal(rsum[:, :, :].rearrange("p j h -> p (j h)"), heads[:, :, HD]))
                step(V.tensor_tensor(on[:, :, :, :].rearrange("p j h d -> p (j h) d"), heads[:, :, 0:HD],
                                     rsum[:, :, :].rearrange("p j h -> p (j h)")[:, :, None].broadcast_to(
                                         [ROWS, TILES * HEADS, HD]), ALU.mult), on_ready, i + 1)
                dve.wait_ge(ao_mm, i + 1)
                step(V.tensor_tensor(h1[:, :, :].rearrange("p j c -> p (j c)"),
                                     h_sb[:, :, :].rearrange("p j c -> p (j c)"), pb[0:ROWS, 0, :], ALU.add),
                     h1_ready, i + 1)
                for j in range(TILES):
                    step(V.bn_stats(st2[:, j, :], h1[:, j, :]))
                variance(step, st2, mv2)
                step(V.tensor_scalar(vv2[:, :], mv2[:, :, 1], EPS, None, ALU.add), var2_ready, i + 1)
                dve.wait_ge(rs2_ready, i + 1)
                dve.wait_ge(rows_sent, i)
                for j in range(TILES):
                    x = V.tensor_scalar(xf[:, j, :], h1[:, j, :], mv2[:, j, 0:1], rs2[:, j:j + 1],
                                        ALU.subtract, ALU.mult)
                    if j < TILES - 1:
                        step(x)
                    else:
                        step(x, xf_ready, i + 1)
                dve.wait_ge(th_ready, i + 1)
                step(V.scalar_tensor_tensor(out=th[:, :], in0=th[:, :], scalar=1.0, in1=pb[:, 0, 0:COLS],
                                            op0=ALU.add, op1=ALU.mult))
                step(V.tensor_tensor(hm[:, :], th[:, :], pb[:, 1, 0:COLS], ALU.mult), hm_ready, i + 1)
                dve.wait_ge(er_ready, i + 1)
                step(V.tensor_scalar(nu[:, :, :], er[:, :, :], -1.0, -1.0, ALU.mult, ALU.add))
                for j in range(TILES):
                    dve.nop(nofuse=True)
                    step(V.max(tv[:, j, :], nu[:, j, :]))
                for j in range(TILES):
                    dve.nop(nofuse=True)
                    step(V.max_index(ti[:, j, :], tv[:, j, :], nu[:, j, :]))
                step(V.tensor_tensor(idf[:, :, :].rearrange("p k j -> p j k"), ti[:, :, 0:2],
                                     cview(m, "padbig", ROWS).rearrange("p (k j) -> p j k", k=2), ALU.add))
                step(V.tensor_tensor(
                    ohk[:, :, :, :].rearrange("p k j e -> p (k j) e"),
                    cview(m, "iota64", ROWS)[:, None, :].broadcast_to([ROWS, 2 * TILES, E1]),
                    idf[:, :, :].rearrange("p k j -> p (k j)")[:, :, None].broadcast_to([ROWS, 2 * TILES, E1]),
                    ALU.is_equal))
                step(V.tensor_tensor(mk[:, :, :], ohk[:, 0, :, :], ohk[:, 1, :, :], ALU.add), mk_ready, i + 1)
                step(V.reciprocal(sc[:, :, :], tv[:, :, 0:2]))
                step(V.tensor_tensor(den[:, :], sc[:, :, 0], sc[:, :, 1], ALU.add))
                step(V.tensor_scalar(den[:, :], den[:, :], -1e-20, None, ALU.add))
                step(V.reciprocal(den[:, :], den[:, :]))
                w = m.wts1[:, bass.ds(i - 1, 1), :].rearrange("p a (k j) -> p (a k) j", k=2)
                step(V.scalar_tensor_tensor(out=w, in0=sc[:, :, :].rearrange("p j k -> p k j"), scalar=ROUTE_SCALE,
                                            in1=den[:, None, :].broadcast_to([ROWS, 2, TILES]),
                                            op0=ALU.mult, op1=ALU.mult))
                dve.wait_ge(sh_mm, i + 1)
                step(V.tensor_tensor(m.hres[:, bass.ds(i - 1, 1), :, :].rearrange("p a j c -> p (a j c)"),
                                     h1[:, :, :].rearrange("p j c -> p (j c)"), pb[0:ROWS, 0, :], ALU.add),
                     hres_ready, i + 1)
                dve.wait_ge(pos_mm, i + 1)
                pos = pb[0:ROWS, 1, 0:TILES * E1].rearrange("p (j e) -> p j e", j=TILES)
                step(V.tensor_copy(m.carry[:, :], pb[0:1, 1, TILES * E1:TILES * E1 + E1]))
                step(V.tensor_tensor(ap_[:, :, :], pos,
                                     cview(m, "eoff1", ROWS)[:, None, :].broadcast_to([ROWS, TILES, E1]), ALU.add))
                step(V.scalar_tensor_tensor(out=apb[:, :, :], in0=pos, scalar=float(CAP), in1=ap_[:, :, :],
                                            op0=ALU.is_lt, op1=ALU.mult))
                for k in range(2):
                    step(V.tensor_tensor(ohk[:, k, :, :], ohk[:, k, :, :], apb[:, :, :], ALU.mult))
                step(V.tensor_reduce(slf[:, :], ohk[:, :, :, :].rearrange("p k j e -> p (k j) e"), AX_X, ALU.add))
                step(V.tensor_scalar(m.slots1[:, bass.ds(i - 1, 1), :].rearrange("p a n -> p (a n)"), slf[:, :],
                                     float(SLOTS1), None, ALU.add))
                step(V.tensor_scalar(sli[:, :], slf[:, :], float(SLOTS1), None, ALU.add), slot_ready, i + 1)
                assert step.n == STEPS_B, step.n



def expert_phase(nc, m, d, ctx):
    with ExitStack() as own:
        def sb(name, shape, dt=F32):
            return own.enter_context(nc.sbuf_tensor(name, shape, dt))

        def sem(name):
            return ctx.enter_context(nc.semaphore(name))

        WAYS = 2
        two = range(WAYS)
        ident = cview(m, "ident")
        rows = [sb(f"x_rows{n}", [128, 2, HID]) for n in two]
        w13 = [sb(f"w13_{n}", [128, 2 * EH]) for n in two]
        w2 = [sb(f"w2_{n}", [EH, HID]) for n in two]
        xT = [sb(f"x_rows_T{n}", [128, CAP]) for n in two]
        th = [sb(f"x_tanh{n}", [EH, CAP]) for n in two]
        hh = [sb(f"x_hidden{n}", [EH, CAP]) for n in two]
        ys = [sb(f"x_out{n}", [128, 2, HID]) for n in two]
        tps = [own.enter_context(nc.psum_tensor(f"x_T_ps{n}", [128, CAP], F32)) for n in two]
        gps = [own.enter_context(nc.psum_tensor(f"x_gu_ps{n}", [EH, 2, CAP], F32)) for n in two]
        yps = [own.enter_context(nc.psum_tensor(f"x_y_ps{n}", [128, 2, HID], F32)) for n in two]
        x_loaded = [sem(f"x_loaded{n}") for n in two]
        t_mm, xT_ready, gu_mm = sem("x_t_mm"), sem("x_xT_ready"), sem("x_gu_mm")
        th_ready, a_ready, h_ready, y_mm = sem("x_th_ready"), sem("x_a_ready"), sem("x_h_ready"), sem("x_y_mm")
        y_ready, y_stored = sem("x_y_ready"), [sem(f"x_y_stored{n}") for n in two]
        block = own.enter_context(nc.Block())
        N = E1 // WAYS

        @block.sync
        def _(sp):
            for n in two:
                sp.sem_inc(x_loaded[n], 48)
                sp.sem_inc(y_stored[n], 16)
            for s in (t_mm, xT_ready, gu_mm, th_ready, a_ready, h_ready, y_mm, y_ready):
                sp.sem_inc(s, WAYS)
            with sp.Fori(1, N + 1) as i:
                for n in two:
                    e = WAYS * i + (n - WAYS)
                    sp.wait_ge(y_mm, WAYS * i)
                    src = d["buf1"][bass.ds(e * CAP, CAP), :].rearrange("(a p) c -> p a c", p=128)
                    sp.dma_start(rows[n][:, :, :], src).then_inc(x_loaded[n], 16)
                    sp.dma_start(w13[n][:, :], d["w13"][bass.ds(e, 1), :, :].rearrange("a k c -> k (a c)")
                                 ).then_inc(x_loaded[n], 16)
                    sp.dma_start(w2[n][:, :], d["w2"][bass.ds(e, 1), :, :].rearrange("a k c -> k (a c)")
                                 ).then_inc(x_loaded[n], 16)

        @block.tensor
        def _(pe):
            T = nc.tensor
            with pe.Fori(1, N + 1) as i:
                for n in two:
                    pe.wait_ge(x_loaded[n], 48 * i + 48)
                    pe.wait_ge(xT_ready, WAYS * i)
                    for a in range(2):
                        last = T.transpose(tps[n][:, 128 * a:128 * a + 128], rows[n][:, a, :], ident)
                    last.then_inc(t_mm, 1)
                for n in two:
                    pe.wait_ge(xT_ready, WAYS * i + (n + 1))
                    pe.wait_ge(h_ready, WAYS * i)
                    for k in range(2):
                        last = T.matmul(gps[n][:, k, :], lhsT=w13[n][:, EH * k:EH * k + EH], rhs=xT[n][:, :],
                                        start=True, stop=True)
                    last.then_inc(gu_mm, 1)
                for n in two:
                    pe.wait_ge(h_ready, WAYS * i + (n + 1))
                    pe.wait_ge(y_ready, WAYS * i)
                    for a in range(2):
                        last = T.matmul(yps[n][:, a, :], lhsT=hh[n][:, 128 * a:128 * a + 128], rhs=w2[n][:, :],
                                        start=True, stop=True)
                    last.then_inc(y_mm, 1)

        @block.scalar
        def _(act):
            A = nc.scalar
            with act.Fori(1, N + 1) as i:
                for n in two:
                    act.wait_ge(t_mm, WAYS * i + (n + 1))
                    A.activation(xT[n][:, :], tps[n][:, :], ACT.Copy).then_inc(xT_ready, 1)
                for n in two:
                    act.wait_ge(gu_mm, WAYS * i + (n + 1))
                    A.activation(th[n][:, :], gps[n][:, 0, :], ACT.Tanh, scale=0.5).then_inc(th_ready, 1)
                for n in two:
                    act.wait_ge(y_mm, WAYS * i + (n + 1))
                    act.wait_ge(y_stored[n], 16 * i)
                    A.activation(ys[n][:, :, :], yps[n][:, :, :], ACT.Copy).then_inc(y_ready, 1)
                for n in two:
                    act.wait_ge(y_ready, WAYS * i + (n + 1))
                    dst = d["y1"][bass.ds((WAYS * i + (n - WAYS)) * CAP, CAP), :].rearrange("(a p) c -> p a c", p=128)
                    act.dma_start(dst, ys[n][:, :, :]).then_inc(y_stored[n], 16)
            for n in two:
                act.wait_ge(y_stored[n], 16 * (N + 1))

        @block.vector
        def _(dve):
            V = nc.vector
            with dve.Fori(1, N + 1) as i:
                for n in two:
                    dve.wait_ge(th_ready, WAYS * i + (n + 1))
                    V.scalar_tensor_tensor(out=th[n][:, :], in0=th[n][:, :], scalar=1.0, in1=gps[n][:, 0, :],
                                           op0=ALU.add, op1=ALU.mult).then_inc(a_ready, 1)
                    dve.wait_ge(a_ready, WAYS * i + (n + 1))
                    V.scalar_tensor_tensor(out=hh[n][:, :], in0=th[n][:, :], scalar=0.5, in1=gps[n][:, 1, :],
                                           op0=ALU.mult, op1=ALU.mult).then_inc(h_ready, 1)


def ssm_phase(nc, m, d, ctx):
    with ExitStack() as own:
        def sb(name, shape, dt=F32):
            return own.enter_context(nc.sbuf_tensor(name, shape, dt))

        def sem(name):
            return ctx.enter_context(nc.semaphore("s_" + name))

        ident, ones = cview(m, "ident"), cview(m, "ones")
        pb = own.enter_context(nc.psum_tensor("s_work", [128, 4, 512], F32))
        NK = 2 * TILES
        sl = sb("s_slots", [ROWS, NK], I32); wt = sb("s_wts", [ROWS, NK])
        ga = sb("s_gathered", [ROWS, NK, HID]); h = sb("s_h", [ROWS, TILES, HID])
        st, mv = sb("s_stats", [ROWS, TILES, 6]), sb("s_meanvar", [ROWS, TILES, 2])
        vv, rs, nhalf = sb("s_var", [ROWS, 2, TILES]), sb("s_rstd", [ROWS, 2, TILES]), sb("s_nhalf", [ROWS, 2, TILES])
        vv2, rs2 = sb("s_var2", [ROWS, TILES]), sb("s_rstd2", [ROWS, TILES])
        x3, xn = sb("s_x3", [ROWS, TILES, HID]), sb("s_xn", [ROWS, TILES, HID])
        y2, gl = sb("s_y2", [128, COLS]), sb("s_gelu", [128, COLS])
        tg, h4 = sb("s_gate", [ROWS, TILES, HID]), sb("s_h4", [ROWS, TILES, HID])
        xg, xgT = sb("s_xg", [ROWS, TILES, HID]), sb("s_xgT", [128, COLS])
        lg = sb("s_logits", [ROWS, TILES, E2]); tv = sb("s_top", [ROWS, TILES, 8])
        ti = sb("s_top_i", [ROWS, TILES, 8], U32); idf = sb("s_top_f", [ROWS, 2, TILES])
        df, ex, wk = sb("s_diff", [ROWS, TILES]), sb("s_exp", [ROWS, TILES]), sb("s_w", [ROWS, 2, TILES])
        ohk = sb("s_chosen", [ROWS, 2, TILES, E2]); mk = sb("s_mask", [ROWS, TILES, E2], BF16)
        so = sb("s_slot_of", [ROWS, TILES, E2]); slf = sb("s_slot_f", [ROWS, NK]); sli = sb("s_slot_i", [ROWS, NK], I32)

        preset, gathered, comb, idx_in = sem("preset"), sem("gathered"), sem("comb"), sem("idx_in")
        var_ready, rs_ready, xn0_ready, xn_ready = sem("var_ready"), sem("rs_ready"), sem("xn0_ready"), sem("xn_ready")
        hs_ready, xw_done, conv_mm, sq_ready = sem("hs_ready"), sem("xw_done"), sem("conv_mm"), sem("sq_ready")
        in_ready, tanh_ready, gl_ready, out_mm = sem("in_ready"), sem("tanh_ready"), sem("gl_ready"), sem("out_mm")
        gate_ready, h4_ready, var2_ready, rs2_ready = sem("gate_ready"), sem("h4_ready"), sem("var2_ready"), sem("rs2_ready")
        xg_ready, xgT_mm, xgT_ready, rt_mm = sem("xg_ready"), sem("xgT_mm"), sem("xgT_ready"), sem("rt_mm")
        lg_ready, df_ready, ex_ready, mk_ready = sem("lg_ready"), sem("df_ready"), sem("ex_ready"), sem("mk_ready")
        pos_mm, slot_ready, scattered, own_s = sem("pos_mm"), sem("slot_ready"), sem("scattered"), sem("dve")
        wt_in, rows_sent = sem("wt_in"), sem("rows_sent")
        block = own.enter_context(nc.Block())
        STEPS = 63
        C0, C1 = 0.7978845608028654, 0.7978845608028654 * 0.044715

        @block.sync
        def _(sp):
            for s in (comb, idx_in, var_ready, rs_ready, xn0_ready, xn_ready, hs_ready, xw_done, conv_mm, sq_ready,
                      in_ready, tanh_ready, gl_ready, out_mm, gate_ready, h4_ready, var2_ready, rs2_ready,
                      xg_ready, xgT_mm, xgT_ready, rt_mm, lg_ready, df_ready, ex_ready, mk_ready, pos_mm,
                      slot_ready, wt_in, rows_sent):
                sp.sem_inc(s, 1)
            sp.sem_inc(own_s, STEPS)

        @block.gpsimd
        def _(pool):
            nc.gpsimd.memset(nhalf[:, :, :], -0.5).then_inc(preset, 1)
            pool.wait_ge(preset, 1)
            with pool.Fori(1, PAIRS + 1) as i:
                pool.wait_ge(comb, i)
                nc.gpsimd.tensor_copy(sl[:, :], m.slots1[:, bass.ds(i - 1, 1), :].rearrange("p a n -> p (a n)")).then_inc(idx_in, 1)
                pool.wait_ge(idx_in, i + 1)
                pool.nop(nofuse=True)
                for n in range(NK):
                    nc.gpsimd.indirect_dma_start(
                        out=ga[:, n, :], out_offset=None, in_=d["y1"],
                        in_offset=bass.IndirectOffsetOnAxis(ap=sl[:, n:n + 1], axis=0)).then_inc(gathered, 16)
                pool.wait_ge(var_ready, i + 1)
                nc.gpsimd.tensor_tensor(rs[:, :, :], vv[:, :, :], nhalf[:, :, :], ALU.pow).then_inc(rs_ready, 1)
                pool.wait_ge(xn0_ready, i + 1)
                for k, (w, op) in enumerate(((m.normw, ALU.mult), (m.normb, ALU.add))):
                    x = nc.gpsimd.tensor_tensor(xn[:, :, :], xn[:, :, :],
                                                w[:, None, :].broadcast_to([ROWS, TILES, HID]), op)
                    if k == 0:
                        x.then_inc(xw_done, 1)
                        pool.wait_ge(xw_done, i + 1)
                    else:
                        x.then_inc(xn_ready, 1)
                nc.gpsimd.tensor_tensor(h[:, :, :], h[:, :, :], x3[:, :, :], ALU.add).then_inc(hs_ready, 1)
                pool.wait_ge(var2_ready, i + 1)
                nc.gpsimd.tensor_tensor(rs2[:, :], vv2[:, :], nhalf[:, 0, :], ALU.pow).then_inc(rs2_ready, 1)
                pool.wait_ge(slot_ready, i + 1)
                pool.nop(nofuse=True)
                for n in range(NK):
                    nc.gpsimd.indirect_dma_start(
                        out=d["buf2"], out_offset=bass.IndirectOffsetOnAxis(ap=sli[:, n:n + 1], axis=0),
                        in_=xg[:, n % TILES, :], in_offset=None,
                        bounds_check=SLOTS2 - 1, oob_is_err=False).then_inc(scattered, 16)
                pool.wait_ge(scattered, i * (16 * NK))
                pool.sem_inc(rows_sent, 1)

        @block.tensor
        def _(pe):
            T = nc.tensor
            with pe.Fori(1, PAIRS + 1) as i:
                pe.wait_ge(xn_ready, i + 1)
                pe.wait_ge(xgT_ready, i)
                for b in range(2):
                    c = SEQP * b
                    T.matmul(pb[:, 0, c:c + SEQP], lhsT=xn[:, 2 * b, :], rhs=m.toep[:, 0, :], start=True, stop=False)
                    last = T.matmul(pb[:, 0, c + ROWS:c + SEQP], lhsT=xn[0:ROWS - 1, 2 * b + 1, :],
                                    rhs=m.toep[0:ROWS - 1, 1, ROWS:], start=False, stop=True)
                last.then_inc(conv_mm, 1)
                pe.wait_ge(gl_ready, i + 1)
                pe.wait_ge(h4_ready, i)
                for j in range(TILES):
                    o = pb[0:ROWS, 1 + j // 2, 256 * (j % 2):256 * (j % 2) + 256]
                    T.matmul(o, lhsT=gl[:, ROWS * j:ROWS * j + ROWS], rhs=m.outw[:, :], start=True, stop=False)
                    last = T.matmul(o, lhsT=ones[0:1, 0:ROWS], rhs=m.outb[:, :], start=False, stop=True)
                last.then_inc(out_mm, 1)
                pe.wait_ge(xg_ready, i + 1)
                for j in range(TILES):
                    last = T.transpose(pb[:, 0, ROWS * j:ROWS * j + ROWS], xg[:, j, :], ident[0:ROWS, 0:ROWS])
                last.then_inc(xgT_mm, 1)
                pe.wait_ge(xgT_ready, i + 1)
                pe.wait_ge(slot_ready, i)
                for j in range(TILES):
                    last = T.matmul(pb[0:ROWS, 3, E2 * j:E2 * j + E2], lhsT=xgT[:, ROWS * j:ROWS * j + ROWS],
                                    rhs=m.rtw[:, :], start=True, stop=True)
                last.then_inc(rt_mm, 1)
                pe.wait_ge(mk_ready, i + 1)
                out = pb[0:ROWS, 3, 0:TILES * E2].rearrange("p (j e) -> p j e", j=TILES)
                T.matmul(out, lhsT=m.tri_bf[:, :], rhs=mk[:, :, :], start=True, stop=False)
                for j in range(TILES - 1):
                    T.matmul(out[:, j + 1:, :], lhsT=m.ones_bf[:, :],
                             rhs=mk[:, j:j + 1, :].broadcast_to([ROWS, TILES - 1 - j, E2]), start=False, stop=False)
                T.matmul(out, lhsT=ones[0:1, 0:ROWS],
                         rhs=m.carry2[:, None, :].broadcast_to([1, TILES, E2]), start=False, stop=True)
                tot = pb[0:1, 3, TILES * E2:TILES * E2 + E2]
                for j in range(TILES):
                    T.matmul(tot, lhsT=m.ones_bf[:, 0:1], rhs=mk[:, j, :], start=(j == 0), stop=False)
                T.matmul(tot, lhsT=ones[0:1, 0:1], rhs=m.carry2[:, :], start=False, stop=True).then_inc(pos_mm, 1)

        @block.scalar
        def _(act):
            A = nc.scalar
            with act.Fori(1, PAIRS + 1) as i:
                act.wait_ge(conv_mm, i + 1)
                act.wait_ge(in_ready, i)
                A.activation(y2[:, :], pb[:, 0, 0:COLS], ACT.Square).then_inc(sq_ready, 1)
                act.wait_ge(in_ready, i + 1)
                A.activation(y2[:, :], y2[:, :], ACT.Tanh).then_inc(tanh_ready, 1)
                act.wait_ge(out_mm, i + 1)
                z = pb[0:ROWS, 1:3, :].rearrange("p a (j c) -> p (a j) c", j=2)
                A.activation(tg[:, :, :], z[:, :, HID:], ACT.Tanh, scale=0.5).then_inc(gate_ready, 1)
                act.wait_ge(xgT_mm, i + 1)
                A.activation(xgT[:, :], pb[:, 0, 0:COLS], ACT.Copy).then_inc(xgT_ready, 1)
                act.wait_ge(rt_mm, i + 1)
                A.activation(lg[:, :, :].rearrange("p j e -> p (j e)"), pb[0:ROWS, 3, 0:TILES * E2], ACT.Copy
                             ).then_inc(lg_ready, 1)
                act.wait_ge(df_ready, i + 1)
                A.activation(ex[:, :], df[:, :], ACT.Exp).then_inc(ex_ready, 1)

        @block.vector
        def _(dve):
            V = nc.vector
            f = lambda t: t[:, :, :].rearrange("p j c -> p (j c)")

            def variance(step, st, mv):
                step(V.tensor_tensor(mv[:, :, 0], st[:, :, 1], st[:, :, 4], ALU.add))
                step(V.tensor_tensor(mv[:, :, 1], st[:, :, 1], st[:, :, 4], ALU.subtract))
                step(V.scalar_tensor_tensor(out=mv[:, :, 1], in0=mv[:, :, 1], scalar=HID / 4.0, in1=mv[:, :, 1],
                                            op0=ALU.mult, op1=ALU.mult))
                step(V.tensor_tensor(mv[:, :, 1], mv[:, :, 1], st[:, :, 2], ALU.add))
                step(V.tensor_tensor(mv[:, :, 1], mv[:, :, 1], st[:, :, 5], ALU.add))
                step(V.tensor_scalar(mv[:, :, 1], mv[:, :, 1], 1.0 / HID, None, ALU.mult))
                step(V.tensor_scalar(mv[:, :, 0], mv[:, :, 0], 0.5, None, ALU.mult))

            dve.wait_ge(preset, 1)
            with dve.Fori(1, PAIRS + 1) as i:
                step = Steps(dve, own_s, i * STEPS)
                step(V.tensor_scalar(wt[:, :], m.wts1[:, bass.ds(i - 1, 1), :].rearrange("p a n -> p (a n)"), 1.0, None,
                                     ALU.mult), wt_in, i + 1)
                dve.wait_ge(h4_ready, i)
                dve.wait_ge(gathered, i * (16 * NK))
                for n in range(NK):
                    j = n % TILES
                    base = m.hres[:, bass.ds(i - 1, 1), j, :].rearrange("p a c -> p (a c)") if n < TILES else h[:, j, :]
                    x = V.scalar_tensor_tensor(out=h[:, j, :], in0=ga[:, n, :], scalar=wt[:, n:n + 1], in1=base,
                                               op0=ALU.mult, op1=ALU.add)
                    if n < NK - 1:
                        step(x)
                    else:
                        step(x, comb, i + 1)
                for j in range(TILES):
                    step(V.bn_stats(st[:, j, :], h[:, j, :]))
                variance(step, st, mv)
                step(V.tensor_scalar(vv[:, 0, :], mv[:, :, 1], EPS, None, ALU.add))
                step(V.tensor_scalar(vv[:, 1, :], mv[:, :, 1], 1.0 + EPS, EPS * EPS, ALU.mult, ALU.add), var_ready, i + 1)
                dve.wait_ge(rs_ready, i + 1)
                dve.wait_ge(conv_mm, i)
                for k, dst in ((0, x3), (1, xn)):
                    for j in range(TILES):
                        x = V.tensor_scalar(dst[:, j, :], h[:, j, :], mv[:, j, 0:1], rs[:, k, j:j + 1],
                                            ALU.subtract, ALU.mult)
                        if k == 0 or j < TILES - 1:
                            step(x)
                        else:
                            step(x, xn0_ready, i + 1)
                dve.wait_ge(sq_ready, i + 1)
                step(V.tensor_scalar(y2[:, :], y2[:, :], C1, C0, ALU.mult, ALU.add))
                step(V.tensor_tensor(y2[:, :], y2[:, :], pb[:, 0, 0:COLS], ALU.mult), in_ready, i + 1)
                dve.wait_ge(tanh_ready, i + 1)
                step(V.scalar_tensor_tensor(out=gl[:, :], in0=y2[:, :], scalar=1.0, in1=pb[:, 0, 0:COLS],
                                            op0=ALU.add, op1=ALU.mult), gl_ready, i + 1)
                dve.wait_ge(gate_ready, i + 1)
                dve.wait_ge(hs_ready, i + 1)
                z = pb[0:ROWS, 1:3, :].rearrange("p a (j c) -> p (a j) c", j=2)
                step(V.scalar_tensor_tensor(out=tg[:, :, :], in0=tg[:, :, :], scalar=1.0, in1=z[:, :, 0:HID],
                                            op0=ALU.add, op1=ALU.mult))
                step(V.scalar_tensor_tensor(out=f(h4), in0=f(tg), scalar=0.5, in1=f(h), op0=ALU.mult, op1=ALU.add),
                     h4_ready, i + 1)
                step(V.tensor_scalar(m.hres[:, bass.ds(i - 1, 1), :, :].rearrange("p a j c -> p (a j c)"), f(h4), 1.0, None,
                                     ALU.mult))
                for j in range(TILES):
                    step(V.bn_stats(st[:, j, :], h4[:, j, :]))
                variance(step, st, mv)
                step(V.tensor_scalar(vv2[:, :], mv[:, :, 1], EPS, None, ALU.add), var2_ready, i + 1)
                dve.wait_ge(rs2_ready, i + 1)
                dve.wait_ge(rows_sent, i)
                for j in range(TILES):
                    x = V.tensor_scalar(xg[:, j, :], h4[:, j, :], mv[:, j, 0:1], rs2[:, j:j + 1],
                                        ALU.subtract, ALU.mult)
                    if j < TILES - 1:
                        step(x)
                    else:
                        step(x, xg_ready, i + 1)
                dve.wait_ge(lg_ready, i + 1)
                for j in range(TILES):
                    dve.nop(nofuse=True)
                    step(V.max(tv[:, j, :], lg[:, j, :]))
                for j in range(TILES):
                    dve.nop(nofuse=True)
                    step(V.max_index(ti[:, j, :], tv[:, j, :], lg[:, j, :]))
                step(V.tensor_tensor(df[:, :], tv[:, :, 1], tv[:, :, 0], ALU.subtract), df_ready, i + 1)
                step(V.tensor_tensor(idf[:, :, :].rearrange("p k j -> p j k"), ti[:, :, 0:2],
                                     cview(m, "padbig", ROWS).rearrange("p (k j) -> p j k", k=2), ALU.add))
                step(V.tensor_tensor(
                    ohk[:, :, :, :].rearrange("p k j e -> p (k j) e"),
                    cview(m, "iota64", ROWS)[:, None, 0:E2].broadcast_to([ROWS, NK, E2]),
                    idf[:, :, :].rearrange("p k j -> p (k j)")[:, :, None].broadcast_to([ROWS, NK, E2]),
                    ALU.is_equal))
                step(V.tensor_tensor(mk[:, :, :], ohk[:, 0, :, :], ohk[:, 1, :, :], ALU.add), mk_ready, i + 1)
                dve.wait_ge(ex_ready, i + 1)
                step(V.tensor_scalar(wk[:, 1, :], ex[:, :], 1.0, None, ALU.add))
                step(V.reciprocal(wk[:, 0, :], wk[:, 1, :]))
                step(V.tensor_tensor(wk[:, 1, :], wk[:, 0, :], ex[:, :], ALU.mult))
                step(V.tensor_scalar(m.wts2[:, bass.ds(i - 1, 1), :].rearrange("p a n -> p (a n)"),
                                     wk[:, :, :].rearrange("p k j -> p (k j)"), 1.0, None, ALU.mult))
                dve.wait_ge(pos_mm, i + 1)
                pos = pb[0:ROWS, 3, 0:TILES * E2].rearrange("p (j e) -> p j e", j=TILES)
                step(V.tensor_copy(m.carry2[:, :], pb[0:1, 3, TILES * E2:TILES * E2 + E2]))
                step(V.tensor_tensor(so[:, :, :], pos,
                                     cview(m, "eoff2", ROWS)[:, None, :].broadcast_to([ROWS, TILES, E2]), ALU.add))
                for k in range(2):
                    step(V.tensor_tensor(ohk[:, k, :, :], ohk[:, k, :, :], so[:, :, :], ALU.mult))
                step(V.tensor_reduce(slf[:, :], ohk[:, :, :, :].rearrange("p k j e -> p (k j) e"), AX_X, ALU.add))
                step(V.tensor_scalar(m.slots2[:, bass.ds(i - 1, 1), :].rearrange("p a n -> p (a n)"), slf[:, :],
                                     float(SLOTS2), None, ALU.add))
                step(V.tensor_scalar(sli[:, :], slf[:, :], float(SLOTS2), None, ALU.add), slot_ready, i + 1)
                assert step.n == STEPS, step.n


def mixture_phase(nc, m, d, ctx):
    with ExitStack() as own:
        def sb(name, shape, dt=F32):
            return own.enter_context(nc.sbuf_tensor(name, shape, dt))

        WAYS = 4
        ways = range(WAYS)

        def sem(name):
            return ctx.enter_context(nc.semaphore("t_" + name))

        def sems(name):
            return [sem(f"{name}{n}") for n in ways]

        ident = cview(m, "ident")
        nt, se, be, lo = sb("t_tiles", [1, E2]), sb("t_start", [1, E2]), sb("t_base", [1, E2]), sb("t_lower", [1, E2, E2])
        big, big2 = sb("t_big", [1, MT2, E2]), sb("t_big2", [1, MT2, E2])
        fe, fr, ff, fw = (sb(f"t_f{n}", [1, MT2]) for n in range(4))
        tabe, tabr = (sb(f"t_tab{n}", [1, MT2], I32) for n in range(2))
        mv, dl, dls = sb("t_firsts", [1, E2 + 1]), sb("t_moves", [1, E2 + 1]), sb("t_moves_all", [ROWS, E2 + 1])
        slf, acc, mov = (sb(f"t_slots{n}", [ROWS, PAIRS * 2 * TILES]) for n in range(3))
        zb, zi, zt = sb("t_tail_f", [1, E2]), sb("t_tail", [1, E2], I32), sb("t_zeros", [128, HID])
        xr = [sb(f"t_rows{n}", [128, HID]) for n in ways]; xT = [sb(f"t_xT{n}", [128, 128]) for n in ways]
        th = [sb(f"t_tanh{n}", [128, EH2]) for n in ways]; hh = [sb(f"t_hid{n}", [128, EH2]) for n in ways]
        hT = [sb(f"t_hidT{n}", [128, 2, 128]) for n in ways]; ys = [sb(f"t_out{n}", [128, HID]) for n in ways]
        gps = [own.enter_context(nc.psum_tensor(f"t_gu{n}", [128, 2, EH2], F32)) for n in ways]
        tps = [own.enter_context(nc.psum_tensor(f"t_tr{n}", [128, 4, 128], F32)) for n in ways]
        moves_mm, moves_ready, own_p = sem("moves_mm"), sem("moves_ready"), sem("pool")
        own_t, table_ready, zeroed, tails = sem("dve"), sem("table_ready"), sem("zeroed"), sem("tails")
        loaded, t_mm, xT_ready, gu_mm = sems("loaded"), sem("t_mm"), sem("xT_ready"), sem("gu_mm")
        th_ready, a_ready, h_ready, hT_mm = sem("th_ready"), sem("a_ready"), sem("h_ready"), sem("hT_mm")
        hT_ready, y_mm, y_ready, stored = sem("hT_ready"), sem("y_mm"), sem("y_ready"), sems("stored")
        block = own.enter_context(nc.Block())
        N = MT2 // WAYS

        @block.gpsimd
        def _(pool):
            nc.gpsimd.memset(zt[:, :], 0.0).then_inc(zeroed, 1)
            pool.wait_ge(moves_ready, 1)
            step = Steps(pool, own_p)
            all_slots = m.slots2[:, :, :].rearrange("p a n -> p (a n)")
            step(nc.gpsimd.tensor_copy(slf[:, :], all_slots))
            step(nc.gpsimd.tensor_scalar(acc[:, :], slf[:, :], dls[:, 0:1], None, ALU.add))
            for e in range(1, E2 + 1):
                step(nc.gpsimd.tensor_scalar(mov[:, :], slf[:, :], float(REG2 * e), dls[:, e:e + 1], ALU.is_ge, ALU.mult))
                step(nc.gpsimd.tensor_tensor(acc[:, :], acc[:, :], mov[:, :], ALU.add))
            step(nc.gpsimd.tensor_copy(all_slots, acc[:, :]))

        @block.sync
        def _(sp):
            for n in ways:
                sp.sem_inc(loaded[n], 16)
                sp.sem_inc(stored[n], 16)
            for s in (t_mm, xT_ready, gu_mm, th_ready, a_ready, h_ready, hT_mm, hT_ready, y_mm, y_ready):
                sp.sem_inc(s, WAYS)
            sp.wait_ge(zeroed, 1)
            sp.wait_ge(table_ready, 1)
            for e in range(E2):
                at = sp.value_load(zi[0:1, e:e + 1], min_val=0, max_val=SLOTS2 - 128)
                sp.dma_start(d["buf2"][bass.ds(at, 128), :], zt[:, :]).then_inc(tails, 16)
            sp.wait_ge(tails, 16 * E2)
            with sp.Fori(1, N + 1) as i:
                for n in ways:
                    sp.wait_ge(t_mm, WAYS * i)
                    at = sp.value_load(tabr[0:1, bass.ds(WAYS * i + (n - WAYS), 1)], min_val=0, max_val=SLOTS2)
                    sp.dma_start(xr[n][:, :], d["buf2"][bass.ds(at, 128), :]).then_inc(loaded[n], 16)

        @block.tensor
        def _(pe):
            T = nc.tensor
            pe.wait_ge(table_ready, 1)
            T.matmul(tps[0][0:ROWS, 0, 0:E2 + 1], lhsT=cview(m, "ones")[0:1, 0:ROWS], rhs=dl[:, :],
                     start=True, stop=True).then_inc(moves_mm, 1)
            pe.wait_ge(moves_ready, 1)
            with pe.Fori(1, N + 1) as i:
                for n in ways:
                    pe.wait_ge(loaded[n], 16 * i + 16)
                    pe.wait_ge(y_ready, WAYS * i)
                    T.transpose(tps[n][:, 0, :], xr[n][:, :], ident).then_inc(t_mm, 1)
                experts = [pe.value_load(tabe[0:1, bass.ds(WAYS * i + (n - WAYS), 1)], min_val=0, max_val=E2 - 1) for n in ways]
                for n in ways:
                    pe.wait_ge(xT_ready, WAYS * i + (n + 1))
                    pe.wait_ge(h_ready, WAYS * i)
                    T.matmul(gps[n][:, :, :].rearrange("p a c -> p (a c)"), lhsT=xT[n][:, :],
                             rhs=m.wgu[:, bass.ds(experts[n], 1), :].rearrange("p a c -> p (a c)"),
                             start=True, stop=True).then_inc(gu_mm, 1)
                for n in ways:
                    pe.wait_ge(h_ready, WAYS * i + (n + 1))
                    for c in range(2):
                        last = T.transpose(tps[n][:, 1 + c, :], hh[n][:, 128 * c:128 * c + 128], ident)
                    last.then_inc(hT_mm, 1)
                for n in ways:
                    pe.wait_ge(hT_ready, WAYS * i + (n + 1))
                    for c in range(2):
                        last = T.matmul(tps[n][:, 3, :], lhsT=hT[n][:, c, :],
                                        rhs=m.wd[:, bass.ds(experts[n], 1), c, :].rearrange("p a c -> p (a c)"),
                                        start=(c == 0), stop=(c == 1))
                    last.then_inc(y_mm, 1)

        @block.scalar
        def _(act):
            A = nc.scalar
            act.wait_ge(table_ready, 1)
            with act.Fori(1, N + 1) as i:
                for n in ways:
                    act.wait_ge(t_mm, WAYS * i + (n + 1))
                    A.activation(xT[n][:, :], tps[n][:, 0, :], ACT.Copy).then_inc(xT_ready, 1)
                for n in ways:
                    act.wait_ge(gu_mm, WAYS * i + (n + 1))
                    A.activation(th[n][:, :], gps[n][:, 0, :], ACT.Tanh, scale=0.5).then_inc(th_ready, 1)
                for n in ways:
                    act.wait_ge(y_mm, WAYS * i + (n + 1))
                    act.wait_ge(stored[n], 16 * i)
                    A.activation(ys[n][:, :], tps[n][:, 3, :], ACT.Copy).then_inc(y_ready, 1)
                for n in ways:
                    act.wait_ge(y_ready, WAYS * i + (n + 1))
                    act.dma_start(d["y2"][bass.ds((WAYS * i + (n - WAYS)) * 128, 128), :], ys[n][:, :]).then_inc(stored[n], 16)
            for n in ways:
                act.wait_ge(stored[n], 16 * (N + 1))

        @block.vector
        def _(dve):
            V = nc.vector
            step = Steps(dve, own_t)
            step(V.tensor_copy(lo[:, :, :], cview(m, "lower8", 1).rearrange("p (a b) -> p a b", a=E2)))
            step(V.tensor_scalar(nt[:, :], m.carry2[:, :], 1.0 / 128, 127.0 / 256, ALU.mult, ALU.add))
            step(V.tensor_scalar(nt[:, :], nt[:, :], ROUND, None, ALU.add))
            step(V.tensor_scalar(nt[:, :], nt[:, :], ROUND, None, ALU.subtract))
            step(V.tensor_tensor(lo[:, :, :], lo[:, :, :], nt[:, None, :].broadcast_to([1, E2, E2]), ALU.mult))
            step(V.tensor_reduce(se[:, :], lo[:, :, :], AX_X, ALU.add))
            step(V.scalar_tensor_tensor(out=be[:, :], in0=se[:, :], scalar=-128.0, in1=cview(m, "eoff2", 1),
                                        op0=ALU.mult, op1=ALU.add))
            step(V.tensor_tensor(nt[:, :], nt[:, :], se[:, :], ALU.add))
            index = cview(m, "tile_index", 1)
            wide = lambda t: t[:, :, None].broadcast_to([1, MT2, E2])
            each = lambda t: t[:, None, :].broadcast_to([1, MT2, E2])
            step(V.tensor_tensor(big[:, :, :], each(nt[:, :]), wide(index), ALU.is_le))
            step(V.tensor_reduce(fe[:, :], big[:, :, :], AX_X, ALU.add))
            step(V.tensor_tensor(big[:, :, :], each(cview(m, "iota64", 1)[:, 0:E2]), wide(fe[:, :]), ALU.is_equal))
            step(V.tensor_reduce(ff[:, :], big[:, :, :], AX_X, ALU.add))
            step(V.tensor_tensor(big2[:, :, :], big[:, :, :], each(be[:, :]), ALU.mult))
            step(V.tensor_reduce(fr[:, :], big2[:, :, :], AX_X, ALU.add))
            step(V.tensor_tensor(fw[:, :], ff[:, :], index, ALU.mult))
            step(V.scalar_tensor_tensor(out=fr[:, :], in0=fw[:, :], scalar=128.0, in1=fr[:, :], op0=ALU.mult, op1=ALU.add))
            step(V.tensor_scalar(tabr[:, :], fr[:, :], float(SLOTS2), None, ALU.add))
            step(V.tensor_scalar(mv[:, 0:E2], se[:, :], 128.0, None, ALU.mult))
            step(V.memset(mv[:, E2:E2 + 1], float(128 * MT2)))
            step(V.tensor_scalar(dl[:, 0:1], mv[:, 0:1], 1.0, None, ALU.mult))
            step(V.tensor_tensor(dl[:, 1:], mv[:, 1:], mv[:, 0:E2], ALU.subtract))
            step(V.tensor_scalar(dl[:, 1:], dl[:, 1:], float(-REG2), None, ALU.add))
            step(V.tensor_scalar(tabe[:, :], fe[:, :], float(E2 - 1), None, ALU.min))
            step(V.scalar_tensor_tensor(out=zb[:, :], in0=m.carry2[:, :], scalar=float(SLOTS2), in1=cview(m, "eoff2", 1),
                                        op0=ALU.add, op1=ALU.add))
            step(V.tensor_copy(zi[:, :], zb[:, :]), table_ready, 1)
            dve.wait_ge(moves_mm, 1)
            step(V.tensor_copy(dls[:, :], tps[0][0:ROWS, 0, 0:E2 + 1]), moves_ready, 1)
            with dve.Fori(1, N + 1) as i:
                for n in ways:
                    dve.wait_ge(th_ready, WAYS * i + (n + 1))
                    V.scalar_tensor_tensor(out=th[n][:, :], in0=th[n][:, :], scalar=1.0, in1=gps[n][:, 0, :],
                                           op0=ALU.add, op1=ALU.mult).then_inc(a_ready, 1)
                    dve.wait_ge(a_ready, WAYS * i + (n + 1))
                    V.tensor_tensor(hh[n][:, :], th[n][:, :], gps[n][:, 1, :], ALU.mult).then_inc(h_ready, 1)
                for n in ways:
                    dve.wait_ge(hT_mm, WAYS * i + (n + 1))
                    V.tensor_copy(hT[n][:, :, :], tps[n][:, 1:3, :]).then_inc(hT_ready, 1)


def output_phase(nc, m, d, ctx):
    with ExitStack() as own:
        def sem(name):
            return ctx.enter_context(nc.semaphore("o_" + name))

        NK = 2 * TILES
        sl = own.enter_context(nc.sbuf_tensor("o_slots", [ROWS, NK], I32))
        wt = own.enter_context(nc.sbuf_tensor("o_wts", [ROWS, NK], F32))
        ga = own.enter_context(nc.sbuf_tensor("o_gathered", [ROWS, NK, HID], F32))
        o = own.enter_context(nc.sbuf_tensor("o_rows", [ROWS, TILES, HID], F32))
        idx_in, gathered, comb, stored, own_o, wt_in = (sem(n) for n in ("idx_in", "gathered", "comb", "stored", "dve", "wt_in"))
        block = own.enter_context(nc.Block())
        STEPS = NK - 1

        @block.gpsimd
        def _(pool):
            with pool.Fori(1, PAIRS + 1) as i:
                pool.wait_ge(comb, i)
                nc.gpsimd.tensor_copy(sl[:, :], m.slots2[:, bass.ds(i - 1, 1), :].rearrange("p a n -> p (a n)")).then_inc(idx_in, 1)
                pool.wait_ge(idx_in, i + 1)
                pool.nop(nofuse=True)
                for n in range(NK):
                    nc.gpsimd.indirect_dma_start(
                        out=ga[:, n, :], out_offset=None, in_=d["y2"],
                        in_offset=bass.IndirectOffsetOnAxis(ap=sl[:, n:n + 1], axis=0)).then_inc(gathered, 16)

        @block.vector
        def _(dve):
            V = nc.vector
            with dve.Fori(1, PAIRS + 1) as i:
                step = Steps(dve, own_o, i * STEPS)
                step(V.tensor_scalar(wt[:, :], m.wts2[:, bass.ds(i - 1, 1), :].rearrange("p a n -> p (a n)"), 1.0, None,
                                     ALU.mult), wt_in, i + 1)
                dve.wait_ge(gathered, i * (16 * NK))
                dve.wait_ge(stored, 32 * i)
                for n in range(NK):
                    j = n % TILES
                    base = m.hres[:, bass.ds(i - 1, 1), j, :].rearrange("p a c -> p (a c)") if n < TILES else o[:, j, :]
                    x = V.scalar_tensor_tensor(out=o[:, j, :], in0=ga[:, n, :], scalar=wt[:, n:n + 1], in1=base,
                                               op0=ALU.mult, op1=ALU.add)
                    if n < NK - 1:
                        step(x)
                    else:
                        step(x, comb, i + 1)
                assert step.n == STEPS

        @block.sync
        def _(sp):
            for s in (idx_in, comb, wt_in):
                sp.sem_inc(s, 1)
            sp.sem_inc(stored, 32)
            sp.sem_inc(own_o, STEPS)
            with sp.Fori(1, PAIRS + 1) as i:
                sp.wait_ge(comb, i + 1)
                for t in range(2):
                    n = ROWS - t
                    dst = d["out"][bass.ds(2 * i - 2, 2), ROWS * t:ROWS * t + n, :].rearrange("b s c -> s b c")
                    sp.dma_start(dst, o[0:n, t::2, :]).then_inc(stored, 16)
            sp.wait_ge(stored, 32 * (PAIRS + 1))


def program(nc, d):
    for k, shape in SCRATCH.items():
        d[k] = nc.dram_tensor("scratch_" + k, shape, F32).ap()
    with ExitStack() as ctx:
        m = memory(nc, ctx)
        for phase in (setup_phase, patch_phase, token_phase, expert_phase, ssm_phase, mixture_phase, output_phase):
            phase(nc, m, d, ctx)

def _layout(inputs):
    f = lambda k: np.asarray(inputs[k])
    a = {}
    x = f("x").reshape(BATCH, CHANS, GRID, PATCH, GRID, PATCH).transpose(0, 2, 4, 1, 3, 5)
    x = x.reshape(BATCH * NPATCH, PDIM)
    xp = np.zeros((BATCH * NPATCH, KCH * 128), x.dtype)
    xp[:, :PDIM] = x
    a["xpat"] = xp.reshape(2 * GROUPS, GB * NPATCH // 2, KCH, 128).transpose(0, 3, 2, 1)
    w = np.zeros((KCH * 128, HID), x.dtype)
    w[:PDIM] = f("L0_tok_W").T
    a["wtok"] = w.reshape(KCH, 128, HID).transpose(1, 0, 2)
    a["tokb"] = f("L0_tok_b")[:, None]
    a["cls"] = f("L0_tok_class_token").T
    a["posT"] = f("L0_tok_pos_embed").T
    a["ytxt"] = f("x_txt").reshape(PAIRS, 2 * NTEXT)
    a["emb"], a["cw"] = f("L0_txt_emb_weight"), f("L0_txt_conv_weight")[:, 0, :]

    def heads(ws, wp):
        ws, wp = ws.reshape(-1, HEADS, HD), wp.reshape(-1, HEADS, NPT)
        o = np.zeros((ws.shape[0], HEADS, 32), ws.dtype)
        o[:, :, 2:2 + HD], o[:, :, 2 + HD:2 + HD + NPT] = ws, wp
        return o.reshape(-1, 2, 128)

    a["wq"] = heads(f("L0_attn_wq"), f("L0_attn_wqp"))
    a["wk"] = heads(f("L0_attn_wk"), f("L0_attn_wkp"))
    a["brow"] = np.concatenate([heads(f("L0_attn_bq")[None], f("L0_attn_bqp")[None]).reshape(1, 256),
                                heads(f("L0_attn_bk")[None], f("L0_attn_bkp")[None]).reshape(1, 256)], axis=1)
    a["wv"], a["wo"] = f("L0_attn_wv"), f("L0_attn_wo")
    a["bv"], a["bo"] = f("L0_attn_bv")[None], f("L0_attn_bo")[None]
    a["lng"], a["lnb"] = f("L0_attn_ln_g")[:, None], f("L0_attn_ln_b")[:, None]
    a["pscale"] = f("L0_attn_pscale")[:, None]
    a["gatew"] = f("L0_ffn_gate_w").T
    a["sw13"] = np.concatenate([f("L0_ffn_sw1"), f("L0_ffn_sw3")], axis=1)
    a["sw2"] = f("L0_ffn_sw2")
    a["w13"] = np.concatenate([f("L0_ffn_w1"), f("L0_ffn_w3")], axis=2)
    a["w2"] = f("L0_ffn_w2")
    a["normw"], a["normb"] = f("L1_attn_norm_weight")[None], f("L1_attn_norm_bias")[None]
    a["ssm"] = np.stack([np.tile(f("L1_attn_" + k), 2) for k in ("lambda_re", "lambda_im", "p_re", "p_im")])[None]
    a["bc"] = np.stack([np.concatenate([f("L1_attn_b_re"), f("L1_attn_b_im")]),
                        np.concatenate([f("L1_attn_c_re"), f("L1_attn_c_im")])], axis=1)
    a["logstep"] = f("L1_attn_log_step").reshape(1, 1)
    a["dsc"] = f("L1_attn_d").reshape(1, 1)
    a["outw"] = np.concatenate([f("L1_attn_out_w").T, f("L1_attn_out2_w").T], axis=1)
    a["outb"] = np.concatenate([f("L1_attn_out_b"), f("L1_attn_out2_b")])[None]
    a["rtw"] = f("L1_ffn_router_w").T
    a["wgu"] = np.concatenate([f("L1_ffn_w_gate"), f("L1_ffn_w_up")], axis=2).transpose(1, 0, 2)
    a["wd"] = f("L1_ffn_w_down").reshape(E2, 2, 128, HID).transpose(2, 0, 1, 3)
    a["cst"] = CONSTS
    return {k: np.ascontiguousarray(v) for k, v in a.items()}


SCRATCH = {"buf1": [SLOTS1, HID], "y1": [SLOTS1 + 128, HID], "buf2": [SLOTS2 + 128, HID],
           "y2": [128 * MT2 + 128, HID], "kpad": [1, SEQ + SEQP]}


def kernel(**inputs):
    import concourse.bacc as bacc
    from concourse.bass_utils import run_bass_kernel_spmd

    nc = bacc.Bacc("TRN2", target_bir_lowering=False, num_devices=1)
    arrays = _layout(inputs)
    d = {k: nc.dram_tensor("in_" + k, v.shape, mybir.dt.from_np(v.dtype), kind="ExternalInput").ap()
         for k, v in arrays.items()}
    d["out"] = nc.dram_tensor("out", [BATCH, SEQ, HID], F32, kind="ExternalOutput").ap()
    program(nc, d)
    r = run_bass_kernel_spmd(nc, [{"in_" + k: v for k, v in arrays.items()}], core_ids=[0])
    return r.results[0]["out"]
```

```python
from contextlib import ExitStack

import numpy as np
import concourse.bass as bass
from concourse import mybir

F32 = mybir.dt.float32
BF16 = mybir.dt.bfloat16
I32 = mybir.dt.int32
U32 = mybir.dt.uint32
ALU = mybir.AluOpType
ACT = mybir.ActivationFunctionType
AX_X = mybir.AxisListType.X

BATCH, CHANS, IMG, PATCH = 64, 3, 224, 28
GRID = IMG // PATCH
NPATCH = GRID * GRID
PDIM = CHANS * PATCH * PATCH
HID = 128
NTEXT = 128
SEQ = 1 + NPATCH + NTEXT
SEQP = SEQ + 1
ROWS = SEQP // 2
PAIRS = BATCH // 2
TILES = 4
COLS = 2 * SEQP
KCH = -(-PDIM // 128)
GROUPS, GB = 8, 8
VOCAB = 125
HEADS, HD, NPT = 8, 16, 12
EPS = 1e-5
E1, CAP, EH = 64, 256, 64
SLOTS1 = E1 * CAP
E2, EH2 = 8, 256
REG2 = BATCH * SEQ + 128
SLOTS2 = E2 * REG2
MT2 = (2 * BATCH * SEQ) // 128 + E2
MT2 += -MT2 % 4
ROUTE_SCALE = 2.5
NST = 64
ROUND = 1.5 * 2.0 ** 23

CONST_COLS = {}


def constants():
    parts = {}
    p = np.arange(128)
    parts["ident"] = np.eye(128)
    parts["ones"] = np.ones((128, 128))
    tri = np.zeros((128, ROWS))
    tri[:ROWS] = (np.arange(ROWS)[:, None] < np.arange(ROWS)[None, :])
    parts["tri"] = tri
    rev = np.zeros((128, ROWS))
    rev[:ROWS] = np.eye(ROWS)[::-1]
    parts["rev"] = rev
    jm = np.zeros((128, 128))
    for n in range(NST):
        jm[n, n + NST] = -1.0
        jm[n + NST, n] = 1.0
    parts["jmat"] = jm
    hsel = np.zeros((128, 2, 128))
    for h in range(HEADS):
        hsel[h, h // 4, 32 * (h % 4):32 * (h % 4) + 32] = 1.0
    parts["hsel"] = hsel.reshape(128, 256)
    q = p % 32
    parts["row0"] = (q == 0)[:, None]
    parts["row1"] = (q == 1)[:, None]
    parts["rows_s"] = ((q >= 2) & (q < 2 + HD))[:, None]
    parts["rows_p"] = ((q >= 2 + HD) & (q < 2 + HD + NPT))[:, None]
    sel = np.zeros((128, 2, 128))
    for a in p:
        if 2 + HD <= a % 32 < 2 + HD + NPT:
            sel[a, 0, 32 * (a // 32)] = 1.0
            sel[a, 1, 32 * (a // 32) + 1] = 1.0
    parts["psel"] = sel.reshape(128, 256)
    parts["vocab"] = p[:, None]
    parts["iota64"] = np.tile(np.arange(E1), (128, 1))
    parts["eoff1"] = np.tile(CAP * np.arange(E1) - SLOTS1, (128, 1))
    parts["eoff2"] = np.tile(REG2 * np.arange(E2) - SLOTS2, (128, 1))
    pad = np.zeros((128, 2, TILES))
    pad[ROWS - 1, :, 1::2] = 1000.0
    parts["padbig"] = pad.reshape(128, 2 * TILES)
    half = (np.arange(128) >= NST).astype(float)
    ma = np.zeros((128, 128)); ma[0] = 1 - half; ma[1] = half
    mb = np.zeros((128, 128)); mb[0] = half; mb[1] = half - 1
    parts["mask_a"], parts["mask_b"] = ma, mb
    parts["csign"] = (1.0 - 2.0 * (p >= NST))[:, None]
    tix = np.zeros((128, MT2)); tix[:] = np.arange(MT2)
    parts["tile_index"] = tix
    parts["lower8"] = np.zeros((128, 64))
    parts["lower8"][0] = (np.arange(8)[None, :] < np.arange(8)[:, None]).reshape(64)
    at, cols = 0, {}
    for k, v in parts.items():
        cols[k] = (at, v.shape[1])
        at += v.shape[1]
    return np.concatenate([np.asarray(v, np.float32) for v in parts.values()], axis=1), cols


CONSTS, CONST_COLS = constants()
NCONST = CONSTS.shape[1]


class Memory:
    pass


class Steps:

    def __init__(self, eng, own, base=0, start=0):
        self.eng, self.own, self.base, self.n = eng, own, base, start

    def __call__(self, ins, signal=None, value=None):
        if signal is None:
            self.n += 1
            signal, value = self.own, self.base + self.n
        ins.then_inc(signal, 1)
        self.eng.wait_ge(signal, value)


def memory(nc, ctx):
    m = Memory()

    def sb(name, shape, dt=F32):
        return ctx.enter_context(nc.sbuf_tensor(name, shape, dt))

    m.cst = sb("cst", [128, NCONST])
    m.tok = sb("tok", [128, BATCH * NPATCH])
    m.hres = sb("hres", [ROWS, PAIRS, TILES, HID])
    m.slots1 = sb("slots1", [ROWS, PAIRS, 2 * TILES], I32)
    m.wts1 = sb("wts1", [ROWS, PAIRS, 2 * TILES])
    m.slots2 = sb("slots2", [ROWS, PAIRS, 2 * TILES], I32)
    m.wts2 = sb("wts2", [ROWS, PAIRS, 2 * TILES])
    m.wq = sb("wq", [128, 2, 128]); m.wk = sb("wk", [128, 2, 128]); m.wv = sb("wv", [128, 128]); m.wo = sb("wo", [128, 128])
    m.bo_row = sb("bo_row", [1, 128]); m.biasq = sb("biasq", [128, 2]); m.biask = sb("biask", [128, 2])
    m.rawq = sb("rawq", [128, 2]); m.rawk = sb("rawk", [128, 2]); m.scaleq = sb("scaleq", [128, 2])
    m.esq = sb("esq", [128, 2, 128]); m.esk = sb("esk", [128, 2, 128])
    m.embt = sb("embt", [VOCAB, 128]); m.convq = sb("convq", [128, 2])
    m.posT = sb("posT", [128, 1 + NPATCH]); m.tokb = sb("tokb", [128, 1])
    m.gatew = sb("gatew", [128, E1]); m.sw13 = sb("sw13", [128, 256]); m.sw2 = sb("sw2", [128, 128])
    m.outw = sb("outw", [128, 256]); m.outb = sb("outb", [1, 256])
    m.normw = sb("normw", [ROWS, 128]); m.normb = sb("normb", [ROWS, 128])
    m.toep = sb("toep", [ROWS, 2, SEQP])
    m.rtw = sb("rtw", [128, E2])
    m.wgu = sb("wgu", [128, E2, 2 * EH2]); m.wd = sb("wd", [128, E2, 2, 128])
    m.tri_bf = sb("tri_bf", [ROWS, ROWS], BF16); m.ones_bf = sb("ones_bf", [ROWS, ROWS], BF16)
    m.carry = sb("carry", [1, E1]); m.carry2 = sb("carry2", [1, E2])
    m.hT0, m.hT1 = (sb(f"hT{n}", [128, 2, SEQP]) for n in range(2))
    return m


def cview(m, name, rows=128):
    a, n = CONST_COLS[name]
    return m.cst[0:rows, a:a + n]


def setup_phase(nc, m, d, ctx):
    with ExitStack() as own:
        def sb(name, shape, dt=F32):
            return own.enter_context(nc.sbuf_tensor(name, shape, dt))

        sems = []

        def sem(name):
            sems.append(nc.alloc_semaphore(name))
            return sems[-1]

        ps = [own.enter_context(nc.psum_tensor(f"setup_ps{n}", [128, 512], F32)) for n in range(4)]
        emb = sb("emb", [VOCAB, 128]); cw = sb("cw", [128, 2])
        lng = sb("lng", [128, 1]); lnb = sb("lnb", [128, 1])
        brow = sb("brow", [1, 512]); bvrow = sb("bvrow", [1, 128]); borow = sb("borow", [1, 128])
        psc = sb("psc", [HEADS, 1]); psr = sb("psr", [128, 2]); npsr = sb("npsr", [128, 2])
        clsc = sb("clsc", [128, 1])
        ssm = sb("ssm", [2, 4, 128])
        bc = sb("bc", [128, 2])
        ls = sb("ls", [128, 1]); dsc = sb("dsc", [1, 1])
        tq = sb("tq", [128, 8]); tqe = sb("tqe", [128, 128]); tqc = sb("tqc", [128, 2])
        zrow = sb("zrow", [128, 2048])
        z = sb("ssm_z", [2, 20, 128]); z1 = sb("ssm_z1", [2, 12]); zc = sb("ssm_cols", [128, 6])
        a0 = sb("a0", [128, 128]); a0t = sb("a0t", [128, 128])
        a1 = sb("a1", [128, 128]); a1t = sb("a1t", [128, 128])
        pw = sb("pw", [128, 2, 128]); qw = sb("qw", [128, 2, 128])
        vm = sb("vm", [128, 256]); krow = sb("krow", [1, SEQP]); hank = sb("hank", [ROWS, 2, SEQP])
        bvc = sb("bvc", [128, 1])

        ld = sem("setup_loaded"); zs = sem("scratch_zeroed"); kst = sem("kernel_stored")
        hk = sem("hankel_loaded"); zz = sem("zero_row_set"); own_step = sem("setup_dve_step")
        exp_done = sem("step_size_ready")
        scale_mm, bias_mm, bv_mm, bo_mm = sem("scale_mm"), sem("bias_mm"), sem("bv_mm"), sem("bo_mm")
        amax_t, qscale_mm, ssm_mm, ab_mm = sem("amax_t"), sem("qscale_mm"), sem("ssm_mm"), sem("ab_mm")
        power_mm, kern_mm, toep_mm = sem("power_mm"), sem("kern_mm"), sem("toep_mm")
        bv_ready, amax_ready, qscale_ready = sem("bv_ready"), sem("amax_ready"), sem("qscale_ready")
        rank2_ready, a_ready, v0_ready = sem("rank2_ready"), sem("a_ready"), sem("v0_ready")
        power_ready, kern_ready = sem("power_ready"), sem("kern_ready")

        loads = [(m.cst[:, :], d["cst"]), (m.wq[:, :, :], d["wq"]), (m.wk[:, :, :], d["wk"]),
                 (m.wv[:, :], d["wv"]), (m.wo[:, :], d["wo"]), (brow[:, :], d["brow"]),
                 (bvrow[:, :], d["bv"]), (borow[:, :], d["bo"]), (psc[:, :], d["pscale"]),
                 (emb[:, :], d["emb"]), (cw[:, :], d["cw"]), (lng[:, :], d["lng"]), (lnb[:, :], d["lnb"]),
                 (m.posT[:, :], d["posT"]), (m.tokb[:, :], d["tokb"]), (clsc[:, :], d["cls"]),
                 (m.gatew[:, :], d["gatew"]), (m.sw13[:, :], d["sw13"]), (m.sw2[:, :], d["sw2"]),
                 (m.outw[:, :], d["outw"]), (m.outb[:, :], d["outb"]),
                 (m.normw[:, :], d["normw"].broadcast_to([ROWS, 128])),
                 (m.normb[:, :], d["normb"].broadcast_to([ROWS, 128])),
                 (m.rtw[:, :], d["rtw"]), (m.wgu[:, :, :], d["wgu"]), (m.wd[:, :, :, :], d["wd"]),
                 (ssm[:, :, :], d["ssm"].broadcast_to([2, 4, 128])), (bc[:, :], d["bc"]),
                 (ls[:, :], d["logstep"].broadcast_to([128, 1])), (dsc[:, :], d["dsc"])]

        ident, ones = cview(m, "ident"), cview(m, "ones")
        row0, row1 = cview(m, "row0"), cview(m, "row1")
        block = own.enter_context(nc.Block())

        @block.sync
        def _(sp):
            for dst, src in loads:
                sp.dma_start(dst, src, allow_slow_non_contiguous=True).then_inc(ld, 16)
            sp.wait_ge(zz, 1)
            for n in range(SLOTS1 // 2048):
                sp.dma_start(d["buf1"][2048 * n:2048 * n + 2048, :].rearrange("(p a) c -> p (a c)", p=128),
                             zrow[:, :]).then_inc(zs, 16)
            sp.dma_start(d["y1"][SLOTS1:SLOTS1 + 128, :], zrow[:, 0:128]).then_inc(zs, 16)
            sp.dma_start(d["buf2"][SLOTS2:SLOTS2 + 128, :], zrow[:, 0:128]).then_inc(zs, 16)
            sp.dma_start(d["y2"][128 * MT2:128 * MT2 + 128, :], zrow[:, 0:128]).then_inc(zs, 16)
            sp.dma_start(d["kpad"][0:1, 0:SEQ], zrow[0:1, 0:SEQ]).then_inc(kst, 16)
            sp.wait_ge(kern_ready, 1)
            sp.dma_start(d["kpad"][0:1, SEQ:SEQ + SEQP], krow[:, :]).then_inc(kst, 16)
            sp.wait_ge(kst, 32)
            for a in range(2):
                src = bass.AP(tensor=d["kpad"].tensor, offset=ROWS * (1 - a), ap=[[1, ROWS], [1, SEQP]])
                sp.dma_start(hank[:, a, :], src).then_inc(hk, 16)
            sp.wait_ge(zs, 16 * (SLOTS1 // 2048 + 3))

        @block.gpsimd
        def _(pool):
            nc.gpsimd.memset(zrow[:, :], 0.0).then_inc(zz, 1)
        @block.scalar
        def _(act):
            act.wait_ge(ld, 16 * len(loads))
            nc.scalar.activation(zc[:, 0:1], ls[:, :], ACT.Exp).then_inc(exp_done, 1)

        doublings = []
        n = 1
        while n < SEQP:
            doublings.append((n, min(n, SEQP - n)))
            n *= 2

        @block.tensor
        def _(pe):
            T = nc.tensor
            pe.wait_ge(ld, 16 * len(loads))
            for g in range(2):
                last = T.matmul(ps[0][:, g:g + 1], lhsT=cview(m, "hsel")[0:HEADS, 128 * g:128 * g + 128],
                                rhs=psc[:, :], start=True, stop=True)
            last.then_inc(scale_mm, 1)
            for n, w in ((0, m.wq), (2, m.wk)):
                for g in range(2):
                    T.matmul(ps[1][:, n + g:n + g + 1], lhsT=w[:, g, :], rhs=lnb[:, :], start=True, stop=False)
                    last = T.matmul(ps[1][:, n + g:n + g + 1], lhsT=brow[:, 128 * (n + g):128 * (n + g) + 128],
                                    rhs=ones[0:1, 0:1], start=False, stop=True)
            last.then_inc(bias_mm, 1)
            T.matmul(ps[2][:, 0:1], lhsT=m.wv[:, :], rhs=lnb[:, :], start=True, stop=False)
            T.matmul(ps[2][:, 0:1], lhsT=bvrow[:, :], rhs=ones[0:1, 0:1], start=False, stop=True).then_inc(bv_mm, 1)
            pe.wait_ge(bv_ready, 1)
            T.matmul(ps[2][0:1, 0:128], lhsT=bvc[:, :], rhs=m.wo[:, :], start=True, stop=True).then_inc(bo_mm, 1)
            for n, rows in enumerate((VOCAB, 128)):
                pe.wait_ge(amax_ready, n + 1)
                T.transpose(ps[3][0:1, 0:rows], tq[0:rows, 0:1], ident[0:rows, 0:rows]).then_inc(amax_t, 1)
                pe.wait_ge(qscale_ready, n + 1)
                T.matmul(ps[3][:, 256:257], lhsT=ones[0:1, :], rhs=tq[0:1, 2:3],
                         start=True, stop=True).then_inc(qscale_mm, 1)
            pe.wait_ge(rank2_ready, 1)
            for n, row in enumerate((z[0:1, 3, :], z[0:1, 4, :], ssm[0:1, 0, :], ssm[0:1, 1, :])):
                T.matmul(ps[0][:, 8 + n:9 + n], lhsT=row, rhs=ones[0:1, 0:1], start=True, stop=True)
            for n, (a, b) in enumerate(((12, 13), (13, 12), (14, 14))):
                last = T.matmul(ps[1][:, 128 * n:128 * n + 128], lhsT=z[:, a, :], rhs=z[:, b, :], start=True, stop=True)
            last.then_inc(ssm_mm, 1)
            pe.wait_ge(a_ready, 1)
            T.matmul(ps[2][:, 0:128], lhsT=a1t[:, :], rhs=a0[:, :], start=True, stop=True)
            T.matmul(ps[2][:, 128:256], lhsT=a0[:, :], rhs=a1t[:, :], start=True, stop=True)
            T.matmul(ps[2][:, 256:257], lhsT=a1t[:, :], rhs=bc[:, 0:1], start=True, stop=True).then_inc(ab_mm, 1)
            pe.wait_ge(v0_ready, 1)
            for k, (n, c) in enumerate(doublings):
                pe.wait_ge(power_ready, k)
                last = T.matmul(ps[k % 2][:, 0:c], lhsT=qw[:, k % 2, :], rhs=vm[:, 0:c], start=True, stop=True)
                if k < len(doublings) - 1:
                    T.matmul(ps[k % 2][:, 128:256], lhsT=qw[:, k % 2, :], rhs=pw[:, k % 2, :], start=True, stop=True)
                    last = T.matmul(ps[k % 2][:, 256:384], lhsT=pw[:, k % 2, :], rhs=qw[:, k % 2, :],
                                    start=True, stop=True)
                last.then_inc(power_mm, 1)
            pe.wait_ge(power_ready, len(doublings))
            T.matmul(ps[2][0:1, 0:SEQP], lhsT=bc[:, 1:2], rhs=vm[:, 0:SEQP], start=True, stop=True).then_inc(kern_mm, 1)
            pe.wait_ge(hk, 32)
            for a in range(2):
                last = T.matmul(ps[3][0:ROWS, SEQP * a:SEQP * a + SEQP], lhsT=cview(m, "rev", ROWS),
                                rhs=hank[:, a, :], start=True, stop=True)
            last.then_inc(toep_mm, 1)

        @block.vector
        def _(dve):
            V = nc.vector
            step = Steps(dve, own_step)
            dve.wait_ge(ld, 16 * len(loads))
            dve.wait_ge(scale_mm, 1)
            step(V.tensor_copy(psr[:, :], ps[0][:, 0:2]))
            step(V.tensor_scalar(npsr[:, :], psr[:, :], -1.0, None, ALU.mult))
            for g in range(2):
                sc = m.scaleq[:, g:g + 1]
                step(V.tensor_scalar(sc, psr[:, g:g + 1], 2.0, cview(m, "rows_p"), ALU.mult, ALU.mult))
                step(V.scalar_tensor_tensor(out=sc, in0=cview(m, "rows_s"), scalar=float(HD) ** -0.5, in1=sc,
                                            op0=ALU.mult, op1=ALU.add))
                step(V.tensor_tensor(sc, sc, row0, ALU.add))
                for k, es in ((0, m.esq), (1, m.esk)):
                    step(V.tensor_scalar(es[:, g, :], cview(m, "psel")[:, 128 * k:128 * k + 128],
                                         npsr[:, g:g + 1], None, ALU.mult))
            dve.wait_ge(bias_mm, 1)
            step(V.tensor_copy(m.rawq[:, :], ps[1][:, 0:2]))
            step(V.tensor_copy(m.rawk[:, :], ps[1][:, 2:4]))
            step(V.tensor_tensor(m.biasq[:, :], m.rawq[:, :], m.scaleq[:, :], ALU.mult))
            step(V.tensor_scalar(m.biasq[:, :], m.biasq[:, :], row1, None, ALU.add))
            step(V.tensor_scalar(m.biask[:, :], m.rawk[:, :], row0, None, ALU.add))
            dve.wait_ge(bv_mm, 1)
            step(V.tensor_copy(bvc[:, :], ps[2][:, 0:1]), bv_ready, 1)
            dve.wait_ge(bo_mm, 1)
            step(V.tensor_tensor(m.bo_row[:, :], borow[:, :], ps[2][0:1, 0:128], ALU.add))
            step(V.tensor_scalar(m.wq[:, :, :], m.wq[:, :, :], lng[:, 0:1], None, ALU.mult))
            step(V.tensor_scalar(m.wk[:, :, :], m.wk[:, :, :], lng[:, 0:1], None, ALU.mult))
            step(V.tensor_scalar(m.wv[:, :], m.wv[:, :], lng[:, 0:1], None, ALU.mult))
            step(V.tensor_scalar(m.sw2[:, :], m.sw2[:, :], 0.5, None, ALU.mult))
            step(V.tensor_scalar(m.wd[:, :, :, :], m.wd[:, :, :, :], 0.5, None, ALU.mult))
            step(V.tensor_scalar(m.outw[:, :], m.outw[:, :], 0.5, None, ALU.mult))
            step(V.tensor_copy(m.tri_bf[:, :], cview(m, "tri", ROWS)))
            step(V.memset(m.ones_bf[:, :], 1.0))
            step(V.memset(m.carry[:, :], 0.0))
            step(V.memset(m.carry2[:, :], 0.0))
            for h in (m.hT0, m.hT1):
                step(V.memset(h[:, :, SEQ:SEQP], 0.0))
                for b in range(2):
                    step(V.tensor_tensor(h[:, b, 0:1], clsc[:, :], m.posT[:, 0:1], ALU.mult))
            for n, (w, rows, out, t) in enumerate(((emb, VOCAB, m.embt, tqe), (cw, 128, m.convq, tqc))):
                t = t[0:rows, :]
                step(V.tensor_reduce(tq[0:rows, 0:1], w[:, :], AX_X, ALU.max, apply_absolute_value=True),
                     amax_ready, n + 1)
                dve.wait_ge(amax_t, n + 1)
                step(V.tensor_reduce(tq[0:1, 1:2], ps[3][0:1, 0:rows], AX_X, ALU.max))
                step(V.tensor_scalar(tq[0:1, 2:3], tq[0:1, 1:2], 1.0 / 127.0, None, ALU.mult), qscale_ready, n + 1)
                dve.wait_ge(qscale_mm, n + 1)
                step(V.tensor_copy(tq[:, 3:4], ps[3][:, 256:257]))
                step(V.reciprocal(tq[:, 4:5], tq[:, 3:4]))
                step(V.tensor_scalar(t, w[:, :], tq[0:rows, 4:5], None, ALU.mult))
                step(V.tensor_scalar(t, t, ROUND, None, ALU.add))
                step(V.tensor_scalar(t, t, ROUND, None, ALU.subtract))
                step(V.scalar_tensor_tensor(out=t, in0=t, scalar=tq[0:rows, 3:4], in1=w[:, :],
                                            op0=ALU.mult, op1=ALU.subtract))
                step(V.tensor_tensor(out[:, :], w[:, :], t, ALU.add))

            def Z(n):
                return z[:, n, :]

            def S(n):
                return z1[:, n:n + 1]

            def tt(o, a, b, op):
                step(V.tensor_tensor(o, a, b, op))

            lr, li, pr, pi = (ssm[:, n, :] for n in range(4))
            dve.wait_ge(exp_done, 1)
            step(V.reciprocal(zc[:, 1:2], zc[:, 0:1]))
            step(V.tensor_scalar(zc[:, 1:2], zc[:, 1:2], 2.0, None, ALU.mult))
            step(V.tensor_scalar(Z(0), lr, -1.0, zc[0:2, 1:2], ALU.mult, ALU.add))
            tt(Z(1), Z(0), Z(0), ALU.mult)
            tt(Z(2), li, li, ALU.mult)
            tt(Z(1), Z(1), Z(2), ALU.add)
            step(V.reciprocal(Z(2), Z(1)))
            tt(Z(3), Z(0), Z(2), ALU.mult)
            tt(Z(4), li, Z(2), ALU.mult)
            dr, di = Z(3), Z(4)
            tt(Z(9), dr, pr, ALU.mult)
            tt(Z(10), di, pi, ALU.mult)
            tt(Z(5), Z(9), Z(10), ALU.subtract)
            tt(Z(7), Z(9), Z(10), ALU.add)
            tt(Z(9), dr, pi, ALU.mult)
            tt(Z(10), di, pr, ALU.mult)
            tt(Z(6), Z(9), Z(10), ALU.add)
            tt(Z(8), Z(10), Z(9), ALU.subtract)
            tt(Z(9), Z(7), pr, ALU.mult)
            tt(Z(10), Z(8), pi, ALU.mult)
            tt(Z(9), Z(9), Z(10), ALU.subtract)
            step(V.tensor_reduce(S(0), z[:, 9, 0:NST], AX_X, ALU.add))
            step(V.tensor_scalar(S(0), S(0), 1.0, None, ALU.add))
            tt(Z(9), Z(7), pi, ALU.mult)
            tt(Z(10), Z(8), pr, ALU.mult)
            tt(Z(9), Z(9), Z(10), ALU.add)
            step(V.tensor_reduce(S(1), z[:, 9, 0:NST], AX_X, ALU.add))
            tt(S(2), S(0), S(0), ALU.mult)
            tt(S(3), S(1), S(1), ALU.mult)
            tt(S(2), S(2), S(3), ALU.add)
            step(V.reciprocal(S(3), S(2)))
            tt(S(4), S(0), S(3), ALU.mult)
            step(V.scalar_tensor_tensor(out=S(5), in0=S(1), scalar=-1.0, in1=S(3), op0=ALU.mult, op1=ALU.mult))
            step(V.tensor_scalar(Z(11), Z(6), S(5), None, ALU.mult))
            step(V.scalar_tensor_tensor(out=Z(9), in0=Z(5), scalar=S(4), in1=Z(11), op0=ALU.mult, op1=ALU.subtract))
            step(V.tensor_scalar(Z(11), Z(6), S(4), None, ALU.mult))
            step(V.scalar_tensor_tensor(out=Z(10), in0=Z(5), scalar=S(5), in1=Z(11), op0=ALU.mult, op1=ALU.add))
            for o, re, im, sign in ((12, Z(9), Z(10), ALU.add), (13, Z(7), Z(8), ALU.subtract), (14, pr, pi, ALU.add)):
                tt(Z(15), cview(m, "mask_a", 2), re, ALU.mult)
                tt(Z(16), cview(m, "mask_b", 2), im, ALU.mult)
                if o < 14:
                    tt(Z(o), Z(15), Z(16), sign)
            step(V.tensor_tensor(Z(14), Z(15), Z(16), ALU.add), rank2_ready, 1)
            dve.wait_ge(ssm_mm, 1)
            step(V.tensor_copy(zc[:, 2:6], ps[0][:, 8:12]))
            tt(zc[:, 1:2], zc[:, 1:2], zc[:, 4:5], ALU.add)
            for n, (mat, re, im, off, sign) in enumerate((
                    (a1, 2, 3, 0, ALU.add), (a1t, 2, 3, 128, ALU.subtract),
                    (a0t, 1, 5, 256, ALU.subtract), (a0, 1, 5, 256, ALU.add))):
                step(V.tensor_scalar(tqe[:, :], cview(m, "jmat"), zc[:, im:im + 1], None, ALU.mult))
                step(V.scalar_tensor_tensor(out=mat[:, :], in0=ident, scalar=zc[:, re:re + 1], in1=tqe[:, :],
                                            op0=ALU.mult, op1=sign))
                if n < 3:
                    tt(mat[:, :], mat[:, :], ps[1][:, off:off + 128], ALU.subtract)
            step(V.tensor_tensor(a0[:, :], a0[:, :], ps[1][:, 256:384], ALU.subtract), a_ready, 1)
            dve.wait_ge(ab_mm, 1)
            step(V.tensor_copy(pw[:, 0, :], ps[2][:, 0:128]))
            step(V.tensor_copy(qw[:, 0, :], ps[2][:, 128:256]))
            step(V.tensor_scalar(bc[:, 1:2], bc[:, 1:2], cview(m, "csign"), None, ALU.mult))
            step(V.tensor_scalar(vm[:, 0:1], ps[2][:, 256:257], 2.0, None, ALU.mult), v0_ready, 1)
            for k, (n, c) in enumerate(doublings):
                dve.wait_ge(power_mm, k + 1)
                if k < len(doublings) - 1:
                    step(V.tensor_copy(pw[:, (k + 1) % 2, :], ps[k % 2][:, 128:256]))
                    step(V.tensor_copy(qw[:, (k + 1) % 2, :], ps[k % 2][:, 256:384]))
                step(V.tensor_copy(vm[:, n:n + c], ps[k % 2][:, 0:c]), power_ready, k + 1)
            dve.wait_ge(kern_mm, 1)
            step(V.tensor_copy(krow[:, :], ps[2][0:1, 0:SEQP]))
            step(V.tensor_tensor(krow[:, 0:1], krow[:, 0:1], dsc[:, :], ALU.add), kern_ready, 1)
            dve.wait_ge(toep_mm, 1)
            step(V.tensor_copy(m.toep[:, :, :].rearrange("p a n -> p (a n)"), ps[3][0:ROWS, 0:2 * SEQP]))
    nc.clear_and_free_semaphores(sems)
    nc.all_engine_barrier()


def patch_phase(nc, m, d, ctx):
    with ExitStack() as own:
        def sb(name, shape, dt=F32):
            return own.enter_context(nc.sbuf_tensor(name, shape, dt))

        def sem(name):
            return ctx.enter_context(nc.semaphore(name))

        NT = GB * NPATCH
        wtok = sb("wtok", [128, KCH, 128])
        pat = [sb(f"patches{n}", [128, KCH, NT // 2]) for n in range(2)]
        ps = [own.enter_context(nc.psum_tensor(f"tok_ps{n}", [128, NT // 2], F32)) for n in range(2)]
        wl = sem("wtok_loaded")
        loaded = [sem(f"patches_loaded{n}") for n in range(2)]
        mm = [sem(f"patches_mm{n}") for n in range(2)]
        out_ready = [sem(f"tokens_ready{n}") for n in range(2)]
        block = own.enter_context(nc.Block())

        @block.sync
        def _(sp):
            sp.dma_start(wtok[:, :, :], d["wtok"]).then_inc(wl, 16)
            for n in range(2):
                sp.sem_inc(loaded[n], 16)
                sp.sem_inc(mm[n], 1)
                sp.sem_inc(out_ready[n], 1)
            with sp.Fori(1, GROUPS + 1) as i:
                for n in range(2):
                    sp.wait_ge(mm[n], i)
                    sp.dma_start(pat[n][:, :, :], d["xpat"][2 * i + (n - 2)]).then_inc(loaded[n], 16)

        @block.tensor
        def _(pe):
            pe.wait_ge(wl, 16)
            with pe.Fori(1, GROUPS + 1) as i:
                for n in range(2):
                    pe.wait_ge(loaded[n], 16 * i + 16)
                    pe.wait_ge(out_ready[n], i)
                    for k in range(KCH):
                        last = nc.tensor.matmul(ps[n][:, :], lhsT=wtok[:, k, :], rhs=pat[n][:, k, :],
                                                start=(k == 0), stop=(k == KCH - 1))
                    last.then_inc(mm[n], 1)

        @block.vector
        def _(dve):
            pos = m.posT[:, None, 1:1 + NPATCH].broadcast_to([128, GB // 2, NPATCH])
            with dve.Fori(1, GROUPS + 1) as i:
                for n in range(2):
                    dve.wait_ge(mm[n], i + 1)
                    dst = m.tok[:, bass.ds(i * NT + (n * (NT // 2) - NT), NT // 2)].rearrange("p (b t) -> p b t", b=GB // 2)
                    nc.vector.scalar_tensor_tensor(
                        out=dst, in0=ps[n][:, :].rearrange("p (b t) -> p b t", b=GB // 2),
                        scalar=m.tokb[:, 0:1], in1=pos, op0=ALU.add, op1=ALU.mult).then_inc(out_ready[n], 1)


def token_phase(nc, m, d, ctx):
    with ExitStack() as own:
        def sb(name, shape, dt=F32):
            return own.enter_context(nc.sbuf_tensor(name, shape, dt))

        def sem(name):
            return ctx.enter_context(nc.semaphore(name))

        ident, ones = cview(m, "ident"), cview(m, "ones")
        HALF = SEQP
        at = own.enter_context(nc.psum_tensor("scores", [128, 4, 512], F32))
        xb = own.enter_context(nc.psum_tensor("heads_out", [128, 512], F32))
        pb = own.enter_context(nc.psum_tensor("work", [128, 3, 512], F32))

        ybuf = sb("ybuf", [VOCAB, 2, NTEXT], I32)
        oh = sb("onehot", [VOCAB, 2, NTEXT + 1])
        cv = sb("conv", [128, 2, NTEXT])
        hT = m.hT0
        h_sb = sb("h_sb", [ROWS, TILES, HID])
        st, mv = sb("stats", [ROWS, TILES, 6]), sb("meanvar", [ROWS, TILES, 2])
        vv, rs = sb("var_eps", [ROWS, TILES]), sb("rstd", [ROWS, TILES])
        st2, mv2 = sb("stats2", [ROWS, TILES, 6]), sb("meanvar2", [ROWS, TILES, 2])
        vv2, rs2 = sb("var_eps2", [ROWS, TILES]), sb("rstd2", [ROWS, TILES])
        nhalf = sb("nhalf", [ROWS, TILES])
        xh = sb("xh", [ROWS, TILES, HID]); xT = sb("xT", [128, COLS])
        sq = sb("squares", [128, 2, COLS])
        qk2 = [sb(f"qk{n}", [128, 4, COLS]) for n in range(2)]
        vx2 = [sb(f"v_ext{n}", [ROWS, TILES, HEADS, 32]) for n in range(2)]
        mx = sb("maxima", [ROWS, 2, 2, 2]); mp = sb("max_placed", [ROWS, 2, 2, 64])
        q2 = sb("q_shifted", [128, HALF]); pt = sb("probs", [ROWS, 4, 2 * HALF])
        osb2 = [sb(f"heads_sb{n}", [128, 2, COLS]) for n in range(2)]
        rsum = sb("recip_sums", [ROWS, TILES, HEADS]); on = sb("heads_norm", [ROWS, TILES, HEADS, HD])
        oT = sb("oT", [128, COLS]); h1 = sb("h1", [ROWS, TILES, HID])
        xf2 = [sb(f"xf{n}", [ROWS, TILES, HID]) for n in range(2)]; xfT = sb("xfT", [128, COLS])
        th = sb("tanh_g", [128, COLS]); hm = sb("hidden", [128, COLS])
        er = sb("router_exp", [ROWS, TILES, E1]); nu = sb("neg_inv_score", [ROWS, TILES, E1])
        tv, ti = sb("top_vals", [ROWS, TILES, 8]), sb("top_idx", [ROWS, TILES, 8], U32)
        sc, den = sb("top_scores", [ROWS, TILES, 2]), sb("score_sum", [ROWS, TILES])
        idf = sb("top_idx_f", [ROWS, 2, TILES])
        ohk = sb("chosen", [ROWS, 2, TILES, E1]); mk = sb("mask", [ROWS, TILES, E1], BF16)
        ap_, apb = sb("slot_of", [ROWS, TILES, E1]), sb("slot_in_cap", [ROWS, TILES, E1])
        slf = sb("slot_f", [ROWS, 2 * TILES]); sli = sb("slot_i", [ROWS, 2 * TILES], I32)

        y_loaded, oh_ready, emb_mm, cv_ready = sem("y_loaded"), sem("oh_ready"), sem("emb_mm"), sem("cv_ready")
        text_in, patches_in, h_mm, h_sb_ready = sem("text_in"), sem("patches_in"), sem("h_mm"), sem("h_sb_ready")
        var_ready, rs_ready, xh_ready, xT_mm = sem("var_ready"), sem("rs_ready"), sem("xh_ready"), sem("xT_mm")
        xT_ready, proj_mm, sq_ready, esum_mm = sem("xT_ready"), sem("proj_mm"), sem("sq_ready"), sem("esum_mm")
        qk_ready, v_mm, v_ready = sem("qk_ready"), sem("v_mm"), sem("v_ready")
        s_mm, m_ready, mT_mm, q2_ready = sem("s_mm"), sem("m_ready"), sem("mT_mm"), sem("q2_ready")
        st_mm, exp_ready, pv_mm, o_ready = sem("st_mm"), sem("exp_ready"), sem("pv_mm"), sem("o_ready")
        otm_mm, on_ready, oT_mm, oT_ready = sem("otm_mm"), sem("on_ready"), sem("oT_mm"), sem("oT_ready")
        ao_mm, h1_ready, var2_ready, rs2_ready = sem("ao_mm"), sem("h1_ready"), sem("var2_ready"), sem("rs2_ready")
        xf_ready, xfT_mm, xfT_ready, rt_mm = sem("xf_ready"), sem("xfT_mm"), sem("xfT_ready"), sem("rt_mm")
        gu_mm, er_ready, th_ready, hm_ready = sem("gu_mm"), sem("er_ready"), sem("th_ready"), sem("hm_ready")
        sh_mm, hres_ready, mk_ready, pos_mm = sem("sh_mm"), sem("hres_ready"), sem("mk_ready"), sem("pos_mm")
        slot_ready, scattered, rows_sent = sem("slot_ready"), sem("scattered"), sem("rows_sent")
        own_f, own_a, own_b, own_c = sem("dve_front"), sem("dve_att"), sem("dve_back"), sem("dve_routing")
        preset = sem("preset")
        block = own.enter_context(nc.Block())
        STEPS_F, STEPS_B, STEPS_C = 6, 6, 15

        def passes(eng, body):
            body(1, front=True, back=False, routing=False)
            body(2, front=True, back=True, routing=False)
            with eng.Fori(1, (PAIRS - 4) // 2 + 1) as i:
                for n in range(2):
                    body(2 * i + (1 + n), front=True, back=True, routing=True, parity=(1 + n) % 2)
            body(PAIRS - 1, front=True, back=True, routing=True)
            body(PAIRS, front=False, back=True, routing=True)

        @block.sync
        def _(sp):
            for s in (oh_ready, emb_mm, cv_ready, text_in, patches_in, h_mm, h_sb_ready, var_ready, rs_ready,
                      xh_ready, xT_mm, xT_ready, v_mm, v_ready, otm_mm, on_ready, oT_mm, oT_ready, ao_mm,
                      h1_ready, var2_ready, rs2_ready, xf_ready, xfT_mm, xfT_ready, rt_mm, gu_mm, er_ready,
                      th_ready, hm_ready, sh_mm, hres_ready, mk_ready, pos_mm, slot_ready):
                sp.sem_inc(s, 1)
            for s in (qk_ready, proj_mm, sq_ready, esum_mm, pv_mm, o_ready):
                sp.sem_inc(s, 4)
            for s in (s_mm, m_ready, mT_mm, q2_ready, st_mm, exp_ready, own_a):
                sp.sem_inc(s, 8)
            sp.sem_inc(rows_sent, 2)
            sp.sem_inc(y_loaded, 16)
            sp.sem_inc(own_f, STEPS_F)
            sp.sem_inc(own_b, STEPS_B)
            sp.sem_inc(own_c, STEPS_C)
            with sp.Fori(1, PAIRS + 1) as i:
                sp.wait_ge(oh_ready, i)
                src = d["ytxt"][bass.ds(i - 1, 1), :].broadcast_to([VOCAB, 2 * NTEXT])
                sp.dma_start(ybuf[:, :, :].rearrange("p b t -> p (b t)"), src).then_inc(y_loaded, 16)

        @block.gpsimd
        def _(pool):
            nc.gpsimd.memset(oh[:, :, :], 0.0).then_inc(preset, 1)
            for n in range(2):
                nc.gpsimd.memset(vx2[n][:, :, :, :], 0.0).then_inc(preset, 1)
            nc.gpsimd.memset(mp[:, :, :, :], 0.0).then_inc(preset, 1)
            nc.gpsimd.memset(nhalf[:, :], -0.5).then_inc(preset, 1)
            pool.wait_ge(preset, 5)
            for n in range(2):
                nc.gpsimd.memset(vx2[n][:, :, :, HD:HD + 1], 1.0).then_inc(preset, 1)
            pool.wait_ge(preset, 7)

            def patches(f):
                pool.wait_ge(h_mm, f)
                nc.gpsimd.tensor_copy(
                    hT[:, :, 1:1 + NPATCH],
                    m.tok[:, bass.ds(f * (2 * NPATCH) - 2 * NPATCH, 2 * NPATCH)].rearrange("p (b t) -> p b t", b=2)
                ).then_inc(patches_in, 1)

            def rstd(f):
                pool.wait_ge(var_ready, f + 1)
                nc.gpsimd.tensor_tensor(rs[:, :], vv[:, :], nhalf[:, :], ALU.pow).then_inc(rs_ready, 1)

            def rstd2(q):
                pool.wait_ge(var2_ready, q + 1)
                nc.gpsimd.tensor_tensor(rs2[:, :], vv2[:, :], nhalf[:, :], ALU.pow).then_inc(rs2_ready, 1)

            def send_rows(s, xf):
                pool.wait_ge(slot_ready, s + 1)
                pool.nop(nofuse=True)
                for n in range(2 * TILES):
                    nc.gpsimd.indirect_dma_start(
                        out=d["buf1"], out_offset=bass.IndirectOffsetOnAxis(ap=sli[:, n:n + 1], axis=0),
                        in_=xf[:, n % TILES, :], in_offset=None,
                        bounds_check=SLOTS1 - 1, oob_is_err=False).then_inc(scattered, 16)

            def rows_gone(s):
                pool.wait_ge(scattered, s * (16 * 2 * TILES))
                pool.sem_inc(rows_sent, 1)

            def body(r, front, back, routing, parity=None):
                p = r % 2 if parity is None else parity
                if front:
                    patches(r + 1)
                    rstd(r + 1)
                if routing:
                    send_rows(r - 2, xf2[p])
                if back:
                    rstd2(r - 1)
                if routing:
                    rows_gone(r - 2)

            patches(1)
            rstd(1)
            passes(pool, body)
            send_rows(PAIRS - 1, xf2[(PAIRS - 1) % 2])
            rstd2(PAIRS)
            rows_gone(PAIRS - 1)
            send_rows(PAIRS, xf2[PAIRS % 2])
            rows_gone(PAIRS)

        @block.tensor
        def _(pe):
            T = nc.tensor
            pe.wait_ge(preset, 7)

            def embed(f):
                pe.wait_ge(oh_ready, f + 1)
                T.matmul(pb[:, 2, 0:2 * (NTEXT + 1)], lhsT=m.embt[:, :],
                         rhs=oh[:, :, :].rearrange("p b t -> p (b t)"), start=True, stop=True).then_inc(emb_mm, 1)

            def tokens(f):
                pe.wait_ge(patches_in, f + 1)
                pe.wait_ge(text_in, f + 1)
                for j in range(TILES):
                    last = T.transpose(pb[0:ROWS, 2, HID * j:HID * j + HID],
                                       hT[:, j // 2, ROWS * (j % 2):ROWS * (j % 2) + ROWS], ident)
                last.then_inc(h_mm, 1)

            def normed(f):
                pe.wait_ge(xh_ready, f + 1)
                for j in range(TILES):
                    last = T.transpose(pb[:, 2, ROWS * j:ROWS * j + ROWS], xh[:, j, :], ident[0:ROWS, 0:ROWS])
                last.then_inc(xT_mm, 1)

            def project(f, n):
                pe.wait_ge(xT_ready, f + 1)
                pe.wait_ge(qk_ready, 4 * f + n)
                w = (m.wq if n < 2 else m.wk)[:, n % 2, :]
                T.matmul(pb[:, 2, 0:COLS], lhsT=w, rhs=xT[:, :], start=True, stop=True).then_inc(proj_mm, 1)

            def add_squares(f, n):
                pe.wait_ge(sq_ready, 4 * f + (n + 1))
                es = (m.esq if n < 2 else m.esk)[:, n % 2, :]
                T.matmul(pb[:, 2, 0:COLS], lhsT=es, rhs=sq[:, n % 2, :],
                         start=False, stop=True, skip_group_check=True).then_inc(esum_mm, 1)

            def values(f):
                for j in range(TILES):
                    last = T.matmul(pb[0:ROWS, 0, HID * j:HID * j + HID], lhsT=xT[:, ROWS * j:ROWS * j + ROWS],
                                    rhs=m.wv[:, :], start=True, stop=True)
                last.then_inc(v_mm, 1)

            def scores(r, u, e, qk):
                b, g = u // 2, u % 2
                for hh in (2 * e, 2 * e + 1):
                    k = slice(32 * hh, 32 * hh + 32)
                    for qt in range(2):
                        c = HALF * b + ROWS * qt
                        last = T.matmul(at[0:ROWS, hh, HALF * qt:HALF * qt + SEQ], lhsT=qk[k, g, c:c + ROWS],
                                        rhs=qk[k, 2 + g, HALF * b:HALF * b + SEQ], start=True, stop=True)
                last.then_inc(s_mm, 1)

            def maxima(r, u, e):
                if e == 0:
                    pe.wait_ge(o_ready, 4 * r + u)
                pe.wait_ge(m_ready, 8 * r + (2 * u + e + 1))
                for qt in range(2):
                    last = T.matmul(xb[64 * e:64 * e + 64, 256 + ROWS * qt:256 + ROWS * qt + ROWS], lhsT=mp[:, e, qt, :],
                                    rhs=ident[0:ROWS, 0:ROWS], start=True, stop=True)
                last.then_inc(mT_mm, 1)

            def shifted_scores(r, u, e, qk):
                b, g = u // 2, u % 2
                pe.wait_ge(q2_ready, 8 * r + (2 * u + e + 1))
                for hh in (2 * e, 2 * e + 1):
                    k = slice(32 * hh, 32 * hh + 32)
                    for kt in range(2):
                        c = HALF * b + ROWS * kt
                        last = T.matmul(at[0:ROWS, hh, HALF * kt:HALF * kt + HALF],
                                        lhsT=qk[k, 2 + g, c:c + ROWS], rhs=q2[k, :], start=True, stop=True)
                last.then_inc(st_mm, 1)

            def weighted_values(r, u, e, vx):
                b, g = u // 2, u % 2
                pe.wait_ge(exp_ready, 8 * r + (2 * u + e + 1))
                for hh in (2 * e, 2 * e + 1):
                    for kt in range(2):
                        n = ROWS - kt
                        last = T.matmul(xb[32 * hh:32 * hh + 32, 0:HALF],
                                        lhsT=vx[0:n, 2 * b + kt, 4 * g + hh, :],
                                        rhs=pt[0:n, hh, HALF * kt:HALF * kt + HALF],
                                        start=(kt == 0), stop=(kt == 1))
                if e == 1:
                    last.then_inc(pv_mm, 1)

            def heads_back(q, osb):
                pe.wait_ge(o_ready, 4 * q + 4)
                for j in range(TILES):
                    for g in range(2):
                        c = 256 * j + 128 * g
                        last = T.transpose(pb[0:ROWS, c // 512, c % 512:c % 512 + 128],
                                           osb[:, g, ROWS * j:ROWS * j + ROWS], ident)
                last.then_inc(otm_mm, 1)

            def heads_normed(q):
                pe.wait_ge(on_ready, q + 1)
                for j in range(TILES):
                    last = T.transpose(pb[:, 0, ROWS * j:ROWS * j + ROWS],
                                       on[:, j, :, :].rearrange("p h d -> p (h d)"), ident[0:ROWS, 0:ROWS])
                last.then_inc(oT_mm, 1)

            def attention_out(q):
                pe.wait_ge(oT_ready, q + 1)
                for j in range(TILES):
                    T.matmul(pb[0:ROWS, 1, HID * j:HID * j + HID], lhsT=oT[:, ROWS * j:ROWS * j + ROWS],
                             rhs=m.wo[:, :], start=True, stop=False)
                    last = T.matmul(pb[0:ROWS, 1, HID * j:HID * j + HID], lhsT=ones[0:1, 0:ROWS],
                                    rhs=m.bo_row[:, :], start=False, stop=True)
                last.then_inc(ao_mm, 1)

            def normed2(s, xf):
                pe.wait_ge(xf_ready, s + 1)
                for j in range(TILES):
                    last = T.transpose(pb[:, 0, ROWS * j:ROWS * j + ROWS], xf[:, j, :], ident[0:ROWS, 0:ROWS])
                last.then_inc(xfT_mm, 1)

            def router(s):
                pe.wait_ge(xfT_ready, s + 1)
                for j in range(TILES):
                    last = T.matmul(pb[0:ROWS, 1, E1 * j:E1 * j + E1], lhsT=xfT[:, ROWS * j:ROWS * j + ROWS],
                                    rhs=m.gatew[:, :], start=True, stop=True)
                last.then_inc(rt_mm, 1)

            def gate_up(s):
                pe.wait_ge(er_ready, s + 1)
                for n in range(2):
                    last = T.matmul(pb[:, n, 0:COLS], lhsT=m.sw13[:, 128 * n:128 * n + 128], rhs=xfT[:, :],
                                    start=True, stop=True)
                last.then_inc(gu_mm, 1)

            def shared_out(s):
                pe.wait_ge(hm_ready, s + 1)
                for j in range(TILES):
                    last = T.matmul(pb[0:ROWS, 0, HID * j:HID * j + HID], lhsT=hm[:, ROWS * j:ROWS * j + ROWS],
                                    rhs=m.sw2[:, :], start=True, stop=True)
                last.then_inc(sh_mm, 1)

            def positions(s):
                pe.wait_ge(mk_ready, s + 1)
                out = pb[0:ROWS, 1, 0:TILES * E1].rearrange("p (j e) -> p j e", j=TILES)
                T.matmul(out, lhsT=m.tri_bf[:, :], rhs=mk[:, :, :], start=True, stop=False)
                for j in range(TILES - 1):
                    T.matmul(out[:, j + 1:, :], lhsT=m.ones_bf[:, :],
                             rhs=mk[:, j:j + 1, :].broadcast_to([ROWS, TILES - 1 - j, E1]), start=False, stop=False)
                T.matmul(out, lhsT=ones[0:1, 0:ROWS],
                         rhs=m.carry[:, None, :].broadcast_to([1, TILES, E1]), start=False, stop=True)
                tot = pb[0:1, 1, TILES * E1:TILES * E1 + E1]
                for j in range(TILES):
                    T.matmul(tot, lhsT=m.ones_bf[:, 0:1], rhs=mk[:, j, :], start=(j == 0), stop=False)
                T.matmul(tot, lhsT=ones[0:1, 0:1], rhs=m.carry[:, :], start=False, stop=True).then_inc(pos_mm, 1)

            def body(r, front, back, routing, parity=None):
                p = r % 2 if parity is None else parity
                f, q, s = r + 1, r - 1, r - 2
                qk, vx = qk2[p], vx2[p]
                pe.wait_ge(qk_ready, 4 * r + 4)
                pe.wait_ge(v_ready, r + 1)
                for u in range(4):
                    scores(r, u, 0, qk)
                    if u > 0:
                        weighted_values(r, u - 1, 1, vx)
                    if u == 0 and routing:
                        normed2(s, xf2[p])
                    if u == 2 and front:
                        project(f, 0)
                    if u == 3 and front:
                        add_squares(f, 1)
                    if u == 3 and back:
                        heads_normed(q)
                    scores(r, u, 1, qk)
                    if u == 0 and routing:
                        router(s)
                    if u == 0 and front:
                        embed(f)
                    if u == 1 and routing:
                        shared_out(s)
                    if u == 2 and front:
                        add_squares(f, 0)
                    if u == 3 and front:
                        project(f, 2)
                    maxima(r, u, 0)
                    shifted_scores(r, u, 0, qk)
                    if u == 0 and routing:
                        gate_up(s)
                    if u == 1 and routing:
                        positions(s)
                    if u == 3 and front:
                        add_squares(f, 2)
                    maxima(r, u, 1)
                    shifted_scores(r, u, 1, qk)
                    if u == 0 and front:
                        tokens(f)
                    if u == 1 and front:
                        normed(f)
                    if u == 2 and back:
                        if routing:
                            pe.wait_ge(hres_ready, s + 1)
                            pe.wait_ge(slot_ready, s + 1)
                        heads_back(q, osb2[1 - p])
                    if u == 2 and front:
                        project(f, 1)
                    if u == 3 and back:
                        attention_out(q)
                    if u == 3 and front:
                        project(f, 3)
                    weighted_values(r, u, 0, vx)
                if front:
                    values(f)
                    add_squares(f, 3)
                weighted_values(r, 3, 1, vx)

            embed(1)
            tokens(1)
            normed(1)
            for n in range(4):
                project(1, n)
                add_squares(1, n)
            values(1)
            passes(pe, body)
            last = PAIRS
            normed2(last - 1, xf2[(last - 1) % 2])
            router(last - 1)
            gate_up(last - 1)
            shared_out(last - 1)
            positions(last - 1)
            pe.wait_ge(hres_ready, last)
            pe.wait_ge(slot_ready, last)
            heads_back(last, osb2[last % 2])
            heads_normed(last)
            attention_out(last)
            normed2(last, xf2[last % 2])
            router(last)
            gate_up(last)
            shared_out(last)
            positions(last)

        @block.scalar
        def _(act):
            A = nc.scalar
            act.wait_ge(preset, 7)

            def conv(f):
                act.wait_ge(emb_mm, f + 1)
                emb = pb[:, 2, 0:2 * (NTEXT + 1)].rearrange("p (b t) -> p b t", b=2)
                A.activation(cv[:, :, :], emb[:, :, 0:NTEXT], ACT.Copy, scale=m.convq[:, 0:1]).then_inc(cv_ready, 1)

            def tokens(f):
                act.wait_ge(h_mm, f + 1)
                A.activation(m.hres[:, bass.ds(f - 1, 1), :, :].rearrange("p a j c -> p (a j c)"), pb[0:ROWS, 2, :], ACT.Copy)
                A.activation(h_sb[:, :, :].rearrange("p j c -> p (j c)"), pb[0:ROWS, 2, :], ACT.Copy).then_inc(h_sb_ready, 1)

            def normed(f):
                act.wait_ge(xT_mm, f + 1)
                A.activation(xT[:, :], pb[:, 2, 0:COLS], ACT.Copy).then_inc(xT_ready, 1)

            def squares(f, n):
                raw = (m.rawq if n < 2 else m.rawk)[:, n % 2:n % 2 + 1]
                act.wait_ge(proj_mm, 4 * f + (n + 1))
                A.activation(sq[:, n % 2, :], pb[:, 2, 0:COLS], ACT.Square, bias=raw).then_inc(sq_ready, 1)

            def projected(f, n, qk):
                act.wait_ge(esum_mm, 4 * f + (n + 1))
                if n < 2:
                    x = A.activation(qk[:, n, :], pb[:, 2, 0:COLS], ACT.Identity, bias=m.biasq[:, n:n + 1],
                                     scale=m.scaleq[:, n:n + 1])
                else:
                    x = A.activation(qk[:, n, :], pb[:, 2, 0:COLS], ACT.Identity, bias=m.biask[:, n - 2:n - 1])
                x.then_inc(qk_ready, 1)

            def values(f, vx):
                act.wait_ge(v_mm, f + 1)
                A.activation(vx[:, :, :, 0:HD].rearrange("p j h d -> p (j h) d"),
                             pb[0:ROWS, 0, :].rearrange("p (n d) -> p n d", d=HD), ACT.Copy).then_inc(v_ready, 1)

            def probs(r, u, e):
                act.wait_ge(st_mm, 8 * r + (2 * u + e + 1))
                h = slice(2 * e, 2 * e + 2)
                A.activation(pt[:, h, :], at[0:ROWS, h, 0:2 * HALF], ACT.Exp).then_inc(exp_ready, 1)

            def heads(r, u, osb):
                b, g = u // 2, u % 2
                act.wait_ge(pv_mm, 4 * r + (u + 1))
                A.activation(osb[:, g, HALF * b:HALF * b + HALF], xb[:, 0:HALF], ACT.Copy).then_inc(o_ready, 1)

            def heads_normed(q):
                act.wait_ge(oT_mm, q + 1)
                A.activation(oT[:, :], pb[:, 0, 0:COLS], ACT.Copy).then_inc(oT_ready, 1)

            def normed2(s):
                act.wait_ge(xfT_mm, s + 1)
                A.activation(xfT[:, :], pb[:, 0, 0:COLS], ACT.Copy).then_inc(xfT_ready, 1)

            def router(s):
                act.wait_ge(rt_mm, s + 1)
                A.activation(er[:, :, :].rearrange("p j e -> p (j e)"), pb[0:ROWS, 1, 0:TILES * E1], ACT.Exp,
                             scale=-1.0).then_inc(er_ready, 1)

            def gate(s):
                act.wait_ge(gu_mm, s + 1)
                A.activation(th[:, :], pb[:, 0, 0:COLS], ACT.Tanh, scale=0.5).then_inc(th_ready, 1)

            def body(r, front, back, routing, parity=None):
                p = r % 2 if parity is None else parity
                f, q, s = r + 1, r - 1, r - 2
                for u in range(4):
                    if u > 0:
                        heads(r, u - 1, osb2[p])
                    if u == 0 and routing:
                        normed2(s)
                        router(s)
                    if u == 0 and front:
                        conv(f)
                    if u == 2 and front:
                        squares(f, 0)
                    if u == 3 and front:
                        projected(f, 1, qk2[1 - p])
                    if u == 3 and back:
                        heads_normed(q)
                    if u == 3 and front:
                        squares(f, 2)
                    probs(r, u, 0)
                    if u == 0 and routing:
                        gate(s)
                    if u == 2 and front:
                        projected(f, 0, qk2[1 - p])
                    if u == 3 and front:
                        projected(f, 2, qk2[1 - p])
                    probs(r, u, 1)
                    if u == 0 and front:
                        tokens(f)
                    if u == 1 and front:
                        normed(f)
                    if u == 2 and front:
                        squares(f, 1)
                    if u == 3 and front:
                        squares(f, 3)
                if front:
                    values(f, vx2[1 - p])
                    projected(f, 3, qk2[1 - p])
                heads(r, 3, osb2[p])

            conv(1)
            tokens(1)
            normed(1)
            for n in range(4):
                squares(1, n)
                projected(1, n, qk2[1])
            values(1, vx2[1])
            passes(act, body)
            normed2(PAIRS - 1)
            router(PAIRS - 1)
            gate(PAIRS - 1)
            heads_normed(PAIRS)
            normed2(PAIRS)
            router(PAIRS)
            gate(PAIRS)

        @block.vector
        def _(dve):
            V = nc.vector
            flat = lambda t: t[:, :, :].rearrange("p j c -> p (j c)")

            def variance(step, x, st, mv):
                for j in range(TILES):
                    ins = V.bn_stats(st[:, j, :], x[:, j, :])
                step(ins)
                V.tensor_tensor(mv[:, :, 0], st[:, :, 1], st[:, :, 4], ALU.add)
                step(V.tensor_tensor(mv[:, :, 1], st[:, :, 1], st[:, :, 4], ALU.subtract))
                V.tensor_scalar(mv[:, :, 0], mv[:, :, 0], 0.5, None, ALU.mult)
                step(V.scalar_tensor_tensor(out=mv[:, :, 1], in0=mv[:, :, 1], scalar=HID / 4.0, in1=mv[:, :, 1],
                                            op0=ALU.mult, op1=ALU.mult))
                step(V.tensor_tensor(mv[:, :, 1], mv[:, :, 1], st[:, :, 2], ALU.add))
                step(V.tensor_tensor(mv[:, :, 1], mv[:, :, 1], st[:, :, 5], ALU.add))

            def one_hot(step, f):
                dve.wait_ge(y_loaded, 16 * f + 16)
                dve.wait_ge(emb_mm, f)
                step(V.tensor_scalar(oh[:, :, 1:], ybuf[:, :, :], float(VOCAB - 1), cview(m, "vocab", VOCAB),
                                     ALU.min, ALU.is_equal), oh_ready, f + 1)

            def text(step, f):
                dve.wait_ge(cv_ready, f + 1)
                emb = pb[:, 2, 0:2 * (NTEXT + 1)].rearrange("p (b t) -> p b t", b=2)
                step(V.scalar_tensor_tensor(out=cv[:, :, :], in0=emb[:, :, 1:], scalar=m.convq[:, 1:2],
                                            in1=cv[:, :, :], op0=ALU.mult, op1=ALU.add))
                dve.wait_ge(h_mm, f)
                step(V.tensor_scalar(hT[:, :, 1 + NPATCH:SEQ], cv[:, :, :], 0.0, None, ALU.max), text_in, f + 1)

            def statistics(step, f):
                dve.wait_ge(h_sb_ready, f + 1)
                variance(step, h_sb, st, mv)
                step(V.tensor_scalar(vv[:, :], mv[:, :, 1], (1.0 + EPS) / HID, EPS * EPS, ALU.mult, ALU.add),
                     var_ready, f + 1)

            def normed(step, f):
                dve.wait_ge(rs_ready, f + 1)
                for j in range(TILES):
                    x = V.tensor_scalar(xh[:, j, :], h_sb[:, j, :], mv[:, j, 0:1],
                                        rs[:, j:j + 1], ALU.subtract, ALU.mult)
                step(x, xh_ready, f + 1)

            def maxima(r, u, e):
                step = Steps(dve, own_a, 8 * r + (2 * u + e))
                dve.wait_ge(s_mm, 8 * r + (2 * u + e + 1))
                sview = at[0:ROWS, 2 * e:2 * e + 2, 0:2 * HALF].rearrange("p h (t k) -> p h t k", t=2)[:, :, :, 0:SEQ]
                step(V.tensor_reduce(mx[:, e, :, :], sview, AX_X, ALU.max))
                step(V.tensor_scalar(mp[:, e, :, :].rearrange("p t (h r) -> p h t r", r=32)[:, :, :, 0],
                                     mx[:, e, :, :], -1.0, None, ALU.mult), m_ready, 8 * r + (2 * u + e + 1))

            def shifted(r, u, e, qk):
                b, g = u // 2, u % 2
                k = slice(64 * e, 64 * e + 64)
                dve.wait_ge(mT_mm, 8 * r + (2 * u + e + 1))
                V.tensor_tensor(q2[k, :], qk[k, g, HALF * b:HALF * b + HALF], xb[k, 256:256 + HALF],
                                ALU.add).then_inc(q2_ready, 1)

            def heads_normed(step, q):
                dve.wait_ge(otm_mm, q + 1)
                heads = pb[0:ROWS, 0:2, :].rearrange("p a c -> p (a c)").rearrange("p (n r) -> p n r", r=32)
                step(V.reciprocal(rsum[:, :, :].rearrange("p j h -> p (j h)"), heads[:, :, HD]))
                step(V.tensor_tensor(on[:, :, :, :].rearrange("p j h d -> p (j h) d"), heads[:, :, 0:HD],
                                     rsum[:, :, :].rearrange("p j h -> p (j h)")[:, :, None].broadcast_to(
                                         [ROWS, TILES * HEADS, HD]), ALU.mult), on_ready, q + 1)

            def residual(step, q):
                dve.wait_ge(ao_mm, q + 1)
                step(V.tensor_tensor(flat(h1), m.hres[:, bass.ds(q - 1, 1), :, :].rearrange("p a j c -> p (a j c)"),
                                     pb[0:ROWS, 1, :], ALU.add), h1_ready, q + 1)
                variance(step, h1, st2, mv2)
                step(V.tensor_scalar(vv2[:, :], mv2[:, :, 1], 1.0 / HID, EPS, ALU.mult, ALU.add), var2_ready, q + 1)

            def normed2(step, q, xf):
                dve.wait_ge(rs2_ready, q + 1)
                dve.wait_ge(rows_sent, q)
                for j in range(TILES):
                    x = V.tensor_scalar(xf[:, j, :], h1[:, j, :], mv2[:, j, 0:1], rs2[:, j:j + 1],
                                        ALU.subtract, ALU.mult)
                step(x, xf_ready, q + 1)

            def hidden(step, s):
                dve.wait_ge(th_ready, s + 1)
                step(V.scalar_tensor_tensor(out=th[:, :], in0=th[:, :], scalar=1.0, in1=pb[:, 0, 0:COLS],
                                            op0=ALU.add, op1=ALU.mult))
                step(V.tensor_tensor(hm[:, :], th[:, :], pb[:, 1, 0:COLS], ALU.mult), hm_ready, s + 1)

            def best(step, s):
                dve.wait_ge(er_ready, s + 1)
                step(V.tensor_scalar(nu[:, :, :], er[:, :, :], -1.0, -1.0, ALU.mult, ALU.add))
                dve.nop(nofuse=True)
                for j in range(TILES):
                    x = V.max(tv[:, j, :], nu[:, j, :])
                step(x)
                dve.nop(nofuse=True)
                for j in range(TILES):
                    x = V.max_index(ti[:, j, :], tv[:, j, :], nu[:, j, :])
                step(x)
                step(V.tensor_tensor(idf[:, :, :].rearrange("p k j -> p j k"), ti[:, :, 0:2],
                                     cview(m, "padbig", ROWS).rearrange("p (k j) -> p j k", k=2), ALU.add))
                step(V.tensor_tensor(
                    ohk[:, :, :, :].rearrange("p k j e -> p (k j) e"),
                    cview(m, "iota64", ROWS)[:, None, :].broadcast_to([ROWS, 2 * TILES, E1]),
                    idf[:, :, :].rearrange("p k j -> p (k j)")[:, :, None].broadcast_to([ROWS, 2 * TILES, E1]),
                    ALU.is_equal))
                step(V.tensor_tensor(mk[:, :, :], ohk[:, 0, :, :], ohk[:, 1, :, :], ALU.add), mk_ready, s + 1)

            def weights(step, s):
                step(V.reciprocal(sc[:, :, :], tv[:, :, 0:2]))
                step(V.tensor_tensor(den[:, :], sc[:, :, 0], sc[:, :, 1], ALU.add))
                step(V.tensor_scalar(den[:, :], den[:, :], -1e-20, None, ALU.add))
                step(V.reciprocal(den[:, :], den[:, :]))
                w = m.wts1[:, bass.ds(s - 1, 1), :].rearrange("p a (k j) -> p (a k) j", k=2)
                step(V.scalar_tensor_tensor(out=w, in0=sc[:, :, :].rearrange("p j k -> p k j"), scalar=ROUTE_SCALE,
                                            in1=den[:, None, :].broadcast_to([ROWS, 2, TILES]),
                                            op0=ALU.mult, op1=ALU.mult))

            def shared_out(step, s):
                dve.wait_ge(sh_mm, s + 1)
                step(V.tensor_tensor(m.hres[:, bass.ds(s - 1, 1), :, :].rearrange("p a j c -> p (a j c)"), flat(h1),
                                     pb[0:ROWS, 0, :], ALU.add), hres_ready, s + 1)

            def slots(step, s):
                dve.wait_ge(pos_mm, s + 1)
                pos = pb[0:ROWS, 1, 0:TILES * E1].rearrange("p (j e) -> p j e", j=TILES)
                V.tensor_copy(m.carry[:, :], pb[0:1, 1, TILES * E1:TILES * E1 + E1])
                step(V.tensor_tensor(ap_[:, :, :], pos,
                                     cview(m, "eoff1", ROWS)[:, None, :].broadcast_to([ROWS, TILES, E1]), ALU.add))
                step(V.scalar_tensor_tensor(out=apb[:, :, :], in0=pos, scalar=float(CAP), in1=ap_[:, :, :],
                                            op0=ALU.is_lt, op1=ALU.mult))
                step(V.tensor_tensor(ohk[:, :, :, :], ohk[:, :, :, :],
                                     apb[:, None, :, :].broadcast_to([ROWS, 2, TILES, E1]), ALU.mult))
                step(V.tensor_reduce(slf[:, :], ohk[:, :, :, :].rearrange("p k j e -> p (k j) e"), AX_X, ALU.add))
                dve.wait_ge(rows_sent, s + 1)
                V.tensor_scalar(m.slots1[:, bass.ds(s - 1, 1), :].rearrange("p a n -> p (a n)"), slf[:, :],
                                float(SLOTS1), None, ALU.add)
                step(V.tensor_scalar(sli[:, :], slf[:, :], float(SLOTS1), None, ALU.add), slot_ready, s + 1)

            def body(r, front, back, routing, parity=None):
                p = r % 2 if parity is None else parity
                f, q, s = r + 1, r - 1, r - 2
                front_step = Steps(dve, own_f, STEPS_F * f)
                back_step = Steps(dve, own_b, STEPS_B * q)
                routing_step = Steps(dve, own_c, STEPS_C * s)
                for u in range(4):
                    maxima(r, u, 0)
                    if u == 0 and front:
                        one_hot(front_step, f)
                    if u == 1 and front:
                        statistics(front_step, f)
                    if u == 2 and routing:
                        weights(routing_step, s)
                    shifted(r, u, 0, qk2[p])
                    maxima(r, u, 1)
                    if u == 0 and front:
                        text(front_step, f)
                    if u == 1 and routing:
                        shared_out(routing_step, s)
                    shifted(r, u, 1, qk2[p])
                    if u == 0 and routing:
                        hidden(routing_step, s)
                        best(routing_step, s)
                    if u == 1 and front:
                        normed(front_step, f)
                    if u == 1 and routing:
                        slots(routing_step, s)
                    if u == 2 and back:
                        heads_normed(back_step, q)
                    if u == 3 and back:
                        residual(back_step, q)
                if back:
                    normed2(back_step, q, xf2[1 - p])
                assert not front or front_step.n == STEPS_F, front_step.n
                assert not back or back_step.n == STEPS_B, back_step.n
                assert not routing or routing_step.n == STEPS_C, routing_step.n

            def routed(s):
                step = Steps(dve, own_c, STEPS_C * s)
                hidden(step, s)
                best(step, s)
                shared_out(step, s)
                slots(step, s)
                weights(step, s)

            dve.wait_ge(preset, 7)
            step = Steps(dve, own_f, STEPS_F)
            one_hot(step, 1)
            text(step, 1)
            statistics(step, 1)
            normed(step, 1)
            passes(dve, body)
            routed(PAIRS - 1)
            step = Steps(dve, own_b, STEPS_B * PAIRS)
            heads_normed(step, PAIRS)
            residual(step, PAIRS)
            normed2(step, PAIRS, xf2[PAIRS % 2])
            routed(PAIRS)




def expert_phase(nc, m, d, ctx):
    with ExitStack() as own:
        def sb(name, shape, dt=F32):
            return own.enter_context(nc.sbuf_tensor(name, shape, dt))

        def sem(name):
            return ctx.enter_context(nc.semaphore("x_" + name))

        WAYS = 4
        ways, two = range(WAYS), range(2)
        N = E1 // WAYS
        ident = cview(m, "ident")
        rows = [sb(f"x_rows{p}", [128, WAYS, 2, HID]) for p in two]
        w13 = [sb(f"x_w13_{p}", [128, WAYS, 2 * EH]) for p in two]
        w2 = [sb(f"x_w2_{p}", [EH, WAYS, HID]) for p in two]
        ys = [sb(f"x_out{p}", [128, WAYS, 2, HID]) for p in two]
        xT = [sb(f"x_rows_T{n}", [128, CAP]) for n in ways]
        th = [sb(f"x_tanh{n}", [EH, CAP]) for n in ways]
        hh = [sb(f"x_hidden{n}", [EH, CAP]) for n in ways]
        gps = [own.enter_context(nc.psum_tensor(f"x_gu_ps{n}", [128, 2, CAP], F32)) for n in ways]
        tps = [own.enter_context(nc.psum_tensor(f"x_ty_ps{n}", [128, 4, 128], F32)) for n in ways]
        loaded, stored = [sem(f"loaded{p}") for p in two], [sem(f"stored{p}") for p in two]
        t_mm, xT_ready, gu_mm, th_ready = sem("t_mm"), sem("xT_ready"), sem("gu_mm"), sem("th_ready")
        a_ready, h_ready, y_mm, y_ready = sem("a_ready"), sem("h_ready"), sem("y_mm"), sem("y_ready")
        block = own.enter_context(nc.Block())

        @block.sync
        def _(sp):
            for s in (t_mm, xT_ready, gu_mm, th_ready, a_ready, h_ready, y_mm, y_ready):
                sp.sem_inc(s, WAYS)
            for p in two:
                sp.sem_inc(stored[p], 16)

            def load(r, p):
                src = d["buf1"][bass.ds(r * (WAYS * CAP) - WAYS * CAP, WAYS * CAP), :]
                sp.dma_start(rows[p][:, :, :, :].rearrange("p n a c -> p (n a) c"),
                             src.rearrange("(b p) c -> p b c", p=128)).then_inc(loaded[p], 16)
                sp.dma_start(w13[p][:, :, :], d["w13"][bass.ds(r * WAYS - WAYS, WAYS), :, :].rearrange("n k c -> k n c")
                             ).then_inc(loaded[p], 16)
                sp.dma_start(w2[p][:, :, :], d["w2"][bass.ds(r * WAYS - WAYS, WAYS), :, :].rearrange("n k c -> k n c")
                             ).then_inc(loaded[p], 16)

            load(1, 0)
            load(2, 1)
            with sp.Fori(1, N // 2) as i:
                for p in two:
                    r = 2 * i + (p + 1)
                    sp.wait_ge(y_mm, WAYS * r - WAYS)
                    load(r, p)

        @block.tensor
        def _(pe):
            T = nc.tensor
            with pe.Fori(1, N // 2 + 1) as i:
                for p in two:
                    r = 2 * i + (p - 1)
                    pe.wait_ge(loaded[p], 48 * i)
                    for n in ways:
                        pe.wait_ge(y_ready, WAYS * r + (n + 1 - WAYS))
                        for a in range(2):
                            last = T.transpose(tps[n][:, a, :], rows[p][:, n, a, :], ident)
                        last.then_inc(t_mm, 1)
                    for n in ways:
                        pe.wait_ge(xT_ready, WAYS * r + (n + 1))
                        pe.wait_ge(h_ready, WAYS * r + (n + 1 - WAYS))
                        for k in range(2):
                            last = T.matmul(gps[n][0:EH, k, :], lhsT=w13[p][:, n, EH * k:EH * k + EH], rhs=xT[n][:, :],
                                            start=True, stop=True)
                        last.then_inc(gu_mm, 1)
                    for n in ways:
                        pe.wait_ge(h_ready, WAYS * r + (n + 1))
                        for a in range(2):
                            last = T.matmul(tps[n][:, 2 + a, :], lhsT=hh[n][:, 128 * a:128 * a + 128],
                                            rhs=w2[p][:, n, :], start=True, stop=True)
                        last.then_inc(y_mm, 1)

        @block.scalar
        def _(act):
            A = nc.scalar
            with act.Fori(1, N // 2 + 1) as i:
                for p in two:
                    r = 2 * i + (p - 1)
                    for n in ways:
                        act.wait_ge(t_mm, WAYS * r + (n + 1))
                        A.activation(xT[n][:, :], tps[n][:, 0:2, :].rearrange("p a c -> p (a c)"), ACT.Copy
                                     ).then_inc(xT_ready, 1)
                    for n in ways:
                        act.wait_ge(gu_mm, WAYS * r + (n + 1))
                        A.activation(th[n][:, :], gps[n][0:EH, 0, :], ACT.Tanh, scale=0.5).then_inc(th_ready, 1)
                    act.wait_ge(stored[p], 16 * i)
                    for n in ways:
                        act.wait_ge(y_mm, WAYS * r + (n + 1))
                        A.activation(ys[p][:, n, :, :], tps[n][:, 2:4, :], ACT.Copy).then_inc(y_ready, 1)
                    act.wait_ge(y_ready, WAYS * r + WAYS)
                    dst = d["y1"][bass.ds(r * (WAYS * CAP) - WAYS * CAP, WAYS * CAP), :].rearrange("(b p) c -> p b c", p=128)
                    act.dma_start(dst, ys[p][:, :, :, :].rearrange("p n a c -> p (n a) c")).then_inc(stored[p], 16)
            for p in two:
                act.wait_ge(stored[p], 16 * (N // 2 + 1))

        @block.vector
        def _(dve):
            V = nc.vector
            with dve.Fori(1, N + 1) as r:
                for n in ways:
                    dve.wait_ge(th_ready, WAYS * r + (n + 1))
                    V.scalar_tensor_tensor(out=th[n][:, :], in0=th[n][:, :], scalar=1.0, in1=gps[n][0:EH, 0, :],
                                           op0=ALU.add, op1=ALU.mult).then_inc(a_ready, 1)
                    dve.wait_ge(a_ready, WAYS * r + (n + 1))
                    V.scalar_tensor_tensor(out=hh[n][:, :], in0=th[n][:, :], scalar=0.5, in1=gps[n][0:EH, 1, :],
                                           op0=ALU.mult, op1=ALU.mult).then_inc(h_ready, 1)


def ssm_phase(nc, m, d, ctx):
    with ExitStack() as own:
        def sb(name, shape, dt=F32):
            return own.enter_context(nc.sbuf_tensor(name, shape, dt))

        def sem(name):
            return ctx.enter_context(nc.semaphore("s_" + name))

        ident, ones = cview(m, "ident"), cview(m, "ones")
        conv_ps, tr_ps, lg_ps, pos_ps = (own.enter_context(nc.psum_tensor("s_" + k, [128, 512], F32))
                                         for k in ("conv_ps", "tr_ps", "lg_ps", "pos_ps"))
        out_ps = own.enter_context(nc.psum_tensor("s_out_ps", [128, 2, 512], F32))
        NK = 2 * TILES
        sl = sb("s_slots", [ROWS, NK], I32); wt = sb("s_wts", [ROWS, NK])
        ga = sb("s_gathered", [ROWS, NK, HID]); h = sb("s_h", [ROWS, TILES, HID])
        st, mv = sb("s_stats", [ROWS, TILES, 6]), sb("s_meanvar", [ROWS, TILES, 2])
        st2, mv2 = sb("s_stats2", [ROWS, TILES, 6]), sb("s_meanvar2", [ROWS, TILES, 2])
        vv, rs, nhalf = sb("s_var", [ROWS, 2, TILES]), sb("s_rstd", [ROWS, 2, TILES]), sb("s_nhalf", [ROWS, 2, TILES])
        vv2, rs2 = sb("s_var2", [ROWS, TILES]), sb("s_rstd2", [ROWS, TILES])
        hsc, hbi = sb("s_skip_scale", [ROWS, TILES]), sb("s_skip_bias", [ROWS, TILES])
        hs, xn = sb("s_skip", [ROWS, TILES, HID]), sb("s_xn", [ROWS, TILES, HID])
        wcol, biasc = sb("s_norm_w", [128, 1]), sb("s_bias_conv", [128, SEQP])
        y, y2, gl = sb("s_y", [128, COLS]), sb("s_y2", [128, COLS]), sb("s_gelu", [128, COLS])
        tg, h4 = sb("s_gate", [ROWS, TILES, HID]), sb("s_h4", [ROWS, TILES, HID])
        xg2 = [sb(f"s_xg{n}", [ROWS, TILES, HID]) for n in range(2)]
        xgT = sb("s_xgT", [128, COLS])
        lg = sb("s_logits", [ROWS, TILES, E2]); tv = sb("s_top", [ROWS, TILES, 8])
        ti = sb("s_top_i", [ROWS, TILES, 8], U32); idf = sb("s_top_f", [ROWS, 2, TILES])
        df, ex, wk = sb("s_diff", [ROWS, TILES]), sb("s_exp", [ROWS, TILES]), sb("s_w", [ROWS, 2, TILES])
        ohk = sb("s_chosen", [ROWS, 2, TILES, E2]); mk = sb("s_mask", [ROWS, TILES, E2], BF16)
        so = sb("s_slot_of", [ROWS, TILES, E2]); slf = sb("s_slot_f", [ROWS, NK]); sli = sb("s_slot_i", [ROWS, NK], I32)

        preset, gathered, comb, idx_in = sem("preset"), sem("gathered"), sem("comb"), sem("idx_in")
        const_mm, const_ready = sem("const_mm"), sem("const_ready")
        var_ready, rs_ready, xn_ready = sem("var_ready"), sem("rs_ready"), sem("xn_ready")
        skip_ready, hs_ready, conv_mm, sq_ready = sem("skip_ready"), sem("hs_ready"), sem("conv_mm"), sem("sq_ready")
        y_ready, in_ready, tanh_ready, gl_ready = sem("y_ready"), sem("in_ready"), sem("tanh_ready"), sem("gl_ready")
        out_mm, gate_ready, h4_ready, kept = sem("out_mm"), sem("gate_ready"), sem("h4_ready"), sem("kept")
        var2_ready, rs2_ready = sem("var2_ready"), sem("rs2_ready")
        xg_ready, xgT_mm, xgT_ready, rt_mm = sem("xg_ready"), sem("xgT_mm"), sem("xgT_ready"), sem("rt_mm")
        lg_ready, df_ready, ex_ready, mk_ready = sem("lg_ready"), sem("df_ready"), sem("ex_ready"), sem("mk_ready")
        pos_mm, slot_ready, scattered, rows_sent = sem("pos_mm"), sem("slot_ready"), sem("scattered"), sem("rows_sent")
        own_x, own_y, own_r = sem("dve_next"), sem("dve_layer"), sem("dve_routing")
        wt_in = sem("wt_in")
        block = own.enter_context(nc.Block())
        STEPS_X, STEPS_Y, STEPS_R = 7, 7, 11
        C0, C1 = 0.7978845608028654, 0.7978845608028654 * 0.044715

        def passes(eng, body):
            body(1, following=True, last=False)
            with eng.Fori(1, (PAIRS - 2) // 2 + 1) as i:
                for n in range(2):
                    body(2 * i + n, following=True, last=True, parity=n)
            body(PAIRS, following=False, last=True)

        @block.sync
        def _(sp):
            for s in (comb, idx_in, var_ready, rs_ready, xn_ready, skip_ready, hs_ready, conv_mm, sq_ready, y_ready,
                      in_ready, tanh_ready, gl_ready, out_mm, gate_ready, h4_ready, kept, var2_ready, rs2_ready,
                      xg_ready, xgT_mm, xgT_ready, rt_mm, lg_ready, df_ready, ex_ready, mk_ready, pos_mm,
                      slot_ready, wt_in):
                sp.sem_inc(s, 1)
            sp.sem_inc(rows_sent, 2)
            sp.sem_inc(own_x, STEPS_X)
            sp.sem_inc(own_y, STEPS_Y)
            sp.sem_inc(own_r, STEPS_R)

        @block.gpsimd
        def _(pool):
            nc.gpsimd.memset(nhalf[:, :, :], -0.5).then_inc(preset, 1)
            pool.wait_ge(preset, 1)

            def gather(f):
                pool.wait_ge(comb, f)
                nc.gpsimd.tensor_copy(sl[:, :], m.slots1[:, bass.ds(f - 1, 1), :].rearrange("p a n -> p (a n)")).then_inc(idx_in, 1)
                pool.wait_ge(idx_in, f + 1)
                pool.nop(nofuse=True)
                for n in range(NK):
                    nc.gpsimd.indirect_dma_start(
                        out=ga[:, n, :], out_offset=None, in_=d["y1"],
                        in_offset=bass.IndirectOffsetOnAxis(ap=sl[:, n:n + 1], axis=0)).then_inc(gathered, 16)

            def rstd(f):
                pool.wait_ge(var_ready, f + 1)
                nc.gpsimd.tensor_tensor(rs[:, :, :], vv[:, :, :], nhalf[:, :, :], ALU.pow).then_inc(rs_ready, 1)

            def rstd2(r):
                pool.wait_ge(var2_ready, r + 1)
                nc.gpsimd.tensor_tensor(rs2[:, :], vv2[:, :], nhalf[:, 0, :], ALU.pow).then_inc(rs2_ready, 1)

            def send_rows(s, xg):
                pool.wait_ge(slot_ready, s + 1)
                pool.nop(nofuse=True)
                for n in range(NK):
                    nc.gpsimd.indirect_dma_start(
                        out=d["buf2"], out_offset=bass.IndirectOffsetOnAxis(ap=sli[:, n:n + 1], axis=0),
                        in_=xg[:, n % TILES, :], in_offset=None,
                        bounds_check=SLOTS2 - 1, oob_is_err=False).then_inc(scattered, 16)

            def rows_gone(s):
                pool.wait_ge(scattered, s * (16 * NK))
                pool.sem_inc(rows_sent, 1)

            gather(1)
            rstd(1)
            gather(2)
            rstd(2)
            gather(3)
            rstd2(1)
            rstd(3)
            gather(4)
            rstd2(2)
            send_rows(1, xg2[1])
            with pool.Fori(1, (PAIRS - 4) // 2 + 1) as i:
                for n in range(2):
                    r = 2 * i + (1 + n)
                    rstd(r + 1)
                    rows_gone(r - 2)
                    gather(r + 2)
                    rstd2(r)
                    send_rows(r - 1, xg2[n])
            rstd(PAIRS)
            rows_gone(PAIRS - 3)
            rstd2(PAIRS - 1)
            send_rows(PAIRS - 2, xg2[(PAIRS - 2) % 2])
            rows_gone(PAIRS - 2)
            rstd2(PAIRS)
            send_rows(PAIRS - 1, xg2[(PAIRS - 1) % 2])
            rows_gone(PAIRS - 1)
            send_rows(PAIRS, xg2[PAIRS % 2])
            rows_gone(PAIRS)

        @block.tensor
        def _(pe):
            T = nc.tensor

            def over_time(ps, c, first, second):
                T.matmul(ps[:, c:c + SEQP], lhsT=first, rhs=m.toep[:, 0, :], start=True, stop=False)
                return T.matmul(ps[:, c + ROWS:c + SEQP], lhsT=second,
                                rhs=m.toep[0:ROWS - 1, 1, ROWS:], start=False, stop=True)

            over_time(tr_ps, 0, m.normb[:, :], m.normb[0:ROWS - 1, :])
            T.matmul(tr_ps[:, 256:257], lhsT=m.normw[0:1, :], rhs=ones[0:1, 0:1], start=True, stop=True).then_inc(const_mm, 1)
            pe.wait_ge(const_ready, 1)

            def layer(r):
                pe.wait_ge(xn_ready, r + 1)
                pe.wait_ge(y_ready, r)
                for b in range(2):
                    last = over_time(conv_ps, SEQP * b, xn[:, 2 * b, :], xn[0:ROWS - 1, 2 * b + 1, :])
                last.then_inc(conv_mm, 1)

            def router(s, xg):
                pe.wait_ge(xg_ready, s + 1)
                pe.wait_ge(xgT_ready, s)
                for j in range(TILES):
                    last = T.transpose(tr_ps[:, ROWS * j:ROWS * j + ROWS], xg[:, j, :], ident[0:ROWS, 0:ROWS])
                last.then_inc(xgT_mm, 1)
                pe.wait_ge(xgT_ready, s + 1)
                pe.wait_ge(lg_ready, s)
                for j in range(TILES):
                    last = T.matmul(lg_ps[0:ROWS, E2 * j:E2 * j + E2], lhsT=xgT[:, ROWS * j:ROWS * j + ROWS],
                                    rhs=m.rtw[:, :], start=True, stop=True)
                last.then_inc(rt_mm, 1)

            def project(r):
                pe.wait_ge(gl_ready, r + 1)
                pe.wait_ge(h4_ready, r)
                for j in range(TILES):
                    o = out_ps[0:ROWS, j // 2, 256 * (j % 2):256 * (j % 2) + 256]
                    T.matmul(o, lhsT=gl[:, ROWS * j:ROWS * j + ROWS], rhs=m.outw[:, :], start=True, stop=False)
                    last = T.matmul(o, lhsT=ones[0:1, 0:ROWS], rhs=m.outb[:, :], start=False, stop=True)
                last.then_inc(out_mm, 1)

            def positions(s):
                pe.wait_ge(mk_ready, s + 1)
                pe.wait_ge(slot_ready, s)
                out = pos_ps[0:ROWS, 0:TILES * E2].rearrange("p (j e) -> p j e", j=TILES)
                T.matmul(out, lhsT=m.tri_bf[:, :], rhs=mk[:, :, :], start=True, stop=False)
                for j in range(TILES - 1):
                    T.matmul(out[:, j + 1:, :], lhsT=m.ones_bf[:, :],
                             rhs=mk[:, j:j + 1, :].broadcast_to([ROWS, TILES - 1 - j, E2]), start=False, stop=False)
                T.matmul(out, lhsT=ones[0:1, 0:ROWS],
                         rhs=m.carry2[:, None, :].broadcast_to([1, TILES, E2]), start=False, stop=True)
                tot = pos_ps[0:1, TILES * E2:TILES * E2 + E2]
                for j in range(TILES):
                    T.matmul(tot, lhsT=m.ones_bf[:, 0:1], rhs=mk[:, j, :], start=(j == 0), stop=False)
                T.matmul(tot, lhsT=ones[0:1, 0:1], rhs=m.carry2[:, :], start=False, stop=True).then_inc(pos_mm, 1)

            def body(r, following, last, parity=None):
                p = r % 2 if parity is None else parity
                layer(r)
                if last:
                    router(r - 1, xg2[1 - p])
                project(r)
                if last:
                    positions(r - 1)

            passes(pe, body)
            router(PAIRS, xg2[PAIRS % 2])
            positions(PAIRS)

        @block.scalar
        def _(act):
            A = nc.scalar

            def skip(f):
                act.wait_ge(skip_ready, f + 1)
                for j in range(TILES):
                    x = A.activation(hs[:, j, :], h[:, j, :], ACT.Identity, bias=hbi[:, j:j + 1], scale=hsc[:, j:j + 1])
                x.then_inc(hs_ready, 1)

            def transposed(s):
                act.wait_ge(xgT_mm, s + 1)
                A.activation(xgT[:, :], tr_ps[:, 0:COLS], ACT.Copy).then_inc(xgT_ready, 1)

            def logits(s):
                act.wait_ge(rt_mm, s + 1)
                A.activation(lg[:, :, :].rearrange("p j e -> p (j e)"), lg_ps[0:ROWS, 0:TILES * E2], ACT.Copy
                             ).then_inc(lg_ready, 1)

            def second_over_first(s):
                act.wait_ge(df_ready, s + 1)
                A.activation(ex[:, :], df[:, :], ACT.Exp).then_inc(ex_ready, 1)

            def body(r, following, last, parity=None):
                act.wait_ge(y_ready, r + 1)
                A.activation(y2[:, :], y[:, :], ACT.Square).then_inc(sq_ready, 1)
                if last:
                    transposed(r - 1)
                act.wait_ge(in_ready, r + 1)
                A.activation(y2[:, :], y2[:, :], ACT.Tanh).then_inc(tanh_ready, 1)
                if last:
                    logits(r - 1)
                act.wait_ge(out_mm, r + 1)
                z = out_ps[0:ROWS, :, :].rearrange("p a (j c) -> p (a j) c", j=2)
                A.activation(tg[:, :, :], z[:, :, HID:], ACT.Tanh, scale=0.5).then_inc(gate_ready, 1)
                act.wait_ge(h4_ready, r + 1)
                A.activation(m.hres[:, bass.ds(r - 1, 1), :, :].rearrange("p a j c -> p (a j c)"),
                             h4[:, :, :].rearrange("p j c -> p (j c)"), ACT.Copy).then_inc(kept, 1)
                if following:
                    skip(r + 1)
                if last:
                    second_over_first(r - 1)

            skip(1)
            passes(act, body)
            transposed(PAIRS)
            logits(PAIRS)
            second_over_first(PAIRS)

        @block.vector
        def _(dve):
            V = nc.vector
            flat = lambda t: t[:, :, :].rearrange("p j c -> p (j c)")

            def variance(step, x, st, mv):
                for j in range(TILES):
                    ins = V.bn_stats(st[:, j, :], x[:, j, :])
                step(ins)
                V.tensor_tensor(mv[:, :, 0], st[:, :, 1], st[:, :, 4], ALU.add)
                step(V.tensor_tensor(mv[:, :, 1], st[:, :, 1], st[:, :, 4], ALU.subtract))
                V.tensor_scalar(mv[:, :, 0], mv[:, :, 0], 0.5, None, ALU.mult)
                step(V.scalar_tensor_tensor(out=mv[:, :, 1], in0=mv[:, :, 1], scalar=HID / 4.0, in1=mv[:, :, 1],
                                            op0=ALU.mult, op1=ALU.mult))
                step(V.tensor_tensor(mv[:, :, 1], mv[:, :, 1], st[:, :, 2], ALU.add))
                step(V.tensor_tensor(mv[:, :, 1], mv[:, :, 1], st[:, :, 5], ALU.add))

            def combine(step, f, k):
                if k == 0:
                    step(V.tensor_scalar(wt[:, :], m.wts1[:, bass.ds(f - 1, 1), :].rearrange("p a n -> p (a n)"), 1.0,
                                         None, ALU.mult), wt_in, f + 1)
                    dve.wait_ge(gathered, f * (16 * NK))
                    dve.wait_ge(hs_ready, f)
                for j in range(TILES):
                    n = TILES * k + j
                    base = m.hres[:, bass.ds(f - 1, 1), j, :].rearrange("p a c -> p (a c)") if k == 0 else h[:, j, :]
                    x = V.scalar_tensor_tensor(out=h[:, j, :], in0=ga[:, n, :], scalar=wt[:, n:n + 1], in1=base,
                                               op0=ALU.mult, op1=ALU.add)
                if k == 0:
                    step(x)
                else:
                    step(x, comb, f + 1)

            def statistics(step, f):
                variance(step, h, st, mv)
                V.tensor_scalar(vv[:, 0, :], mv[:, :, 1], 1.0 / HID, EPS, ALU.mult, ALU.add)
                step(V.tensor_scalar(vv[:, 1, :], mv[:, :, 1], (1.0 + EPS) / HID, EPS * EPS, ALU.mult, ALU.add),
                     var_ready, f + 1)

            def normed(step, f):
                dve.wait_ge(rs_ready, f + 1)
                step(V.scalar_tensor_tensor(out=hbi[:, :], in0=mv[:, :, 0], scalar=-1.0, in1=rs[:, 0, :],
                                            op0=ALU.mult, op1=ALU.mult))
                step(V.tensor_scalar(hsc[:, :], rs[:, 0, :], 1.0, None, ALU.add), skip_ready, f + 1)
                dve.wait_ge(conv_mm, f)
                for j in range(TILES):
                    x = V.tensor_scalar(xn[:, j, :], h[:, j, :], mv[:, j, 0:1], rs[:, 1, j:j + 1],
                                        ALU.subtract, ALU.mult)
                step(x, xn_ready, f + 1)

            def layer_out(r):
                dve.wait_ge(conv_mm, r + 1)
                V.scalar_tensor_tensor(
                    out=y[:, :].rearrange("p (b t) -> p b t", b=2),
                    in0=conv_ps[:, 0:COLS].rearrange("p (b t) -> p b t", b=2), scalar=wcol[:, 0:1],
                    in1=biasc[:, None, :].broadcast_to([128, 2, SEQP]), op0=ALU.mult, op1=ALU.add).then_inc(y_ready, 1)

            def gelu_in(step, r):
                dve.wait_ge(sq_ready, r + 1)
                step(V.tensor_scalar(y2[:, :], y2[:, :], C1, C0, ALU.mult, ALU.add))
                step(V.tensor_tensor(y2[:, :], y2[:, :], y[:, :], ALU.mult), in_ready, r + 1)

            def gelu(step, r):
                dve.wait_ge(tanh_ready, r + 1)
                step(V.scalar_tensor_tensor(out=gl[:, :], in0=y2[:, :], scalar=1.0, in1=y[:, :],
                                            op0=ALU.add, op1=ALU.mult), gl_ready, r + 1)

            def gated(step, r):
                dve.wait_ge(gate_ready, r + 1)
                dve.wait_ge(hs_ready, r + 1)
                dve.wait_ge(kept, r)
                z = out_ps[0:ROWS, :, :].rearrange("p a (j c) -> p (a j) c", j=2)
                step(V.scalar_tensor_tensor(out=tg[:, :, :], in0=tg[:, :, :], scalar=1.0, in1=z[:, :, 0:HID],
                                            op0=ALU.add, op1=ALU.mult))
                step(V.scalar_tensor_tensor(out=flat(h4), in0=flat(tg), scalar=0.5, in1=flat(hs), op0=ALU.mult,
                                            op1=ALU.add), h4_ready, r + 1)
                variance(step, h4, st2, mv2)
                step(V.tensor_scalar(vv2[:, :], mv2[:, :, 1], 1.0 / HID, EPS, ALU.mult, ALU.add), var2_ready, r + 1)

            def normed2(step, r, xg):
                dve.wait_ge(rs2_ready, r + 1)
                dve.wait_ge(rows_sent, r)
                for j in range(TILES):
                    x = V.tensor_scalar(xg[:, j, :], h4[:, j, :], mv2[:, j, 0:1], rs2[:, j:j + 1],
                                        ALU.subtract, ALU.mult)
                step(x, xg_ready, r + 1)

            def best(step, s):
                dve.wait_ge(lg_ready, s + 1)
                dve.nop(nofuse=True)
                for j in range(TILES):
                    x = V.max(tv[:, j, :], lg[:, j, :])
                step(x)
                dve.nop(nofuse=True)
                for j in range(TILES):
                    x = V.max_index(ti[:, j, :], tv[:, j, :], lg[:, j, :])
                step(x)
                step(V.tensor_tensor(df[:, :], tv[:, :, 1], tv[:, :, 0], ALU.subtract), df_ready, s + 1)
                step(V.tensor_tensor(idf[:, :, :].rearrange("p k j -> p j k"), ti[:, :, 0:2],
                                     cview(m, "padbig", ROWS).rearrange("p (k j) -> p j k", k=2), ALU.add))
                step(V.tensor_tensor(
                    ohk[:, :, :, :].rearrange("p k j e -> p (k j) e"),
                    cview(m, "iota64", ROWS)[:, None, 0:E2].broadcast_to([ROWS, NK, E2]),
                    idf[:, :, :].rearrange("p k j -> p (k j)")[:, :, None].broadcast_to([ROWS, NK, E2]),
                    ALU.is_equal))
                step(V.tensor_tensor(mk[:, :, :], ohk[:, 0, :, :], ohk[:, 1, :, :], ALU.add), mk_ready, s + 1)

            def weights(step, s):
                dve.wait_ge(ex_ready, s + 1)
                step(V.tensor_scalar(wk[:, 1, :], ex[:, :], 1.0, None, ALU.add))
                step(V.reciprocal(wk[:, 0, :], wk[:, 1, :]))
                step(V.tensor_tensor(wk[:, 1, :], wk[:, 0, :], ex[:, :], ALU.mult))
                step(V.tensor_scalar(m.wts2[:, bass.ds(s - 1, 1), :].rearrange("p a n -> p (a n)"),
                                     wk[:, :, :].rearrange("p k j -> p (k j)"), 1.0, None, ALU.mult))

            def slots(step, s):
                dve.wait_ge(pos_mm, s + 1)
                pos = pos_ps[0:ROWS, 0:TILES * E2].rearrange("p (j e) -> p j e", j=TILES)
                V.tensor_copy(m.carry2[:, :], pos_ps[0:1, TILES * E2:TILES * E2 + E2])
                step(V.tensor_tensor(so[:, :, :], pos,
                                     cview(m, "eoff2", ROWS)[:, None, :].broadcast_to([ROWS, TILES, E2]), ALU.add))
                for k in range(2):
                    x = V.tensor_tensor(ohk[:, k, :, :], ohk[:, k, :, :], so[:, :, :], ALU.mult)
                step(x)
                step(V.tensor_reduce(slf[:, :], ohk[:, :, :, :].rearrange("p k j e -> p (k j) e"), AX_X, ALU.add))
                dve.wait_ge(rows_sent, s + 1)
                V.tensor_scalar(m.slots2[:, bass.ds(s - 1, 1), :].rearrange("p a n -> p (a n)"), slf[:, :],
                                float(SLOTS2), None, ALU.add)
                step(V.tensor_scalar(sli[:, :], slf[:, :], float(SLOTS2), None, ALU.add), slot_ready, s + 1)

            def body(r, following, last, parity=None):
                p = r % 2 if parity is None else parity
                f, s = r + 1, r - 1
                next_step = Steps(dve, own_x, STEPS_X * f)
                step = Steps(dve, own_y, STEPS_Y * r)
                routing_step = Steps(dve, own_r, STEPS_R * s)
                layer_out(r)
                if following:
                    combine(next_step, f, 0)
                gelu_in(step, r)
                if following:
                    combine(next_step, f, 1)
                gelu(step, r)
                if following:
                    statistics(next_step, f)
                gated(step, r)
                if following:
                    normed(next_step, f)
                if last:
                    best(routing_step, s)
                    slots(routing_step, s)
                normed2(step, r, xg2[p])
                if last:
                    weights(routing_step, s)
                assert not following or next_step.n == STEPS_X, next_step.n
                assert step.n == STEPS_Y, step.n
                assert not last or routing_step.n == STEPS_R, routing_step.n

            dve.wait_ge(preset, 1)
            dve.wait_ge(const_mm, 1)
            V.tensor_copy(biasc[:, :], tr_ps[:, 0:SEQP])
            V.tensor_copy(wcol[:, :], tr_ps[:, 256:257]).then_inc(const_ready, 1)
            dve.wait_ge(const_ready, 1)
            step = Steps(dve, own_x, STEPS_X)
            combine(step, 1, 0)
            combine(step, 1, 1)
            statistics(step, 1)
            normed(step, 1)
            passes(dve, body)
            step = Steps(dve, own_r, STEPS_R * PAIRS)
            best(step, PAIRS)
            slots(step, PAIRS)
            weights(step, PAIRS)


def mixture_phase(nc, m, d, ctx):
    with ExitStack() as own:
        def sb(name, shape, dt=F32):
            return own.enter_context(nc.sbuf_tensor(name, shape, dt))

        WAYS = 4
        ways = range(WAYS)

        def sem(name):
            return ctx.enter_context(nc.semaphore("t_" + name))

        def sems(name):
            return [sem(f"{name}{n}") for n in ways]

        ident = cview(m, "ident")
        nt, se, be, lo = sb("t_tiles", [1, E2]), sb("t_start", [1, E2]), sb("t_base", [1, E2]), sb("t_lower", [1, E2, E2])
        big, big2 = sb("t_big", [1, MT2, E2]), sb("t_big2", [1, MT2, E2])
        fe, fr, ff, fw = (sb(f"t_f{n}", [1, MT2]) for n in range(4))
        tabe, tabr = (sb(f"t_tab{n}", [1, MT2], I32) for n in range(2))
        mv, dl, dls = sb("t_firsts", [1, E2 + 1]), sb("t_moves", [1, E2 + 1]), sb("t_moves_all", [ROWS, E2 + 1])
        slf, acc, mov = (sb(f"t_slots{n}", [ROWS, PAIRS * 2 * TILES]) for n in range(3))
        zb, zi, zt = sb("t_tail_f", [1, E2]), sb("t_tail", [1, E2], I32), sb("t_zeros", [128, HID])
        xr = [sb(f"t_rows{n}", [128, HID]) for n in ways]; xT = [sb(f"t_xT{n}", [128, 128]) for n in ways]
        th = [sb(f"t_tanh{n}", [128, EH2]) for n in ways]; hh = [sb(f"t_hid{n}", [128, EH2]) for n in ways]
        hT = [sb(f"t_hidT{n}", [128, 2, 128]) for n in ways]; ys = sb("t_out", [128, WAYS, HID])
        gps = [own.enter_context(nc.psum_tensor(f"t_gu{n}", [128, 2, EH2], F32)) for n in ways]
        tps = [own.enter_context(nc.psum_tensor(f"t_tr{n}", [128, 4, 128], F32)) for n in ways]
        moves_mm, moves_ready, own_p = sem("moves_mm"), sem("moves_ready"), sem("pool")
        own_t, table_ready, zeroed, tails = sem("dve"), sem("table_ready"), sem("zeroed"), sem("tails")
        loaded, t_mm, xT_ready, gu_mm = sems("loaded"), sem("t_mm"), sem("xT_ready"), sem("gu_mm")
        th_ready, a_ready, h_ready, hT_mm = sem("th_ready"), sem("a_ready"), sem("h_ready"), sem("hT_mm")
        hT_ready, y_mm, y_ready, stored = sem("hT_ready"), sem("y_mm"), sem("y_ready"), sem("stored")
        block = own.enter_context(nc.Block())
        N = MT2 // WAYS

        @block.gpsimd
        def _(pool):
            nc.gpsimd.memset(zt[:, :], 0.0).then_inc(zeroed, 1)
            pool.wait_ge(moves_ready, 1)
            step = Steps(pool, own_p)
            all_slots = m.slots2[:, :, :].rearrange("p a n -> p (a n)")
            step(nc.gpsimd.tensor_copy(slf[:, :], all_slots))
            step(nc.gpsimd.tensor_scalar(acc[:, :], slf[:, :], dls[:, 0:1], None, ALU.add))
            for e in range(1, E2 + 1):
                step(nc.gpsimd.tensor_scalar(mov[:, :], slf[:, :], float(REG2 * e), dls[:, e:e + 1], ALU.is_ge, ALU.mult))
                step(nc.gpsimd.tensor_tensor(acc[:, :], acc[:, :], mov[:, :], ALU.add))
            step(nc.gpsimd.tensor_copy(all_slots, acc[:, :]))

        @block.sync
        def _(sp):
            for s in (t_mm, xT_ready, gu_mm, th_ready, a_ready, h_ready, hT_mm, hT_ready, y_mm, y_ready):
                sp.sem_inc(s, WAYS)
            sp.sem_inc(stored, 16)
            sp.wait_ge(zeroed, 1)
            sp.wait_ge(table_ready, 1)
            for e in range(E2):
                at = sp.value_load(zi[0:1, e:e + 1], min_val=0, max_val=SLOTS2 - 128)
                sp.dma_start(d["buf2"][bass.ds(at, 128), :], zt[:, :]).then_inc(tails, 16)
            sp.wait_ge(tails, 16 * E2)
            with sp.Fori(1, N + 1) as i:
                for n in ways:
                    sp.wait_ge(t_mm, WAYS * i + (n + 1 - WAYS))
                    at = sp.value_load(tabr[0:1, bass.ds(WAYS * i + (n - WAYS), 1)], min_val=0, max_val=SLOTS2)
                    sp.dma_start(xr[n][:, :], d["buf2"][bass.ds(at, 128), :]).then_inc(loaded[n], 16)

        @block.tensor
        def _(pe):
            T = nc.tensor
            pe.wait_ge(table_ready, 1)
            T.matmul(tps[0][0:ROWS, 0, 0:E2 + 1], lhsT=cview(m, "ones")[0:1, 0:ROWS], rhs=dl[:, :],
                     start=True, stop=True).then_inc(moves_mm, 1)
            pe.wait_ge(moves_ready, 1)

            def gate_up(i, n):
                expert = pe.value_load(tabe[0:1, bass.ds(WAYS * i + (n - WAYS), 1)], min_val=0, max_val=E2 - 1)
                pe.wait_ge(xT_ready, WAYS * i + (n + 1))
                T.matmul(gps[n][:, :, :].rearrange("p a c -> p (a c)"), lhsT=xT[n][:, :],
                         rhs=m.wgu[:, bass.ds(expert, 1), :].rearrange("p a c -> p (a c)"),
                         start=True, stop=True).then_inc(gu_mm, 1)

            def transpose_rows(i, n):
                pe.wait_ge(loaded[n], 16 * i)
                T.transpose(tps[n][:, 0, :], xr[n][:, :], ident).then_inc(t_mm, 1)

            def transpose_hidden(i, n):
                pe.wait_ge(h_ready, WAYS * i + (n + 1))
                for c in range(2):
                    last = T.transpose(tps[n][:, 1 + c, :], hh[n][:, 128 * c:128 * c + 128], ident)
                last.then_inc(hT_mm, 1)

            def down(i, n):
                expert = pe.value_load(tabe[0:1, bass.ds(WAYS * i + (n - WAYS), 1)], min_val=0, max_val=E2 - 1)
                pe.wait_ge(hT_ready, WAYS * i + (n + 1))
                for c in range(2):
                    last = T.matmul(tps[n][:, 3, :], lhsT=hT[n][:, c, :],
                                    rhs=m.wd[:, bass.ds(expert, 1), c, :].rearrange("p a c -> p (a c)"),
                                    start=(c == 0), stop=(c == 1))
                last.then_inc(y_mm, 1)

            for n in ways:
                transpose_rows(1, n)
            for n in ways:
                gate_up(1, n)
            with pe.Fori(2, N + 1) as i:
                for n in ways:
                    pe.wait_ge(y_ready, WAYS * i + (n + 1 - 2 * WAYS))
                    transpose_rows(i, n)
                for n in ways:
                    pe.wait_ge(xT_ready, WAYS * i + (n + 1))
                    transpose_hidden(i - 1, n)
                    gate_up(i, n)
                for n in ways:
                    down(i - 1, n)
            for n in ways:
                pe.wait_ge(y_ready, WAYS * N + (n + 1 - WAYS))
                transpose_hidden(N, n)
            for n in ways:
                down(N, n)

        @block.scalar
        def _(act):
            A = nc.scalar
            act.wait_ge(table_ready, 1)

            def rows_in(i, n):
                act.wait_ge(t_mm, WAYS * i + (n + 1))
                A.activation(xT[n][:, :], tps[n][:, 0, :], ACT.Copy).then_inc(xT_ready, 1)

            def gate(i, n):
                act.wait_ge(gu_mm, WAYS * i + (n + 1))
                A.activation(th[n][:, :], gps[n][:, 0, :], ACT.Tanh, scale=0.5).then_inc(th_ready, 1)

            def results(i):
                act.wait_ge(stored, 16 * i)
                for n in ways:
                    act.wait_ge(y_mm, WAYS * i + (n + 1))
                    A.activation(ys[:, n, :], tps[n][:, 3, :], ACT.Copy).then_inc(y_ready, 1)
                act.wait_ge(y_ready, WAYS * i + WAYS)
                dst = d["y2"][bass.ds(i * (WAYS * 128) - WAYS * 128, WAYS * 128), :].rearrange("(n p) c -> p n c", p=128)
                act.dma_start(dst, ys[:, :, :]).then_inc(stored, 16)

            for n in ways:
                rows_in(1, n)
            for n in ways:
                gate(1, n)
            with act.Fori(2, N + 1) as i:
                for n in ways:
                    rows_in(i, n)
                for n in ways:
                    gate(i, n)
                results(i - 1)
            results(N)
            act.wait_ge(stored, 16 * (N + 1))

        @block.vector
        def _(dve):
            V = nc.vector
            step = Steps(dve, own_t)
            step(V.tensor_copy(lo[:, :, :], cview(m, "lower8", 1).rearrange("p (a b) -> p a b", a=E2)))
            step(V.tensor_scalar(nt[:, :], m.carry2[:, :], 1.0 / 128, 127.0 / 256, ALU.mult, ALU.add))
            step(V.tensor_scalar(nt[:, :], nt[:, :], ROUND, None, ALU.add))
            step(V.tensor_scalar(nt[:, :], nt[:, :], ROUND, None, ALU.subtract))
            step(V.tensor_tensor(lo[:, :, :], lo[:, :, :], nt[:, None, :].broadcast_to([1, E2, E2]), ALU.mult))
            step(V.tensor_reduce(se[:, :], lo[:, :, :], AX_X, ALU.add))
            step(V.scalar_tensor_tensor(out=be[:, :], in0=se[:, :], scalar=-128.0, in1=cview(m, "eoff2", 1),
                                        op0=ALU.mult, op1=ALU.add))
            step(V.tensor_tensor(nt[:, :], nt[:, :], se[:, :], ALU.add))
            index = cview(m, "tile_index", 1)
            wide = lambda t: t[:, :, None].broadcast_to([1, MT2, E2])
            each = lambda t: t[:, None, :].broadcast_to([1, MT2, E2])
            step(V.tensor_tensor(big[:, :, :], each(nt[:, :]), wide(index), ALU.is_le))
            step(V.tensor_reduce(fe[:, :], big[:, :, :], AX_X, ALU.add))
            step(V.tensor_tensor(big[:, :, :], each(cview(m, "iota64", 1)[:, 0:E2]), wide(fe[:, :]), ALU.is_equal))
            step(V.tensor_reduce(ff[:, :], big[:, :, :], AX_X, ALU.add))
            step(V.tensor_tensor(big2[:, :, :], big[:, :, :], each(be[:, :]), ALU.mult))
            step(V.tensor_reduce(fr[:, :], big2[:, :, :], AX_X, ALU.add))
            step(V.tensor_tensor(fw[:, :], ff[:, :], index, ALU.mult))
            step(V.scalar_tensor_tensor(out=fr[:, :], in0=fw[:, :], scalar=128.0, in1=fr[:, :], op0=ALU.mult, op1=ALU.add))
            step(V.tensor_scalar(tabr[:, :], fr[:, :], float(SLOTS2), None, ALU.add))
            step(V.tensor_scalar(mv[:, 0:E2], se[:, :], 128.0, None, ALU.mult))
            step(V.memset(mv[:, E2:E2 + 1], float(128 * MT2)))
            step(V.tensor_scalar(dl[:, 0:1], mv[:, 0:1], 1.0, None, ALU.mult))
            step(V.tensor_tensor(dl[:, 1:], mv[:, 1:], mv[:, 0:E2], ALU.subtract))
            step(V.tensor_scalar(dl[:, 1:], dl[:, 1:], float(-REG2), None, ALU.add))
            step(V.tensor_scalar(tabe[:, :], fe[:, :], float(E2 - 1), None, ALU.min))
            step(V.scalar_tensor_tensor(out=zb[:, :], in0=m.carry2[:, :], scalar=float(SLOTS2), in1=cview(m, "eoff2", 1),
                                        op0=ALU.add, op1=ALU.add))
            step(V.tensor_copy(zi[:, :], zb[:, :]), table_ready, 1)
            dve.wait_ge(moves_mm, 1)
            step(V.tensor_copy(dls[:, :], tps[0][0:ROWS, 0, 0:E2 + 1]), moves_ready, 1)

            def hidden(i, n):
                dve.wait_ge(th_ready, WAYS * i + (n + 1))
                V.scalar_tensor_tensor(out=th[n][:, :], in0=th[n][:, :], scalar=1.0, in1=gps[n][:, 0, :],
                                       op0=ALU.add, op1=ALU.mult).then_inc(a_ready, 1)
                dve.wait_ge(a_ready, WAYS * i + (n + 1))
                V.tensor_tensor(hh[n][:, :], th[n][:, :], gps[n][:, 1, :], ALU.mult).then_inc(h_ready, 1)

            def transposed(i, n):
                dve.wait_ge(hT_mm, WAYS * i + (n + 1))
                V.tensor_copy(hT[n][:, :, :], tps[n][:, 1:3, :]).then_inc(hT_ready, 1)

            for n in ways:
                hidden(1, n)
            with dve.Fori(2, N + 1) as i:
                for n in ways:
                    transposed(i - 1, n)
                    hidden(i, n)
            for n in ways:
                transposed(N, n)


def output_phase(nc, m, d, ctx):
    with ExitStack() as own:
        def sem(name):
            return ctx.enter_context(nc.semaphore("o_" + name))

        def sb(name, shape, dt=F32):
            return [own.enter_context(nc.sbuf_tensor(f"{name}{p}", shape, dt)) for p in two]

        two = range(2)
        NK = 2 * TILES
        sl, wt = sb("o_slots", [ROWS, NK], I32), sb("o_wts", [ROWS, NK])
        ga, o = sb("o_gathered", [ROWS, NK, HID]), sb("o_rows", [ROWS, TILES, HID])
        idx_in, comb, own_o, wt_in = (sem(n) for n in ("idx_in", "comb", "dve", "wt_in"))
        gathered, stored = [sem(f"gathered{p}") for p in two], [sem(f"stored{p}") for p in two]
        block = own.enter_context(nc.Block())

        @block.gpsimd
        def _(pool):
            with pool.Fori(1, PAIRS // 2 + 1) as i:
                for p in two:
                    r = 2 * i + (p - 1)
                    pool.wait_ge(comb, r)
                    nc.gpsimd.tensor_copy(sl[p][:, :], m.slots2[:, bass.ds(r - 1, 1), :].rearrange("p a n -> p (a n)")
                                          ).then_inc(idx_in, 1)
                    pool.wait_ge(idx_in, r)
                    pool.nop(nofuse=True)
                    for n in range(NK):
                        nc.gpsimd.indirect_dma_start(
                            out=ga[p][:, n, :], out_offset=None, in_=d["y2"],
                            in_offset=bass.IndirectOffsetOnAxis(ap=sl[p][:, n:n + 1], axis=0)).then_inc(gathered[p], 16)

        @block.vector
        def _(dve):
            V = nc.vector
            with dve.Fori(1, PAIRS // 2 + 1) as i:
                for p in two:
                    r = 2 * i + (p - 1)
                    step = Steps(dve, own_o, r - 1)
                    step(V.tensor_scalar(wt[p][:, :], m.wts2[:, bass.ds(r - 1, 1), :].rearrange("p a n -> p (a n)"), 1.0,
                                         None, ALU.mult), wt_in, r)
                    dve.wait_ge(gathered[p], i * (16 * NK))
                    dve.wait_ge(stored[p], 32 * i)
                    for n in range(NK):
                        j = n % TILES
                        base = m.hres[:, bass.ds(r - 1, 1), j, :].rearrange("p a c -> p (a c)") if n < TILES else o[p][:, j, :]
                        x = V.scalar_tensor_tensor(out=o[p][:, j, :], in0=ga[p][:, n, :], scalar=wt[p][:, n:n + 1],
                                                   in1=base, op0=ALU.mult, op1=ALU.add)
                        if n == TILES - 1:
                            step(x)
                    x.then_inc(comb, 1)

        @block.sync
        def _(sp):
            sp.sem_inc(comb, 2)
            for p in two:
                sp.sem_inc(stored[p], 32)
            with sp.Fori(1, PAIRS // 2 + 1) as i:
                for p in two:
                    sp.wait_ge(comb, 2 * i + (p + 1))
                    for t in range(2):
                        n = ROWS - t
                        dst = d["out"][bass.ds(4 * i + (2 * p - 4), 2), ROWS * t:ROWS * t + n, :].rearrange("b s c -> s b c")
                        sp.dma_start(dst, o[p][0:n, t::2, :]).then_inc(stored[p], 16)
            for p in two:
                sp.wait_ge(stored[p], 32 * (PAIRS // 2 + 1))


def program(nc, d):
    for k, shape in SCRATCH.items():
        d[k] = nc.dram_tensor("scratch_" + k, shape, F32).ap()
    with ExitStack() as ctx:
        m = memory(nc, ctx)
        for phase in (setup_phase, patch_phase, token_phase, expert_phase, ssm_phase, mixture_phase, output_phase):
            phase(nc, m, d, ctx)

def _layout(inputs):
    f = lambda k: np.asarray(inputs[k])
    a = {}
    x = f("x").reshape(BATCH, CHANS, GRID, PATCH, GRID, PATCH).transpose(0, 2, 4, 1, 3, 5)
    x = x.reshape(BATCH * NPATCH, PDIM)
    xp = np.zeros((BATCH * NPATCH, KCH * 128), x.dtype)
    xp[:, :PDIM] = x
    a["xpat"] = xp.reshape(2 * GROUPS, GB * NPATCH // 2, KCH, 128).transpose(0, 3, 2, 1)
    w = np.zeros((KCH * 128, HID), x.dtype)
    w[:PDIM] = f("L0_tok_W").T
    a["wtok"] = w.reshape(KCH, 128, HID).transpose(1, 0, 2)
    a["tokb"] = f("L0_tok_b")[:, None]
    a["cls"] = f("L0_tok_class_token").T
    a["posT"] = f("L0_tok_pos_embed").T
    a["ytxt"] = f("x_txt").reshape(PAIRS, 2 * NTEXT)
    a["emb"], a["cw"] = f("L0_txt_emb_weight"), f("L0_txt_conv_weight")[:, 0, :]

    def heads(ws, wp):
        ws, wp = ws.reshape(-1, HEADS, HD), wp.reshape(-1, HEADS, NPT)
        o = np.zeros((ws.shape[0], HEADS, 32), ws.dtype)
        o[:, :, 2:2 + HD], o[:, :, 2 + HD:2 + HD + NPT] = ws, wp
        return o.reshape(-1, 2, 128)

    a["wq"] = heads(f("L0_attn_wq"), f("L0_attn_wqp"))
    a["wk"] = heads(f("L0_attn_wk"), f("L0_attn_wkp"))
    a["brow"] = np.concatenate([heads(f("L0_attn_bq")[None], f("L0_attn_bqp")[None]).reshape(1, 256),
                                heads(f("L0_attn_bk")[None], f("L0_attn_bkp")[None]).reshape(1, 256)], axis=1)
    a["wv"], a["wo"] = f("L0_attn_wv"), f("L0_attn_wo")
    a["bv"], a["bo"] = f("L0_attn_bv")[None], f("L0_attn_bo")[None]
    a["lng"], a["lnb"] = f("L0_attn_ln_g")[:, None], f("L0_attn_ln_b")[:, None]
    a["pscale"] = f("L0_attn_pscale")[:, None]
    a["gatew"] = f("L0_ffn_gate_w").T
    a["sw13"] = np.concatenate([f("L0_ffn_sw1"), f("L0_ffn_sw3")], axis=1)
    a["sw2"] = f("L0_ffn_sw2")
    a["w13"] = np.concatenate([f("L0_ffn_w1"), f("L0_ffn_w3")], axis=2)
    a["w2"] = f("L0_ffn_w2")
    a["normw"], a["normb"] = f("L1_attn_norm_weight")[None], f("L1_attn_norm_bias")[None]
    a["ssm"] = np.stack([np.tile(f("L1_attn_" + k), 2) for k in ("lambda_re", "lambda_im", "p_re", "p_im")])[None]
    a["bc"] = np.stack([np.concatenate([f("L1_attn_b_re"), f("L1_attn_b_im")]),
                        np.concatenate([f("L1_attn_c_re"), f("L1_attn_c_im")])], axis=1)
    a["logstep"] = f("L1_attn_log_step").reshape(1, 1)
    a["dsc"] = f("L1_attn_d").reshape(1, 1)
    a["outw"] = np.concatenate([f("L1_attn_out_w").T, f("L1_attn_out2_w").T], axis=1)
    a["outb"] = np.concatenate([f("L1_attn_out_b"), f("L1_attn_out2_b")])[None]
    a["rtw"] = f("L1_ffn_router_w").T
    a["wgu"] = np.concatenate([f("L1_ffn_w_gate"), f("L1_ffn_w_up")], axis=2).transpose(1, 0, 2)
    a["wd"] = f("L1_ffn_w_down").reshape(E2, 2, 128, HID).transpose(2, 0, 1, 3)
    a["cst"] = CONSTS
    return {k: np.ascontiguousarray(v) for k, v in a.items()}


SCRATCH = {"buf1": [SLOTS1, HID], "y1": [SLOTS1 + 128, HID], "buf2": [SLOTS2 + 128, HID],
           "y2": [128 * MT2 + 128, HID], "kpad": [1, SEQ + SEQP]}


def kernel(**inputs):
    import concourse.bacc as bacc
    from concourse.bass_utils import run_bass_kernel_spmd

    nc = bacc.Bacc("TRN2", target_bir_lowering=False, num_devices=1)
    arrays = _layout(inputs)
    d = {k: nc.dram_tensor("in_" + k, v.shape, mybir.dt.from_np(v.dtype), kind="ExternalInput").ap()
         for k, v in arrays.items()}
    d["out"] = nc.dram_tensor("out", [BATCH, SEQ, HID], F32, kind="ExternalOutput").ap()
    program(nc, d)
    r = run_bass_kernel_spmd(nc, [{"in_" + k: v for k, v in arrays.items()}], core_ids=[0])
    return r.results[0]["out"]
```

```python
from contextlib import ExitStack

import numpy as np
import concourse.bass as bass
from concourse import mybir

F32 = mybir.dt.float32
BF16 = mybir.dt.bfloat16
I32 = mybir.dt.int32
U32 = mybir.dt.uint32
ALU = mybir.AluOpType
ACT = mybir.ActivationFunctionType
AX_X = mybir.AxisListType.X

BATCH, CHANS, IMG, PATCH = 64, 3, 224, 28
GRID = IMG // PATCH
NPATCH = GRID * GRID
PDIM = CHANS * PATCH * PATCH
HID = 128
NTEXT = 128
SEQ = 1 + NPATCH + NTEXT
SEQP = SEQ + 1
ROWS = SEQP // 2
PAIRS = BATCH // 2
TILES = 4
COLS = 2 * SEQP
KCH = -(-PDIM // 128)
GROUPS, GB = 8, 8
VOCAB = 125
HEADS, HD, NPT = 8, 16, 12
EPS = 1e-5
E1, CAP, EH = 64, 256, 64
SLOTS1 = E1 * CAP
E2, EH2 = 8, 256
REG2 = BATCH * SEQ + 128
SLOTS2 = E2 * REG2
MT2 = (2 * BATCH * SEQ) // 128 + E2
MT2 += -MT2 % 4
ROUTE_SCALE = 2.5
NST = 64
ROUND = 1.5 * 2.0 ** 23

CONST_COLS = {}


def constants():
    parts = {}
    p = np.arange(128)
    parts["ident"] = np.eye(128)
    parts["ones"] = np.ones((128, 128))
    tri = np.zeros((128, ROWS))
    tri[:ROWS] = (np.arange(ROWS)[:, None] < np.arange(ROWS)[None, :])
    parts["tri"] = tri
    rev = np.zeros((128, ROWS))
    rev[:ROWS] = np.eye(ROWS)[::-1]
    parts["rev"] = rev
    jm = np.zeros((128, 128))
    for n in range(NST):
        jm[n, n + NST] = -1.0
        jm[n + NST, n] = 1.0
    parts["jmat"] = jm
    hsel = np.zeros((128, 2, 128))
    for h in range(HEADS):
        hsel[h, h // 4, 32 * (h % 4):32 * (h % 4) + 32] = 1.0
    parts["hsel"] = hsel.reshape(128, 256)
    q = p % 32
    parts["row0"] = (q == 0)[:, None]
    parts["row1"] = (q == 1)[:, None]
    parts["rows_s"] = ((q >= 2) & (q < 2 + HD))[:, None]
    parts["rows_p"] = ((q >= 2 + HD) & (q < 2 + HD + NPT))[:, None]
    sel = np.zeros((128, 2, 128))
    for a in p:
        if 2 + HD <= a % 32 < 2 + HD + NPT:
            sel[a, 0, 32 * (a // 32)] = 1.0
            sel[a, 1, 32 * (a // 32) + 1] = 1.0
    parts["psel"] = sel.reshape(128, 256)
    parts["vocab"] = p[:, None]
    parts["iota64"] = np.tile(np.arange(E1), (128, 1))
    parts["eoff1"] = np.tile(CAP * np.arange(E1) - SLOTS1, (128, 1))
    parts["eoff2"] = np.tile(REG2 * np.arange(E2) - SLOTS2, (128, 1))
    pad = np.zeros((128, 2, TILES))
    pad[ROWS - 1, :, 1::2] = 1000.0
    parts["padbig"] = pad.reshape(128, 2 * TILES)
    half = (np.arange(128) >= NST).astype(float)
    ma = np.zeros((128, 128)); ma[0] = 1 - half; ma[1] = half
    mb = np.zeros((128, 128)); mb[0] = half; mb[1] = half - 1
    parts["mask_a"], parts["mask_b"] = ma, mb
    parts["csign"] = (1.0 - 2.0 * (p >= NST))[:, None]
    tix = np.zeros((128, MT2)); tix[:] = np.arange(MT2)
    parts["tile_index"] = tix
    parts["lower8"] = np.zeros((128, 64))
    parts["lower8"][0] = (np.arange(8)[None, :] < np.arange(8)[:, None]).reshape(64)
    at, cols = 0, {}
    for k, v in parts.items():
        cols[k] = (at, v.shape[1])
        at += v.shape[1]
    return np.concatenate([np.asarray(v, np.float32) for v in parts.values()], axis=1), cols


CONSTS, CONST_COLS = constants()
NCONST = CONSTS.shape[1]


class Memory:
    pass


class Steps:

    def __init__(self, eng, own, base=0, start=0):
        self.eng, self.own, self.base, self.n = eng, own, base, start

    def __call__(self, ins, signal=None, value=None):
        if signal is None:
            self.n += 1
            signal, value = self.own, self.base + self.n
        ins.then_inc(signal, 1)
        self.eng.wait_ge(signal, value)


def memory(nc, ctx):
    m = Memory()

    def sb(name, shape, dt=F32):
        return ctx.enter_context(nc.sbuf_tensor(name, shape, dt))

    m.cst = sb("cst", [128, NCONST])
    m.tok = sb("tok", [128, max(BATCH * NPATCH, E2 * 2 * EH2)])
    m.hres = sb("hres", [ROWS, PAIRS, TILES, HID])
    m.slots1 = sb("slots1", [ROWS, PAIRS, 2 * TILES], I32)
    m.wts1 = sb("wts1", [ROWS, PAIRS, 2 * TILES])
    m.slots2 = sb("slots2", [ROWS, PAIRS, 2 * TILES], I32)
    m.wts2 = sb("wts2", [ROWS, PAIRS, 2 * TILES])
    m.wq = sb("wq", [128, 2, 128]); m.wk = sb("wk", [128, 2, 128]); m.wv = sb("wv", [128, 128]); m.wo = sb("wo", [128, 128])
    m.bo_row = sb("bo_row", [1, 128]); m.biasq = sb("biasq", [128, 2]); m.biask = sb("biask", [128, 2])
    m.rawq = sb("rawq", [128, 2]); m.rawk = sb("rawk", [128, 2]); m.scaleq = sb("scaleq", [128, 2])
    m.esq = sb("esq", [128, 2, 128]); m.esk = sb("esk", [128, 2, 128])
    m.embt = sb("embt", [VOCAB, 128]); m.convq = sb("convq", [128, 2])
    m.posT = sb("posT", [128, 1 + NPATCH]); m.tokb = sb("tokb", [128, 1])
    m.gatew = sb("gatew", [128, E1]); m.sw13 = sb("sw13", [128, 256]); m.sw2 = sb("sw2", [128, 128])
    m.outw = sb("outw", [128, 256]); m.outb = sb("outb", [1, 256])
    m.normw = sb("normw", [ROWS, 128]); m.normb = sb("normb", [ROWS, 128])
    m.toep = sb("toep", [ROWS, 2, SEQP])
    m.rtw = sb("rtw", [128, E2])
    m.wd = sb("wd", [128, E2, 2, 128])
    m.tri_bf = sb("tri_bf", [ROWS, ROWS], BF16); m.ones_bf = sb("ones_bf", [ROWS, ROWS], BF16)
    m.carry = sb("carry", [1, E1]); m.carry2 = sb("carry2", [1, E2])
    m.hT = sb("hT", [128, 2, SEQP])
    return m


def cview(m, name, rows=128):
    a, n = CONST_COLS[name]
    return m.cst[0:rows, a:a + n]


def setup_phase(nc, m, d, ctx):
    m.patch_memory = ExitStack()
    m.wtok = m.patch_memory.enter_context(nc.sbuf_tensor("wtok", [128, KCH, 128], F32))
    m.pat = [m.patch_memory.enter_context(nc.sbuf_tensor(f"patches{n}", [128, KCH, GB * NPATCH // 2], F32))
             for n in range(2)]
    m.wtok_loaded = ctx.enter_context(nc.semaphore("wtok_loaded"))
    m.patches_loaded = [ctx.enter_context(nc.semaphore(f"patches_loaded{n}")) for n in range(2)]
    with ExitStack() as own:
        def sb(name, shape, dt=F32):
            return own.enter_context(nc.sbuf_tensor(name, shape, dt))

        sems = []

        def sem(name):
            sems.append(nc.alloc_semaphore(name))
            return sems[-1]

        ps = [own.enter_context(nc.psum_tensor(f"setup_ps{n}", [128, 512], F32)) for n in range(4)]
        emb = sb("emb", [VOCAB, 128]); cw = sb("cw", [128, 2])
        lng = sb("lng", [128, 1]); lnb = sb("lnb", [128, 1])
        brow = sb("brow", [1, 512]); bvrow = sb("bvrow", [1, 128]); borow = sb("borow", [1, 128])
        psc = sb("psc", [HEADS, 1]); psr = sb("psr", [128, 2]); npsr = sb("npsr", [128, 2])
        clsc = sb("clsc", [128, 1])
        ssm = sb("ssm", [2, 4, 128])
        bc = sb("bc", [128, 2])
        ls = sb("ls", [128, 1]); dsc = sb("dsc", [1, 1])
        tq = sb("tq", [128, 8]); tqe = sb("tqe", [128, 128]); tqc = sb("tqc", [128, 2])
        zrow = sb("zrow", [128, 2048])
        z = sb("ssm_z", [2, 20, 128]); z1 = sb("ssm_z1", [2, 12]); zc = sb("ssm_cols", [128, 6])
        a0 = sb("a0", [128, 128]); a0t = sb("a0t", [128, 128])
        a1 = sb("a1", [128, 128]); a1t = sb("a1t", [128, 128])
        pw = sb("pw", [128, 2, 128]); qw = sb("qw", [128, 2, 128])
        vm = sb("vm", [128, 256]); krow = sb("krow", [1, SEQP]); hank = sb("hank", [ROWS, 2, SEQP])
        bvc = sb("bvc", [128, 1])

        ld = sem("setup_loaded"); zs = sem("scratch_zeroed"); kst = sem("kernel_stored")
        hk = sem("hankel_loaded"); zz = sem("zero_row_set"); own_step = sem("setup_dve_step")
        exp_done = sem("step_size_ready")
        scale_mm, bias_mm, bv_mm, bo_mm = sem("scale_mm"), sem("bias_mm"), sem("bv_mm"), sem("bo_mm")
        amax_t, qscale_mm, ssm_mm, ab_mm = sem("amax_t"), sem("qscale_mm"), sem("ssm_mm"), sem("ab_mm")
        power_mm, kern_mm, toep_mm = sem("power_mm"), sem("kern_mm"), sem("toep_mm")
        bv_ready, amax_ready, qscale_ready = sem("bv_ready"), sem("amax_ready"), sem("qscale_ready")
        rank2_ready, a_ready, v0_ready = sem("rank2_ready"), sem("a_ready"), sem("v0_ready")
        power_ready, kern_ready = sem("power_ready"), sem("kern_ready")

        loads = [(m.cst[:, :], d["cst"]), (m.wq[:, :, :], d["wq"]), (m.wk[:, :, :], d["wk"]),
                 (m.wv[:, :], d["wv"]), (m.wo[:, :], d["wo"]), (brow[:, :], d["brow"]),
                 (bvrow[:, :], d["bv"]), (borow[:, :], d["bo"]), (psc[:, :], d["pscale"]),
                 (emb[:, :], d["emb"]), (cw[:, :], d["cw"]), (lng[:, :], d["lng"]), (lnb[:, :], d["lnb"]),
                 (m.posT[:, :], d["posT"]), (m.tokb[:, :], d["tokb"]), (clsc[:, :], d["cls"]),
                 (m.gatew[:, :], d["gatew"]), (m.sw13[:, :], d["sw13"]), (m.sw2[:, :], d["sw2"]),
                 (m.outw[:, :], d["outw"]), (m.outb[:, :], d["outb"]),
                 (m.normw[:, :], d["normw"].broadcast_to([ROWS, 128])),
                 (m.normb[:, :], d["normb"].broadcast_to([ROWS, 128])),
                 (m.rtw[:, :], d["rtw"]), (m.wd[:, :, :, :], d["wd"]),
                 (ssm[:, :, :], d["ssm"].broadcast_to([2, 4, 128])), (bc[:, :], d["bc"]),
                 (ls[:, :], d["logstep"].broadcast_to([128, 1])), (dsc[:, :], d["dsc"])]

        ident, ones = cview(m, "ident"), cview(m, "ones")
        row0, row1 = cview(m, "row0"), cview(m, "row1")
        block = own.enter_context(nc.Block())

        @block.sync
        def _(sp):
            for dst, src in loads:
                sp.dma_start(dst, src, allow_slow_non_contiguous=True).then_inc(ld, 16)
            sp.dma_start(m.wtok[:, :, :], d["wtok"]).then_inc(m.wtok_loaded, 16)
            for n in range(2):
                sp.sem_inc(m.patches_loaded[n], 16)
                sp.dma_start(m.pat[n][:, :, :], d["xpat"][n]).then_inc(m.patches_loaded[n], 16)
            sp.wait_ge(zz, 1)
            for n in range(SLOTS1 // 2048):
                sp.dma_start(d["buf1"][2048 * n:2048 * n + 2048, :].rearrange("(p a) c -> p (a c)", p=128),
                             zrow[:, :]).then_inc(zs, 16)
            sp.dma_start(d["y1"][SLOTS1:SLOTS1 + 128, :], zrow[:, 0:128]).then_inc(zs, 16)
            sp.dma_start(d["buf2"][SLOTS2:SLOTS2 + 128, :], zrow[:, 0:128]).then_inc(zs, 16)
            sp.dma_start(d["y2"][128 * MT2:128 * MT2 + 128, :], zrow[:, 0:128]).then_inc(zs, 16)
            sp.dma_start(d["kpad"][0:1, 0:SEQ], zrow[0:1, 0:SEQ]).then_inc(kst, 16)
            sp.wait_ge(kern_ready, 1)
            sp.dma_start(d["kpad"][0:1, SEQ:SEQ + SEQP], krow[:, :]).then_inc(kst, 16)
            sp.wait_ge(kst, 32)
            for a in range(2):
                src = bass.AP(tensor=d["kpad"].tensor, offset=ROWS * (1 - a), ap=[[1, ROWS], [1, SEQP]])
                sp.dma_start(hank[:, a, :], src).then_inc(hk, 16)
            sp.wait_ge(zs, 16 * (SLOTS1 // 2048 + 3))

        @block.gpsimd
        def _(pool):
            nc.gpsimd.memset(zrow[:, :], 0.0).then_inc(zz, 1)
        @block.scalar
        def _(act):
            act.wait_ge(ld, 16 * len(loads))
            nc.scalar.activation(zc[:, 0:1], ls[:, :], ACT.Exp).then_inc(exp_done, 1)

        doublings = []
        n = 1
        while n < SEQP:
            doublings.append((n, min(n, SEQP - n)))
            n *= 2

        @block.tensor
        def _(pe):
            T = nc.tensor
            pe.wait_ge(ld, 16 * len(loads))
            for g in range(2):
                last = T.matmul(ps[0][:, g:g + 1], lhsT=cview(m, "hsel")[0:HEADS, 128 * g:128 * g + 128],
                                rhs=psc[:, :], start=True, stop=True)
            last.then_inc(scale_mm, 1)
            for n, w in ((0, m.wq), (2, m.wk)):
                for g in range(2):
                    T.matmul(ps[1][:, n + g:n + g + 1], lhsT=w[:, g, :], rhs=lnb[:, :], start=True, stop=False)
                    last = T.matmul(ps[1][:, n + g:n + g + 1], lhsT=brow[:, 128 * (n + g):128 * (n + g) + 128],
                                    rhs=ones[0:1, 0:1], start=False, stop=True)
            last.then_inc(bias_mm, 1)
            T.matmul(ps[2][:, 0:1], lhsT=m.wv[:, :], rhs=lnb[:, :], start=True, stop=False)
            T.matmul(ps[2][:, 0:1], lhsT=bvrow[:, :], rhs=ones[0:1, 0:1], start=False, stop=True).then_inc(bv_mm, 1)
            pe.wait_ge(bv_ready, 1)
            T.matmul(ps[2][0:1, 0:128], lhsT=bvc[:, :], rhs=m.wo[:, :], start=True, stop=True).then_inc(bo_mm, 1)
            for n, rows in enumerate((VOCAB, 128)):
                pe.wait_ge(amax_ready, n + 1)
                T.transpose(ps[3][0:1, 0:rows], tq[0:rows, 0:1], ident[0:rows, 0:rows]).then_inc(amax_t, 1)
                pe.wait_ge(qscale_ready, n + 1)
                T.matmul(ps[3][:, 256:257], lhsT=ones[0:1, :], rhs=tq[0:1, 2:3],
                         start=True, stop=True).then_inc(qscale_mm, 1)
            pe.wait_ge(rank2_ready, 1)
            for n, row in enumerate((z[0:1, 3, :], z[0:1, 4, :], ssm[0:1, 0, :], ssm[0:1, 1, :])):
                T.matmul(ps[0][:, 8 + n:9 + n], lhsT=row, rhs=ones[0:1, 0:1], start=True, stop=True)
            for n, (a, b) in enumerate(((12, 13), (13, 12), (14, 14))):
                last = T.matmul(ps[1][:, 128 * n:128 * n + 128], lhsT=z[:, a, :], rhs=z[:, b, :], start=True, stop=True)
            last.then_inc(ssm_mm, 1)
            pe.wait_ge(a_ready, 1)
            T.matmul(ps[2][:, 0:128], lhsT=a1t[:, :], rhs=a0[:, :], start=True, stop=True)
            T.matmul(ps[2][:, 128:256], lhsT=a0[:, :], rhs=a1t[:, :], start=True, stop=True)
            T.matmul(ps[2][:, 256:257], lhsT=a1t[:, :], rhs=bc[:, 0:1], start=True, stop=True).then_inc(ab_mm, 1)
            pe.wait_ge(v0_ready, 1)
            for k, (n, c) in enumerate(doublings):
                pe.wait_ge(power_ready, k)
                last = T.matmul(ps[k % 2][:, 0:c], lhsT=qw[:, k % 2, :], rhs=vm[:, 0:c], start=True, stop=True)
                if k < len(doublings) - 1:
                    T.matmul(ps[k % 2][:, 128:256], lhsT=qw[:, k % 2, :], rhs=pw[:, k % 2, :], start=True, stop=True)
                    last = T.matmul(ps[k % 2][:, 256:384], lhsT=pw[:, k % 2, :], rhs=qw[:, k % 2, :],
                                    start=True, stop=True)
                last.then_inc(power_mm, 1)
            pe.wait_ge(power_ready, len(doublings))
            T.matmul(ps[2][0:1, 0:SEQP], lhsT=bc[:, 1:2], rhs=vm[:, 0:SEQP], start=True, stop=True).then_inc(kern_mm, 1)
            pe.wait_ge(hk, 32)
            for a in range(2):
                last = T.matmul(ps[3][0:ROWS, SEQP * a:SEQP * a + SEQP], lhsT=cview(m, "rev", ROWS),
                                rhs=hank[:, a, :], start=True, stop=True)
            last.then_inc(toep_mm, 1)

        @block.vector
        def _(dve):
            V = nc.vector
            step = Steps(dve, own_step)
            dve.wait_ge(ld, 16 * len(loads))
            dve.wait_ge(scale_mm, 1)
            step(V.tensor_copy(psr[:, :], ps[0][:, 0:2]))
            step(V.tensor_scalar(npsr[:, :], psr[:, :], -1.0, None, ALU.mult))
            for g in range(2):
                sc = m.scaleq[:, g:g + 1]
                step(V.tensor_scalar(sc, psr[:, g:g + 1], 2.0, cview(m, "rows_p"), ALU.mult, ALU.mult))
                step(V.scalar_tensor_tensor(out=sc, in0=cview(m, "rows_s"), scalar=float(HD) ** -0.5, in1=sc,
                                            op0=ALU.mult, op1=ALU.add))
                step(V.tensor_tensor(sc, sc, row0, ALU.add))
                for k, es in ((0, m.esq), (1, m.esk)):
                    step(V.tensor_scalar(es[:, g, :], cview(m, "psel")[:, 128 * k:128 * k + 128],
                                         npsr[:, g:g + 1], None, ALU.mult))
            dve.wait_ge(bias_mm, 1)
            step(V.tensor_copy(m.rawq[:, :], ps[1][:, 0:2]))
            step(V.tensor_copy(m.rawk[:, :], ps[1][:, 2:4]))
            step(V.tensor_tensor(m.biasq[:, :], m.rawq[:, :], m.scaleq[:, :], ALU.mult))
            step(V.tensor_scalar(m.biasq[:, :], m.biasq[:, :], row1, None, ALU.add))
            step(V.tensor_scalar(m.biask[:, :], m.rawk[:, :], row0, None, ALU.add))
            dve.wait_ge(bv_mm, 1)
            step(V.tensor_copy(bvc[:, :], ps[2][:, 0:1]), bv_ready, 1)
            dve.wait_ge(bo_mm, 1)
            step(V.tensor_tensor(m.bo_row[:, :], borow[:, :], ps[2][0:1, 0:128], ALU.add))
            step(V.tensor_scalar(m.wq[:, :, :], m.wq[:, :, :], lng[:, 0:1], None, ALU.mult))
            step(V.tensor_scalar(m.wk[:, :, :], m.wk[:, :, :], lng[:, 0:1], None, ALU.mult))
            step(V.tensor_scalar(m.wv[:, :], m.wv[:, :], lng[:, 0:1], None, ALU.mult))
            step(V.tensor_scalar(m.sw2[:, :], m.sw2[:, :], 0.5, None, ALU.mult))
            step(V.tensor_scalar(m.wd[:, :, :, :], m.wd[:, :, :, :], 0.5, None, ALU.mult))
            step(V.tensor_scalar(m.outw[:, :], m.outw[:, :], 0.5, None, ALU.mult))
            step(V.tensor_copy(m.tri_bf[:, :], cview(m, "tri", ROWS)))
            step(V.memset(m.ones_bf[:, :], 1.0))
            step(V.memset(m.carry[:, :], 0.0))
            step(V.memset(m.carry2[:, :], 0.0))
            step(V.memset(m.hT[:, :, SEQ:SEQP], 0.0))
            for b in range(2):
                step(V.tensor_tensor(m.hT[:, b, 0:1], clsc[:, :], m.posT[:, 0:1], ALU.mult))
            for n, (w, rows, out, t) in enumerate(((emb, VOCAB, m.embt, tqe), (cw, 128, m.convq, tqc))):
                t = t[0:rows, :]
                step(V.tensor_reduce(tq[0:rows, 0:1], w[:, :], AX_X, ALU.max, apply_absolute_value=True),
                     amax_ready, n + 1)
                dve.wait_ge(amax_t, n + 1)
                step(V.tensor_reduce(tq[0:1, 1:2], ps[3][0:1, 0:rows], AX_X, ALU.max))
                step(V.tensor_scalar(tq[0:1, 2:3], tq[0:1, 1:2], 1.0 / 127.0, None, ALU.mult), qscale_ready, n + 1)
                dve.wait_ge(qscale_mm, n + 1)
                step(V.tensor_copy(tq[:, 3:4], ps[3][:, 256:257]))
                step(V.reciprocal(tq[:, 4:5], tq[:, 3:4]))
                step(V.tensor_scalar(t, w[:, :], tq[0:rows, 4:5], None, ALU.mult))
                step(V.tensor_scalar(t, t, ROUND, None, ALU.add))
                step(V.tensor_scalar(t, t, ROUND, None, ALU.subtract))
                step(V.scalar_tensor_tensor(out=t, in0=t, scalar=tq[0:rows, 3:4], in1=w[:, :],
                                            op0=ALU.mult, op1=ALU.subtract))
                step(V.tensor_tensor(out[:, :], w[:, :], t, ALU.add))

            def Z(n):
                return z[:, n, :]

            def S(n):
                return z1[:, n:n + 1]

            def tt(o, a, b, op):
                step(V.tensor_tensor(o, a, b, op))

            lr, li, pr, pi = (ssm[:, n, :] for n in range(4))
            dve.wait_ge(exp_done, 1)
            step(V.reciprocal(zc[:, 1:2], zc[:, 0:1]))
            step(V.tensor_scalar(zc[:, 1:2], zc[:, 1:2], 2.0, None, ALU.mult))
            step(V.tensor_scalar(Z(0), lr, -1.0, zc[0:2, 1:2], ALU.mult, ALU.add))
            tt(Z(1), Z(0), Z(0), ALU.mult)
            tt(Z(2), li, li, ALU.mult)
            tt(Z(1), Z(1), Z(2), ALU.add)
            step(V.reciprocal(Z(2), Z(1)))
            tt(Z(3), Z(0), Z(2), ALU.mult)
            tt(Z(4), li, Z(2), ALU.mult)
            dr, di = Z(3), Z(4)
            tt(Z(9), dr, pr, ALU.mult)
            tt(Z(10), di, pi, ALU.mult)
            tt(Z(5), Z(9), Z(10), ALU.subtract)
            tt(Z(7), Z(9), Z(10), ALU.add)
            tt(Z(9), dr, pi, ALU.mult)
            tt(Z(10), di, pr, ALU.mult)
            tt(Z(6), Z(9), Z(10), ALU.add)
            tt(Z(8), Z(10), Z(9), ALU.subtract)
            tt(Z(9), Z(7), pr, ALU.mult)
            tt(Z(10), Z(8), pi, ALU.mult)
            tt(Z(9), Z(9), Z(10), ALU.subtract)
            step(V.tensor_reduce(S(0), z[:, 9, 0:NST], AX_X, ALU.add))
            step(V.tensor_scalar(S(0), S(0), 1.0, None, ALU.add))
            tt(Z(9), Z(7), pi, ALU.mult)
            tt(Z(10), Z(8), pr, ALU.mult)
            tt(Z(9), Z(9), Z(10), ALU.add)
            step(V.tensor_reduce(S(1), z[:, 9, 0:NST], AX_X, ALU.add))
            tt(S(2), S(0), S(0), ALU.mult)
            tt(S(3), S(1), S(1), ALU.mult)
            tt(S(2), S(2), S(3), ALU.add)
            step(V.reciprocal(S(3), S(2)))
            tt(S(4), S(0), S(3), ALU.mult)
            step(V.scalar_tensor_tensor(out=S(5), in0=S(1), scalar=-1.0, in1=S(3), op0=ALU.mult, op1=ALU.mult))
            step(V.tensor_scalar(Z(11), Z(6), S(5), None, ALU.mult))
            step(V.scalar_tensor_tensor(out=Z(9), in0=Z(5), scalar=S(4), in1=Z(11), op0=ALU.mult, op1=ALU.subtract))
            step(V.tensor_scalar(Z(11), Z(6), S(4), None, ALU.mult))
            step(V.scalar_tensor_tensor(out=Z(10), in0=Z(5), scalar=S(5), in1=Z(11), op0=ALU.mult, op1=ALU.add))
            for o, re, im, sign in ((12, Z(9), Z(10), ALU.add), (13, Z(7), Z(8), ALU.subtract), (14, pr, pi, ALU.add)):
                tt(Z(15), cview(m, "mask_a", 2), re, ALU.mult)
                tt(Z(16), cview(m, "mask_b", 2), im, ALU.mult)
                if o < 14:
                    tt(Z(o), Z(15), Z(16), sign)
            step(V.tensor_tensor(Z(14), Z(15), Z(16), ALU.add), rank2_ready, 1)
            dve.wait_ge(ssm_mm, 1)
            step(V.tensor_copy(zc[:, 2:6], ps[0][:, 8:12]))
            tt(zc[:, 1:2], zc[:, 1:2], zc[:, 4:5], ALU.add)
            for n, (mat, re, im, off, sign) in enumerate((
                    (a1, 2, 3, 0, ALU.add), (a1t, 2, 3, 128, ALU.subtract),
                    (a0t, 1, 5, 256, ALU.subtract), (a0, 1, 5, 256, ALU.add))):
                step(V.tensor_scalar(tqe[:, :], cview(m, "jmat"), zc[:, im:im + 1], None, ALU.mult))
                step(V.scalar_tensor_tensor(out=mat[:, :], in0=ident, scalar=zc[:, re:re + 1], in1=tqe[:, :],
                                            op0=ALU.mult, op1=sign))
                if n < 3:
                    tt(mat[:, :], mat[:, :], ps[1][:, off:off + 128], ALU.subtract)
            step(V.tensor_tensor(a0[:, :], a0[:, :], ps[1][:, 256:384], ALU.subtract), a_ready, 1)
            dve.wait_ge(ab_mm, 1)
            step(V.tensor_copy(pw[:, 0, :], ps[2][:, 0:128]))
            step(V.tensor_copy(qw[:, 0, :], ps[2][:, 128:256]))
            step(V.tensor_scalar(bc[:, 1:2], bc[:, 1:2], cview(m, "csign"), None, ALU.mult))
            step(V.tensor_scalar(vm[:, 0:1], ps[2][:, 256:257], 2.0, None, ALU.mult), v0_ready, 1)
            for k, (n, c) in enumerate(doublings):
                dve.wait_ge(power_mm, k + 1)
                if k < len(doublings) - 1:
                    step(V.tensor_copy(pw[:, (k + 1) % 2, :], ps[k % 2][:, 128:256]))
                    step(V.tensor_copy(qw[:, (k + 1) % 2, :], ps[k % 2][:, 256:384]))
                step(V.tensor_copy(vm[:, n:n + c], ps[k % 2][:, 0:c]), power_ready, k + 1)
            dve.wait_ge(kern_mm, 1)
            step(V.tensor_copy(krow[:, :], ps[2][0:1, 0:SEQP]))
            step(V.tensor_tensor(krow[:, 0:1], krow[:, 0:1], dsc[:, :], ALU.add), kern_ready, 1)
            dve.wait_ge(toep_mm, 1)
            step(V.tensor_copy(m.toep[:, :, :].rearrange("p a n -> p (a n)"), ps[3][0:ROWS, 0:2 * SEQP]))
    nc.clear_and_free_semaphores(sems)
    nc.all_engine_barrier()


def patch_phase(nc, m, d, ctx):
    with ExitStack() as own:
        def sb(name, shape, dt=F32):
            return own.enter_context(nc.sbuf_tensor(name, shape, dt))

        def sem(name):
            return ctx.enter_context(nc.semaphore(name))

        NT = GB * NPATCH
        wtok, pat = m.wtok, m.pat
        ps = [own.enter_context(nc.psum_tensor(f"tok_ps{n}", [128, NT // 2], F32)) for n in range(2)]
        wl, loaded = m.wtok_loaded, m.patches_loaded
        mm = [sem(f"patches_mm{n}") for n in range(2)]
        out_ready = [sem(f"tokens_ready{n}") for n in range(2)]
        block = own.enter_context(nc.Block())

        @block.sync
        def _(sp):
            for n in range(2):
                sp.sem_inc(mm[n], 1)
                sp.sem_inc(out_ready[n], 1)
            with sp.Fori(2, GROUPS + 1) as i:
                for n in range(2):
                    sp.wait_ge(mm[n], i)
                    sp.dma_start(pat[n][:, :, :], d["xpat"][2 * i + (n - 2)]).then_inc(loaded[n], 16)

        @block.tensor
        def _(pe):
            pe.wait_ge(wl, 16)
            with pe.Fori(1, GROUPS + 1) as i:
                for n in range(2):
                    pe.wait_ge(loaded[n], 16 * i + 16)
                    pe.wait_ge(out_ready[n], i)
                    for k in range(KCH):
                        last = nc.tensor.matmul(ps[n][:, :], lhsT=wtok[:, k, :], rhs=pat[n][:, k, :],
                                                start=(k == 0), stop=(k == KCH - 1))
                    last.then_inc(mm[n], 1)

        @block.vector
        def _(dve):
            pos = m.posT[:, None, 1:1 + NPATCH].broadcast_to([128, GB // 2, NPATCH])
            with dve.Fori(1, GROUPS + 1) as i:
                for n in range(2):
                    dve.wait_ge(mm[n], i + 1)
                    dst = m.tok[:, bass.ds(i * NT + (n * (NT // 2) - NT), NT // 2)].rearrange("p (b t) -> p b t", b=GB // 2)
                    nc.vector.scalar_tensor_tensor(
                        out=dst, in0=ps[n][:, :].rearrange("p (b t) -> p b t", b=GB // 2),
                        scalar=m.tokb[:, 0:1], in1=pos, op0=ALU.add, op1=ALU.mult).then_inc(out_ready[n], 1)
    m.patch_memory.close()


def token_phase(nc, m, d, ctx):
    with ExitStack() as own:
        def sb(name, shape, dt=F32):
            return own.enter_context(nc.sbuf_tensor(name, shape, dt))

        def sem(name):
            return ctx.enter_context(nc.semaphore(name))

        ident, ones = cview(m, "ident"), cview(m, "ones")
        HALF = SEQP
        at = own.enter_context(nc.psum_tensor("scores", [128, 4, 512], F32))
        xb = own.enter_context(nc.psum_tensor("heads_out", [128, 512], F32))
        pb = own.enter_context(nc.psum_tensor("work", [128, 3, 512], F32))

        ybuf = sb("ybuf", [VOCAB, 2, NTEXT], I32)
        oh = sb("onehot", [VOCAB, 2, NTEXT + 1])
        cv = sb("conv", [128, 2, NTEXT])
        hT = m.hT
        h_sb = sb("h_sb", [ROWS, TILES, HID])
        st, mv = sb("stats", [ROWS, TILES, 6]), sb("meanvar", [ROWS, TILES, 2])
        vv, rs = sb("var_eps", [ROWS, TILES]), sb("rstd", [ROWS, TILES])
        st2, mv2 = sb("stats2", [ROWS, TILES, 6]), sb("meanvar2", [ROWS, TILES, 2])
        vv2, rs2 = sb("var_eps2", [ROWS, TILES]), sb("rstd2", [ROWS, TILES])
        nhalf = sb("nhalf", [ROWS, TILES])
        xh = sb("xh", [ROWS, TILES, HID]); xT = sb("xT", [128, COLS])
        sq = sb("squares", [128, 2, COLS])
        q_2 = [sb(f"q{n}", [128, 2, COLS]) for n in range(2)]
        k_2 = [sb(f"k{n}", [128, HEADS, COLS]) for n in range(2)]
        vx2 = [sb(f"v_ext{n}", [ROWS, TILES, HEADS, 32]) for n in range(2)]
        mx = sb("maxima", [ROWS, 2, 2, 2]); mp = sb("max_placed", [ROWS, 2, 2, 64])
        q2 = [sb(f"q_shifted{e}", [128, HALF]) for e in range(2)]
        pt = sb("probs", [ROWS, 4, 2 * HALF])
        osb2 = [sb(f"heads_sb{n}", [128, 2, COLS]) for n in range(2)]
        rsum = sb("recip_sums", [ROWS, TILES, HEADS]); on = sb("heads_norm", [ROWS, TILES, HEADS, HD])
        oT = sb("oT", [128, COLS]); h1 = sb("h1", [ROWS, TILES, HID])
        xf2 = [sb(f"xf{n}", [ROWS, TILES, HID]) for n in range(2)]; xfT = sb("xfT", [128, COLS])
        th = sb("tanh_g", [128, COLS]); hm = sb("hidden", [128, COLS])
        er = sb("router_exp", [ROWS, TILES, E1]); nu = sb("neg_inv_score", [ROWS, TILES, E1])
        tv, ti = sb("top_vals", [ROWS, TILES, 8]), sb("top_idx", [ROWS, TILES, 8], U32)
        sc, den = sb("top_scores", [ROWS, TILES, 2]), sb("score_sum", [ROWS, TILES])
        idf = sb("top_idx_f", [ROWS, 2, TILES])
        ohk = sb("chosen", [ROWS, 2, TILES, E1]); mk = sb("mask", [ROWS, TILES, E1], BF16)
        ap_, apb = sb("slot_of", [ROWS, TILES, E1]), sb("slot_in_cap", [ROWS, TILES, E1])
        slf = sb("slot_f", [ROWS, 2 * TILES]); sli = sb("slot_i", [ROWS, 2 * TILES], I32)

        y_loaded, oh_ready, emb_mm, cv_ready = sem("y_loaded"), sem("oh_ready"), sem("emb_mm"), sem("cv_ready")
        text_in, patches_in, h_mm, h_sb_ready = sem("text_in"), sem("patches_in"), sem("h_mm"), sem("h_sb_ready")
        var_ready, rs_ready, xh_ready, xT_mm = sem("var_ready"), sem("rs_ready"), sem("xh_ready"), sem("xT_mm")
        xT_ready, proj_mm, sq_ready, esum_mm = sem("xT_ready"), sem("proj_mm"), sem("sq_ready"), sem("esum_mm")
        qk_ready, v_mm, v_ready = sem("qk_ready"), sem("v_mm"), sem("v_ready")
        s_mm, m_ready, mT_mm, q2_ready = sem("s_mm"), sem("m_ready"), sem("mT_mm"), sem("q2_ready")
        st_mm, exp_ready, pv_mm, o_ready = sem("st_mm"), sem("exp_ready"), sem("pv_mm"), sem("o_ready")
        otm_mm, on_ready, oT_mm, oT_ready = sem("otm_mm"), sem("on_ready"), sem("oT_mm"), sem("oT_ready")
        ao_mm, h1_ready, var2_ready, rs2_ready = sem("ao_mm"), sem("h1_ready"), sem("var2_ready"), sem("rs2_ready")
        xf_ready, xfT_mm, xfT_ready, rt_mm = sem("xf_ready"), sem("xfT_mm"), sem("xfT_ready"), sem("rt_mm")
        gu_mm, er_ready, th_ready, hm_ready = sem("gu_mm"), sem("er_ready"), sem("th_ready"), sem("hm_ready")
        sh_mm, hres_ready, mk_ready, pos_mm = sem("sh_mm"), sem("hres_ready"), sem("mk_ready"), sem("pos_mm")
        slot_ready, scattered, rows_sent = sem("slot_ready"), sem("scattered"), sem("rows_sent")
        own_f, own_a, own_b, own_c = sem("dve_front"), sem("dve_att"), sem("dve_back"), sem("dve_routing")
        preset = sem("preset")
        block = own.enter_context(nc.Block())
        STEPS_F, STEPS_B, STEPS_C = 6, 6, 15

        ORDER = (0, 2, 1, 3)

        def passes(eng, body):
            body(1, ahead=True, front=True, back=False, routing=False)
            body(2, ahead=True, front=True, back=True, routing=False)
            with eng.Fori(1, (PAIRS - 4) // 2 + 1) as i:
                for n in range(2):
                    body(2 * i + (1 + n), ahead=True, front=True, back=True, routing=True, parity=(1 + n) % 2)
            body(PAIRS - 1, ahead=False, front=True, back=True, routing=True)
            body(PAIRS, ahead=False, front=False, back=True, routing=True)

        @block.sync
        def _(sp):
            for s in (oh_ready, emb_mm, cv_ready, text_in, patches_in, h_mm, h_sb_ready, var_ready, rs_ready,
                      xh_ready, xT_mm, xT_ready, v_mm, v_ready, otm_mm, on_ready, oT_mm, oT_ready, ao_mm,
                      h1_ready, var2_ready, rs2_ready, xf_ready, xfT_mm, xfT_ready, rt_mm, gu_mm, er_ready,
                      th_ready, hm_ready, sh_mm, hres_ready, mk_ready, pos_mm, slot_ready):
                sp.sem_inc(s, 1)
            for s in (qk_ready, proj_mm, sq_ready, esum_mm, pv_mm, o_ready):
                sp.sem_inc(s, 4)
            for s in (s_mm, m_ready, mT_mm, q2_ready, st_mm, exp_ready, own_a):
                sp.sem_inc(s, 8)
            sp.sem_inc(rows_sent, 2)
            sp.sem_inc(y_loaded, 16)
            sp.sem_inc(own_f, STEPS_F)
            sp.sem_inc(own_b, STEPS_B)
            sp.sem_inc(own_c, STEPS_C)
            with sp.Fori(1, PAIRS + 1) as i:
                sp.wait_ge(oh_ready, i)
                src = d["ytxt"][bass.ds(i - 1, 1), :].broadcast_to([VOCAB, 2 * NTEXT])
                sp.dma_start(ybuf[:, :, :].rearrange("p b t -> p (b t)"), src).then_inc(y_loaded, 16)

        @block.gpsimd
        def _(pool):
            nc.gpsimd.memset(oh[:, :, :], 0.0).then_inc(preset, 1)
            for n in range(2):
                nc.gpsimd.memset(vx2[n][:, :, :, :], 0.0).then_inc(preset, 1)
                nc.gpsimd.memset(k_2[n][:, :, :], 0.0).then_inc(preset, 1)
                nc.gpsimd.memset(q2[n][:, :], 0.0).then_inc(preset, 1)
            nc.gpsimd.memset(mp[:, :, :, :], 0.0).then_inc(preset, 1)
            nc.gpsimd.memset(nhalf[:, :], -0.5).then_inc(preset, 1)
            pool.wait_ge(preset, 9)
            for n in range(2):
                nc.gpsimd.memset(vx2[n][:, :, :, HD:HD + 1], 1.0).then_inc(preset, 1)
            pool.wait_ge(preset, 11)

            def patches(f):
                pool.wait_ge(h_mm, f)
                nc.gpsimd.tensor_copy(
                    hT[:, :, 1:1 + NPATCH],
                    m.tok[:, bass.ds(f * (2 * NPATCH) - 2 * NPATCH, 2 * NPATCH)].rearrange("p (b t) -> p b t", b=2)
                ).then_inc(patches_in, 1)

            def rstd(f):
                pool.wait_ge(var_ready, f + 1)
                nc.gpsimd.tensor_tensor(rs[:, :], vv[:, :], nhalf[:, :], ALU.pow).then_inc(rs_ready, 1)

            def rstd2(q):
                pool.wait_ge(var2_ready, q + 1)
                nc.gpsimd.tensor_tensor(rs2[:, :], vv2[:, :], nhalf[:, :], ALU.pow).then_inc(rs2_ready, 1)

            def send_rows(s, xf):
                pool.wait_ge(slot_ready, s + 1)
                pool.nop(nofuse=True)
                for n in range(2 * TILES):
                    nc.gpsimd.indirect_dma_start(
                        out=d["buf1"], out_offset=bass.IndirectOffsetOnAxis(ap=sli[:, n:n + 1], axis=0),
                        in_=xf[:, n % TILES, :], in_offset=None,
                        bounds_check=SLOTS1 - 1, oob_is_err=False).then_inc(scattered, 16)

            def rows_gone(s):
                pool.wait_ge(scattered, s * (16 * 2 * TILES))
                pool.sem_inc(rows_sent, 1)

            def body(r, ahead, front, back, routing, parity=None):
                p = r % 2 if parity is None else parity
                if front:
                    rstd(r + 1)
                if back:
                    rstd2(r - 1)
                if ahead:
                    patches(r + 2)
                if routing:
                    send_rows(r - 2, xf2[p])
                    rows_gone(r - 2)

            patches(1)
            rstd(1)
            patches(2)
            passes(pool, body)
            rstd2(PAIRS)
            send_rows(PAIRS - 1, xf2[(PAIRS - 1) % 2])
            rows_gone(PAIRS - 1)
            send_rows(PAIRS, xf2[PAIRS % 2])
            rows_gone(PAIRS)

        @block.tensor
        def _(pe):
            T = nc.tensor
            pe.wait_ge(preset, 11)

            def embed(f):
                pe.wait_ge(oh_ready, f + 1)
                T.matmul(pb[:, 2, 0:2 * (NTEXT + 1)], lhsT=m.embt[:, :],
                         rhs=oh[:, :, :].rearrange("p b t -> p (b t)"), start=True, stop=True).then_inc(emb_mm, 1)

            def tokens(f):
                pe.wait_ge(patches_in, f + 1)
                pe.wait_ge(text_in, f + 1)
                for j in range(TILES):
                    last = T.transpose(pb[0:ROWS, 2, HID * j:HID * j + HID],
                                       hT[:, j // 2, ROWS * (j % 2):ROWS * (j % 2) + ROWS], ident)
                last.then_inc(h_mm, 1)

            def normed(f):
                pe.wait_ge(xh_ready, f + 1)
                for j in range(TILES):
                    last = T.transpose(pb[:, 2, ROWS * j:ROWS * j + ROWS], xh[:, j, :], ident[0:ROWS, 0:ROWS])
                last.then_inc(xT_mm, 1)

            def project(f, k):
                pe.wait_ge(xT_ready, f + 1)
                pe.wait_ge(qk_ready, 4 * f + k)
                n = ORDER[k]
                w = (m.wq if n < 2 else m.wk)[:, n % 2, :]
                T.matmul(pb[:, 2, 0:COLS], lhsT=w, rhs=xT[:, :], start=True, stop=True).then_inc(proj_mm, 1)

            def add_squares(f, k):
                pe.wait_ge(sq_ready, 4 * f + (k + 1))
                n = ORDER[k]
                es = (m.esq if n < 2 else m.esk)[:, n % 2, :]
                T.matmul(pb[:, 2, 0:COLS], lhsT=es, rhs=sq[:, k % 2, :],
                         start=False, stop=True, skip_group_check=True).then_inc(esum_mm, 1)

            def values(f):
                for j in range(TILES):
                    last = T.matmul(pb[0:ROWS, 0, HID * j:HID * j + HID], lhsT=xT[:, ROWS * j:ROWS * j + ROWS],
                                    rhs=m.wv[:, :], start=True, stop=True)
                last.then_inc(v_mm, 1)

            def scores(r, u, hh, q_, k_):
                b, g = u // 2, u % 2
                for qt in range(2):
                    c = HALF * b + ROWS * qt
                    last = T.matmul(at[0:ROWS, hh, HALF * qt:HALF * qt + SEQ], lhsT=q_[:, g, c:c + ROWS],
                                    rhs=k_[:, 4 * g + hh, HALF * b:HALF * b + SEQ], start=True, stop=True)
                if hh % 2 == 1:
                    last.then_inc(s_mm, 1)

            def maxima(r, u, e):
                if e == 0:
                    pe.wait_ge(o_ready, 4 * r + u)
                pe.wait_ge(m_ready, 8 * r + (2 * u + e + 1))
                for qt in range(2):
                    last = T.matmul(xb[64 * e:64 * e + 64, 256 + ROWS * qt:256 + ROWS * qt + ROWS], lhsT=mp[:, e, qt, :],
                                    rhs=ident[0:ROWS, 0:ROWS], start=True, stop=True)
                last.then_inc(mT_mm, 1)

            def shifted_scores(r, u, e, k_):
                b, g = u // 2, u % 2
                pe.wait_ge(q2_ready, 8 * r + (2 * u + e + 1))
                for hh in (2 * e, 2 * e + 1):
                    for kt in range(2):
                        c = HALF * b + ROWS * kt
                        last = T.matmul(at[0:ROWS, hh, HALF * kt:HALF * kt + HALF],
                                        lhsT=k_[:, 4 * g + hh, c:c + ROWS], rhs=q2[e][:, :], start=True, stop=True)
                last.then_inc(st_mm, 1)

            def weighted_values(r, u, e, vx):
                b, g = u // 2, u % 2
                pe.wait_ge(exp_ready, 8 * r + (2 * u + e + 1))
                for hh in (2 * e, 2 * e + 1):
                    for kt in range(2):
                        n = ROWS - kt
                        last = T.matmul(xb[32 * hh:32 * hh + 32, 0:HALF],
                                        lhsT=vx[0:n, 2 * b + kt, 4 * g + hh, :],
                                        rhs=pt[0:n, hh, HALF * kt:HALF * kt + HALF],
                                        start=(kt == 0), stop=(kt == 1))
                if e == 1:
                    last.then_inc(pv_mm, 1)

            def heads_back(q, osb):
                pe.wait_ge(o_ready, 4 * q + 4)
                for j in range(TILES):
                    for g in range(2):
                        c = 256 * j + 128 * g
                        last = T.transpose(pb[0:ROWS, c // 512, c % 512:c % 512 + 128],
                                           osb[:, g, ROWS * j:ROWS * j + ROWS], ident)
                last.then_inc(otm_mm, 1)

            def heads_normed(q):
                pe.wait_ge(on_ready, q + 1)
                for j in range(TILES):
                    last = T.transpose(pb[:, 0, ROWS * j:ROWS * j + ROWS],
                                       on[:, j, :, :].rearrange("p h d -> p (h d)"), ident[0:ROWS, 0:ROWS])
                last.then_inc(oT_mm, 1)

            def attention_out(q):
                pe.wait_ge(oT_ready, q + 1)
                for j in range(TILES):
                    T.matmul(pb[0:ROWS, 1, HID * j:HID * j + HID], lhsT=oT[:, ROWS * j:ROWS * j + ROWS],
                             rhs=m.wo[:, :], start=True, stop=False)
                    last = T.matmul(pb[0:ROWS, 1, HID * j:HID * j + HID], lhsT=ones[0:1, 0:ROWS],
                                    rhs=m.bo_row[:, :], start=False, stop=True)
                last.then_inc(ao_mm, 1)

            def normed2(s, xf):
                pe.wait_ge(xf_ready, s + 1)
                for j in range(TILES):
                    last = T.transpose(pb[:, 0, ROWS * j:ROWS * j + ROWS], xf[:, j, :], ident[0:ROWS, 0:ROWS])
                last.then_inc(xfT_mm, 1)

            def router(s):
                pe.wait_ge(xfT_ready, s + 1)
                pe.wait_ge(h1_ready, s + 1)
                for j in range(TILES):
                    last = T.matmul(pb[0:ROWS, 1, E1 * j:E1 * j + E1], lhsT=xfT[:, ROWS * j:ROWS * j + ROWS],
                                    rhs=m.gatew[:, :], start=True, stop=True)
                last.then_inc(rt_mm, 1)

            def gate_up(s):
                pe.wait_ge(er_ready, s + 1)
                for n in range(2):
                    last = T.matmul(pb[:, n, 0:COLS], lhsT=m.sw13[:, 128 * n:128 * n + 128], rhs=xfT[:, :],
                                    start=True, stop=True)
                last.then_inc(gu_mm, 1)

            def shared_out(s):
                pe.wait_ge(hm_ready, s + 1)
                for j in range(TILES):
                    last = T.matmul(pb[0:ROWS, 0, HID * j:HID * j + HID], lhsT=hm[:, ROWS * j:ROWS * j + ROWS],
                                    rhs=m.sw2[:, :], start=True, stop=True)
                last.then_inc(sh_mm, 1)

            def positions(s):
                pe.wait_ge(mk_ready, s + 1)
                out = pb[0:ROWS, 1, 0:TILES * E1].rearrange("p (j e) -> p j e", j=TILES)
                T.matmul(out, lhsT=m.tri_bf[:, :], rhs=mk[:, :, :], start=True, stop=False)
                for j in range(TILES - 1):
                    T.matmul(out[:, j + 1:, :], lhsT=m.ones_bf[:, :],
                             rhs=mk[:, j:j + 1, :].broadcast_to([ROWS, TILES - 1 - j, E1]), start=False, stop=False)
                T.matmul(out, lhsT=ones[0:1, 0:ROWS],
                         rhs=m.carry[:, None, :].broadcast_to([1, TILES, E1]), start=False, stop=True)
                tot = pb[0:1, 1, TILES * E1:TILES * E1 + E1]
                for j in range(TILES):
                    T.matmul(tot, lhsT=m.ones_bf[:, 0:1], rhs=mk[:, j, :], start=(j == 0), stop=False)
                T.matmul(tot, lhsT=ones[0:1, 0:1], rhs=m.carry[:, :], start=False, stop=True).then_inc(pos_mm, 1)

            def body(r, ahead, front, back, routing, parity=None):
                p = r % 2 if parity is None else parity
                f, q, s = r + 1, r - 1, r - 2
                q_, k_, vx = q_2[p], k_2[p], vx2[p]
                for u in range(4):
                    if u < 2:
                        pe.wait_ge(qk_ready, 4 * r + (2 * u + 2))
                    scores(r, u, 0, q_, k_)
                    scores(r, u, 1, q_, k_)
                    if u > 0:
                        weighted_values(r, u - 1, 1, vx)
                    if u == 0:
                        add_squares(r, 2)
                    if u == 1 and front:
                        tokens(f)
                    if u == 2 and back:
                        if routing:
                            pe.wait_ge(hres_ready, s + 1)
                        heads_back(q, osb2[1 - p])
                    if u == 3 and front:
                        add_squares(f, 0)
                    if u == 3 and back:
                        if routing:
                            pe.wait_ge(slot_ready, s + 1)
                        attention_out(q)
                    scores(r, u, 2, q_, k_)
                    maxima(r, u, 0)
                    scores(r, u, 3, q_, k_)
                    if u == 0:
                        project(r, 3)
                    if u == 0 and routing:
                        normed2(s, xf2[p])
                    if u == 3 and front:
                        project(f, 1)
                    shifted_scores(r, u, 0, k_)
                    maxima(r, u, 1)
                    if u == 0 and routing:
                        router(s)
                    if u == 0:
                        add_squares(r, 3)
                    if u == 1 and routing:
                        shared_out(s)
                    if u == 2 and front:
                        normed(f)
                    if u == 3 and front:
                        add_squares(f, 1)
                        if back:
                            pe.wait_ge(oT_ready, q + 1)
                        values(f)
                    shifted_scores(r, u, 1, k_)
                    if u == 0 and routing:
                        gate_up(s)
                    if u == 0 and front:
                        pe.wait_ge(qk_ready, 4 * r + 4)
                        embed(f)
                    if u == 2 and back:
                        heads_normed(q)
                    if u == 2 and routing:
                        positions(s)
                    if u == 2 and front:
                        project(f, 0)
                    if u == 3 and front:
                        project(f, 2)
                    if u == 0:
                        pe.wait_ge(v_ready, r + 1)
                    weighted_values(r, u, 0, vx)
                weighted_values(r, 3, 1, vx)

            embed(1)
            tokens(1)
            normed(1)
            for k in range(3):
                project(1, k)
                if k < 2:
                    add_squares(1, k)
            values(1)
            passes(pe, body)
            last = PAIRS
            pe.wait_ge(h1_ready, last)
            normed2(last - 1, xf2[(last - 1) % 2])
            router(last - 1)
            gate_up(last - 1)
            shared_out(last - 1)
            positions(last - 1)
            pe.wait_ge(hres_ready, last)
            pe.wait_ge(slot_ready, last)
            heads_back(last, osb2[last % 2])
            heads_normed(last)
            attention_out(last)
            normed2(last, xf2[last % 2])
            router(last)
            gate_up(last)
            shared_out(last)
            positions(last)

        @block.scalar
        def _(act):
            A = nc.scalar
            act.wait_ge(preset, 11)

            def conv(f):
                act.wait_ge(emb_mm, f + 1)
                emb = pb[:, 2, 0:2 * (NTEXT + 1)].rearrange("p (b t) -> p b t", b=2)
                A.activation(cv[:, :, :], emb[:, :, 0:NTEXT], ACT.Copy, scale=m.convq[:, 0:1]).then_inc(cv_ready, 1)

            def tokens(f):
                act.wait_ge(h_mm, f + 1)
                A.activation(m.hres[:, bass.ds(f - 1, 1), :, :].rearrange("p a j c -> p (a j c)"), pb[0:ROWS, 2, :], ACT.Copy)
                A.activation(h_sb[:, :, :].rearrange("p j c -> p (j c)"), pb[0:ROWS, 2, :], ACT.Copy).then_inc(h_sb_ready, 1)

            def normed(f):
                act.wait_ge(xT_mm, f + 1)
                A.activation(xT[:, :], pb[:, 2, 0:COLS], ACT.Copy).then_inc(xT_ready, 1)

            def squares(f, k):
                n = ORDER[k]
                raw = (m.rawq if n < 2 else m.rawk)[:, n % 2:n % 2 + 1]
                act.wait_ge(proj_mm, 4 * f + (k + 1))
                A.activation(sq[:, k % 2, :], pb[:, 2, 0:COLS], ACT.Square, bias=raw).then_inc(sq_ready, 1)

            def projected(f, k, q_, k_):
                n = ORDER[k]
                act.wait_ge(esum_mm, 4 * f + (k + 1))
                if n < 2:
                    x = A.activation(q_[:, n, :], pb[:, 2, 0:COLS], ACT.Identity, bias=m.biasq[:, n:n + 1],
                                     scale=m.scaleq[:, n:n + 1])
                else:
                    for hh in range(4):
                        rows = slice(32 * hh, 32 * hh + 32)
                        x = A.activation(k_[rows, 4 * (n - 2) + hh, :], pb[rows, 2, 0:COLS], ACT.Identity,
                                         bias=m.biask[rows, n - 2:n - 1])
                x.then_inc(qk_ready, 1)

            def values(f, vx):
                act.wait_ge(v_mm, f + 1)
                A.activation(vx[:, :, :, 0:HD].rearrange("p j h d -> p (j h) d"),
                             pb[0:ROWS, 0, :].rearrange("p (n d) -> p n d", d=HD), ACT.Copy).then_inc(v_ready, 1)

            def probs(r, u, e):
                act.wait_ge(st_mm, 8 * r + (2 * u + e + 1))
                h = slice(2 * e, 2 * e + 2)
                A.activation(pt[:, h, :], at[0:ROWS, h, 0:2 * HALF], ACT.Exp).then_inc(exp_ready, 1)

            def heads(r, u, osb):
                b, g = u // 2, u % 2
                act.wait_ge(pv_mm, 4 * r + (u + 1))
                A.activation(osb[:, g, HALF * b:HALF * b + HALF], xb[:, 0:HALF], ACT.Copy).then_inc(o_ready, 1)

            def heads_normed(q):
                act.wait_ge(oT_mm, q + 1)
                A.activation(oT[:, :], pb[:, 0, 0:COLS], ACT.Copy).then_inc(oT_ready, 1)

            def normed2(s):
                act.wait_ge(xfT_mm, s + 1)
                A.activation(xfT[:, :], pb[:, 0, 0:COLS], ACT.Copy).then_inc(xfT_ready, 1)

            def router(s):
                act.wait_ge(rt_mm, s + 1)
                A.activation(er[:, :, :].rearrange("p j e -> p (j e)"), pb[0:ROWS, 1, 0:TILES * E1], ACT.Exp,
                             scale=-1.0).then_inc(er_ready, 1)

            def gate(s):
                act.wait_ge(gu_mm, s + 1)
                A.activation(th[:, :], pb[:, 0, 0:COLS], ACT.Tanh, scale=0.5).then_inc(th_ready, 1)

            def body(r, ahead, front, back, routing, parity=None):
                p = r % 2 if parity is None else parity
                f, q, s = r + 1, r - 1, r - 2
                for u in range(4):
                    if u > 0:
                        heads(r, u - 1, osb2[p])
                    if u == 0:
                        projected(r, 2, q_2[p], k_2[p])
                        squares(r, 3)
                    if u == 0 and routing:
                        normed2(s)
                    if u == 1 and front:
                        tokens(f)
                    if u == 3 and front:
                        projected(f, 0, q_2[1 - p], k_2[1 - p])
                        squares(f, 1)
                    probs(r, u, 0)
                    if u == 0 and routing:
                        router(s)
                    if u == 0:
                        projected(r, 3, q_2[p], k_2[p])
                    if u == 2 and front:
                        normed(f)
                    if u == 3 and front:
                        projected(f, 1, q_2[1 - p], k_2[1 - p])
                        values(f, vx2[1 - p])
                    probs(r, u, 1)
                    if u == 0 and routing:
                        gate(s)
                    if u == 0 and front:
                        conv(f)
                    if u == 2 and back:
                        heads_normed(q)
                    if u == 2 and front:
                        squares(f, 0)
                    if u == 3 and front:
                        squares(f, 2)
                heads(r, 3, osb2[p])

            conv(1)
            tokens(1)
            normed(1)
            for k in range(2):
                squares(1, k)
                projected(1, k, q_2[1], k_2[1])
            squares(1, 2)
            values(1, vx2[1])
            passes(act, body)
            normed2(PAIRS - 1)
            router(PAIRS - 1)
            gate(PAIRS - 1)
            heads_normed(PAIRS)
            normed2(PAIRS)
            router(PAIRS)
            gate(PAIRS)

        @block.vector
        def _(dve):
            V = nc.vector
            flat = lambda t: t[:, :, :].rearrange("p j c -> p (j c)")

            def variance(step, x, st, mv):
                for j in range(TILES):
                    ins = V.bn_stats(st[:, j, :], x[:, j, :])
                step(ins)
                V.tensor_tensor(mv[:, :, 0], st[:, :, 1], st[:, :, 4], ALU.add)
                step(V.tensor_tensor(mv[:, :, 1], st[:, :, 1], st[:, :, 4], ALU.subtract))
                V.tensor_scalar(mv[:, :, 0], mv[:, :, 0], 0.5, None, ALU.mult)
                step(V.scalar_tensor_tensor(out=mv[:, :, 1], in0=mv[:, :, 1], scalar=HID / 4.0, in1=mv[:, :, 1],
                                            op0=ALU.mult, op1=ALU.mult))
                step(V.tensor_tensor(mv[:, :, 1], mv[:, :, 1], st[:, :, 2], ALU.add))
                step(V.tensor_tensor(mv[:, :, 1], mv[:, :, 1], st[:, :, 5], ALU.add))

            def one_hot(step, f):
                dve.wait_ge(y_loaded, 16 * f + 16)
                dve.wait_ge(emb_mm, f)
                step(V.tensor_scalar(oh[:, :, 1:], ybuf[:, :, :], float(VOCAB - 1), cview(m, "vocab", VOCAB),
                                     ALU.min, ALU.is_equal), oh_ready, f + 1)

            def text(step, f):
                dve.wait_ge(cv_ready, f + 1)
                emb = pb[:, 2, 0:2 * (NTEXT + 1)].rearrange("p (b t) -> p b t", b=2)
                step(V.scalar_tensor_tensor(out=cv[:, :, :], in0=emb[:, :, 1:], scalar=m.convq[:, 1:2],
                                            in1=cv[:, :, :], op0=ALU.mult, op1=ALU.add))
                dve.wait_ge(h_mm, f)
                step(V.tensor_scalar(hT[:, :, 1 + NPATCH:SEQ], cv[:, :, :], 0.0, None, ALU.max), text_in, f + 1)

            def statistics(step, f):
                dve.wait_ge(h_sb_ready, f + 1)
                variance(step, h_sb, st, mv)
                step(V.tensor_scalar(vv[:, :], mv[:, :, 1], (1.0 + EPS) / HID, EPS * EPS, ALU.mult, ALU.add),
                     var_ready, f + 1)

            def normed(step, f):
                dve.wait_ge(rs_ready, f + 1)
                for j in range(TILES):
                    x = V.tensor_scalar(xh[:, j, :], h_sb[:, j, :], mv[:, j, 0:1],
                                        rs[:, j:j + 1], ALU.subtract, ALU.mult)
                step(x, xh_ready, f + 1)

            def maxima(r, u, e):
                step = Steps(dve, own_a, 8 * r + (2 * u + e))
                dve.wait_ge(s_mm, 8 * r + (2 * u + e + 1))
                sview = at[0:ROWS, 2 * e:2 * e + 2, 0:2 * HALF].rearrange("p h (t k) -> p h t k", t=2)[:, :, :, 0:SEQ]
                step(V.tensor_reduce(mx[:, e, :, :], sview, AX_X, ALU.max))
                step(V.tensor_scalar(mp[:, e, :, :].rearrange("p t (h r) -> p h t r", r=32)[:, :, :, 0],
                                     mx[:, e, :, :], -1.0, None, ALU.mult), m_ready, 8 * r + (2 * u + e + 1))

            def shifted(r, u, e, q_):
                b, g = u // 2, u % 2
                k = slice(64 * e, 64 * e + 64)
                dve.wait_ge(mT_mm, 8 * r + (2 * u + e + 1))
                V.tensor_tensor(q2[e][k, :], q_[k, g, HALF * b:HALF * b + HALF], xb[k, 256:256 + HALF],
                                ALU.add).then_inc(q2_ready, 1)

            def heads_normed(step, q):
                dve.wait_ge(otm_mm, q + 1)
                heads = pb[0:ROWS, 0:2, :].rearrange("p a c -> p (a c)").rearrange("p (n r) -> p n r", r=32)
                step(V.reciprocal(rsum[:, :, :].rearrange("p j h -> p (j h)"), heads[:, :, HD]))
                step(V.tensor_tensor(on[:, :, :, :].rearrange("p j h d -> p (j h) d"), heads[:, :, 0:HD],
                                     rsum[:, :, :].rearrange("p j h -> p (j h)")[:, :, None].broadcast_to(
                                         [ROWS, TILES * HEADS, HD]), ALU.mult), on_ready, q + 1)

            def residual(step, q):
                dve.wait_ge(ao_mm, q + 1)
                step(V.tensor_tensor(flat(h1), m.hres[:, bass.ds(q - 1, 1), :, :].rearrange("p a j c -> p (a j c)"),
                                     pb[0:ROWS, 1, :], ALU.add), h1_ready, q + 1)

            def statistics2(step, q):
                variance(step, h1, st2, mv2)
                step(V.tensor_scalar(vv2[:, :], mv2[:, :, 1], 1.0 / HID, EPS, ALU.mult, ALU.add), var2_ready, q + 1)

            def normed2(step, q, xf):
                dve.wait_ge(rs2_ready, q + 1)
                dve.wait_ge(rows_sent, q)
                for j in range(TILES):
                    x = V.tensor_scalar(xf[:, j, :], h1[:, j, :], mv2[:, j, 0:1], rs2[:, j:j + 1],
                                        ALU.subtract, ALU.mult)
                step(x, xf_ready, q + 1)

            def hidden(step, s):
                dve.wait_ge(th_ready, s + 1)
                step(V.scalar_tensor_tensor(out=th[:, :], in0=th[:, :], scalar=1.0, in1=pb[:, 0, 0:COLS],
                                            op0=ALU.add, op1=ALU.mult))
                step(V.tensor_tensor(hm[:, :], th[:, :], pb[:, 1, 0:COLS], ALU.mult), hm_ready, s + 1)

            def best(step, s):
                dve.wait_ge(er_ready, s + 1)
                step(V.tensor_scalar(nu[:, :, :], er[:, :, :], -1.0, -1.0, ALU.mult, ALU.add))
                dve.nop(nofuse=True)
                for j in range(TILES):
                    x = V.max(tv[:, j, :], nu[:, j, :])
                step(x)
                dve.nop(nofuse=True)
                for j in range(TILES):
                    x = V.max_index(ti[:, j, :], tv[:, j, :], nu[:, j, :])
                step(x)

            def chosen(step, s):
                step(V.tensor_tensor(idf[:, :, :].rearrange("p k j -> p j k"), ti[:, :, 0:2],
                                     cview(m, "padbig", ROWS).rearrange("p (k j) -> p j k", k=2), ALU.add))
                step(V.tensor_tensor(
                    ohk[:, :, :, :].rearrange("p k j e -> p (k j) e"),
                    cview(m, "iota64", ROWS)[:, None, :].broadcast_to([ROWS, 2 * TILES, E1]),
                    idf[:, :, :].rearrange("p k j -> p (k j)")[:, :, None].broadcast_to([ROWS, 2 * TILES, E1]),
                    ALU.is_equal))
                step(V.tensor_tensor(mk[:, :, :], ohk[:, 0, :, :], ohk[:, 1, :, :], ALU.add), mk_ready, s + 1)

            def weights(step, s):
                step(V.reciprocal(sc[:, :, :], tv[:, :, 0:2]))
                step(V.tensor_tensor(den[:, :], sc[:, :, 0], sc[:, :, 1], ALU.add))
                step(V.tensor_scalar(den[:, :], den[:, :], -1e-20, None, ALU.add))
                step(V.reciprocal(den[:, :], den[:, :]))
                w = m.wts1[:, bass.ds(s - 1, 1), :].rearrange("p a (k j) -> p (a k) j", k=2)
                step(V.scalar_tensor_tensor(out=w, in0=sc[:, :, :].rearrange("p j k -> p k j"), scalar=ROUTE_SCALE,
                                            in1=den[:, None, :].broadcast_to([ROWS, 2, TILES]),
                                            op0=ALU.mult, op1=ALU.mult))

            def shared_out(step, s):
                dve.wait_ge(sh_mm, s + 1)
                step(V.tensor_tensor(m.hres[:, bass.ds(s - 1, 1), :, :].rearrange("p a j c -> p (a j c)"), flat(h1),
                                     pb[0:ROWS, 0, :], ALU.add), hres_ready, s + 1)

            def slots(step, s):
                dve.wait_ge(pos_mm, s + 1)
                pos = pb[0:ROWS, 1, 0:TILES * E1].rearrange("p (j e) -> p j e", j=TILES)
                V.tensor_copy(m.carry[:, :], pb[0:1, 1, TILES * E1:TILES * E1 + E1])
                step(V.tensor_tensor(ap_[:, :, :], pos,
                                     cview(m, "eoff1", ROWS)[:, None, :].broadcast_to([ROWS, TILES, E1]), ALU.add))
                step(V.scalar_tensor_tensor(out=apb[:, :, :], in0=pos, scalar=float(CAP), in1=ap_[:, :, :],
                                            op0=ALU.is_lt, op1=ALU.mult))
                step(V.tensor_tensor(ohk[:, :, :, :], ohk[:, :, :, :],
                                     apb[:, None, :, :].broadcast_to([ROWS, 2, TILES, E1]), ALU.mult))
                step(V.tensor_reduce(slf[:, :], ohk[:, :, :, :].rearrange("p k j e -> p (k j) e"), AX_X, ALU.add))
                dve.wait_ge(rows_sent, s + 1)
                V.tensor_scalar(m.slots1[:, bass.ds(s - 1, 1), :].rearrange("p a n -> p (a n)"), slf[:, :],
                                float(SLOTS1), None, ALU.add)
                step(V.tensor_scalar(sli[:, :], slf[:, :], float(SLOTS1), None, ALU.add), slot_ready, s + 1)

            def body(r, ahead, front, back, routing, parity=None):
                p = r % 2 if parity is None else parity
                f, q, s = r + 1, r - 1, r - 2
                front_step = Steps(dve, own_f, STEPS_F * f)
                back_step = Steps(dve, own_b, STEPS_B * q)
                routing_step = Steps(dve, own_c, STEPS_C * s)
                for u in range(4):
                    maxima(r, u, 0)
                    if u == 0 and routing:
                        normed2(routing_step, s, xf2[p])
                    if u == 1 and routing:
                        hidden(routing_step, s)
                    if u == 2 and front:
                        normed(front_step, f)
                    shifted(r, u, 0, q_2[p])
                    maxima(r, u, 1)
                    if u == 0 and front:
                        one_hot(front_step, f)
                    shifted(r, u, 1, q_2[p])
                    if u == 2 and back:
                        heads_normed(back_step, q)
                    if u == 0 and routing:
                        best(routing_step, s)
                    if u == 0 and front:
                        text(front_step, f)
                    if u == 1 and front:
                        statistics(front_step, f)
                    if u == 1 and routing:
                        shared_out(routing_step, s)
                    if u == 1 and routing:
                        chosen(routing_step, s)
                    if u == 2 and routing:
                        slots(routing_step, s)
                    if u == 3 and routing:
                        weights(routing_step, s)
                    if u == 3 and back:
                        residual(back_step, q)
                        statistics2(back_step, q)
                assert not front or front_step.n == STEPS_F, front_step.n
                assert not back or back_step.n == STEPS_B, back_step.n
                assert not routing or routing_step.n == STEPS_C, routing_step.n

            def routed(s):
                step = Steps(dve, own_c, STEPS_C * s)
                normed2(step, s, xf2[s % 2])
                hidden(step, s)
                best(step, s)
                chosen(step, s)
                shared_out(step, s)
                slots(step, s)
                weights(step, s)

            dve.wait_ge(preset, 11)
            step = Steps(dve, own_f, STEPS_F)
            one_hot(step, 1)
            text(step, 1)
            statistics(step, 1)
            normed(step, 1)
            passes(dve, body)
            routed(PAIRS - 1)
            step = Steps(dve, own_b, STEPS_B * PAIRS)
            heads_normed(step, PAIRS)
            residual(step, PAIRS)
            statistics2(step, PAIRS)
            routed(PAIRS)




def expert_phase(nc, m, d, ctx):
    with ExitStack() as own:
        def sb(name, shape, dt=F32):
            return own.enter_context(nc.sbuf_tensor(name, shape, dt))

        def sem(name):
            return ctx.enter_context(nc.semaphore("x_" + name))

        WAYS = 4
        ways, two = range(WAYS), range(2)
        N = E1 // WAYS
        ident = cview(m, "ident")
        rows = [sb(f"x_rows{p}", [128, WAYS, 2, HID]) for p in two]
        w13 = [sb(f"x_w13_{p}", [128, WAYS, 2 * EH]) for p in two]
        w2 = [sb(f"x_w2_{p}", [EH, WAYS, HID]) for p in two]
        ys = [sb(f"x_out{p}", [128, WAYS, 2, HID]) for p in two]
        xT = [sb(f"x_rows_T{n}", [128, CAP]) for n in ways]
        th = [sb(f"x_tanh{n}", [EH, CAP]) for n in ways]
        hh = [sb(f"x_hidden{n}", [EH, CAP]) for n in ways]
        gps = [own.enter_context(nc.psum_tensor(f"x_gu_ps{n}", [128, 2, CAP], F32)) for n in ways]
        tps = [own.enter_context(nc.psum_tensor(f"x_ty_ps{n}", [128, 4, 128], F32)) for n in ways]
        loaded, stored = [sem(f"loaded{p}") for p in two], [sem(f"stored{p}") for p in two]
        wgu_loaded = sem("wgu_loaded")
        t_mm, xT_ready, gu_mm, th_ready = sem("t_mm"), sem("xT_ready"), sem("gu_mm"), sem("th_ready")
        a_ready, h_ready, y_mm, y_ready = sem("a_ready"), sem("h_ready"), sem("y_mm"), sem("y_ready")
        block = own.enter_context(nc.Block())

        @block.sync
        def _(sp):
            for s in (t_mm, xT_ready, gu_mm, th_ready, a_ready, h_ready, y_mm, y_ready):
                sp.sem_inc(s, WAYS)
            for p in two:
                sp.sem_inc(stored[p], 16)

            def load(r, p):
                src = d["buf1"][bass.ds(r * (WAYS * CAP) - WAYS * CAP, WAYS * CAP), :]
                sp.dma_start(rows[p][:, :, :, :].rearrange("p n a c -> p (n a) c"),
                             src.rearrange("(b p) c -> p b c", p=128)).then_inc(loaded[p], 16)
                sp.dma_start(w13[p][:, :, :], d["w13"][bass.ds(r * WAYS - WAYS, WAYS), :, :].rearrange("n k c -> k n c")
                             ).then_inc(loaded[p], 16)
                sp.dma_start(w2[p][:, :, :], d["w2"][bass.ds(r * WAYS - WAYS, WAYS), :, :].rearrange("n k c -> k n c")
                             ).then_inc(loaded[p], 16)

            load(1, 0)
            load(2, 1)
            sp.dma_start(m.tok[:, 0:E2 * 2 * EH2], d["wgu"].rearrange("p e c -> p (e c)")).then_inc(wgu_loaded, 16)
            with sp.Fori(1, N // 2) as i:
                for p in two:
                    r = 2 * i + (p + 1)
                    sp.wait_ge(y_mm, WAYS * r - WAYS)
                    load(r, p)
            sp.wait_ge(wgu_loaded, 16)

        @block.tensor
        def _(pe):
            T = nc.tensor
            with pe.Fori(1, N // 2 + 1) as i:
                for p in two:
                    r = 2 * i + (p - 1)
                    pe.wait_ge(loaded[p], 48 * i)
                    for n in ways:
                        pe.wait_ge(y_ready, WAYS * r + (n + 1 - WAYS))
                        for a in range(2):
                            last = T.transpose(tps[n][:, a, :], rows[p][:, n, a, :], ident)
                        last.then_inc(t_mm, 1)
                    for n in ways:
                        pe.wait_ge(xT_ready, WAYS * r + (n + 1))
                        pe.wait_ge(h_ready, WAYS * r + (n + 1 - WAYS))
                        for k in range(2):
                            last = T.matmul(gps[n][0:EH, k, :], lhsT=w13[p][:, n, EH * k:EH * k + EH], rhs=xT[n][:, :],
                                            start=True, stop=True)
                        last.then_inc(gu_mm, 1)
                    for n in ways:
                        pe.wait_ge(h_ready, WAYS * r + (n + 1))
                        for a in range(2):
                            last = T.matmul(tps[n][:, 2 + a, :], lhsT=hh[n][:, 128 * a:128 * a + 128],
                                            rhs=w2[p][:, n, :], start=True, stop=True)
                        last.then_inc(y_mm, 1)

        @block.scalar
        def _(act):
            A = nc.scalar
            with act.Fori(1, N // 2 + 1) as i:
                for p in two:
                    r = 2 * i + (p - 1)
                    for n in ways:
                        act.wait_ge(t_mm, WAYS * r + (n + 1))
                        A.activation(xT[n][:, :], tps[n][:, 0:2, :].rearrange("p a c -> p (a c)"), ACT.Copy
                                     ).then_inc(xT_ready, 1)
                    for n in ways:
                        act.wait_ge(gu_mm, WAYS * r + (n + 1))
                        A.activation(th[n][:, :], gps[n][0:EH, 0, :], ACT.Tanh, scale=0.5).then_inc(th_ready, 1)
                    act.wait_ge(stored[p], 16 * i)
                    for n in ways:
                        act.wait_ge(y_mm, WAYS * r + (n + 1))
                        A.activation(ys[p][:, n, :, :], tps[n][:, 2:4, :], ACT.Copy).then_inc(y_ready, 1)
                    act.wait_ge(y_ready, WAYS * r + WAYS)
                    dst = d["y1"][bass.ds(r * (WAYS * CAP) - WAYS * CAP, WAYS * CAP), :].rearrange("(b p) c -> p b c", p=128)
                    act.dma_start(dst, ys[p][:, :, :, :].rearrange("p n a c -> p (n a) c")).then_inc(stored[p], 16)
            for p in two:
                act.wait_ge(stored[p], 16 * (N // 2 + 1))

        @block.vector
        def _(dve):
            V = nc.vector
            with dve.Fori(1, N + 1) as r:
                for n in ways:
                    dve.wait_ge(th_ready, WAYS * r + (n + 1))
                    V.scalar_tensor_tensor(out=th[n][:, :], in0=th[n][:, :], scalar=1.0, in1=gps[n][0:EH, 0, :],
                                           op0=ALU.add, op1=ALU.mult).then_inc(a_ready, 1)
                    dve.wait_ge(a_ready, WAYS * r + (n + 1))
                    V.scalar_tensor_tensor(out=hh[n][:, :], in0=th[n][:, :], scalar=0.5, in1=gps[n][0:EH, 1, :],
                                           op0=ALU.mult, op1=ALU.mult).then_inc(h_ready, 1)


def ssm_phase(nc, m, d, ctx):
    with ExitStack() as own:
        def sb(name, shape, dt=F32):
            return own.enter_context(nc.sbuf_tensor(name, shape, dt))

        def sem(name):
            return ctx.enter_context(nc.semaphore("s_" + name))

        ident, ones = cview(m, "ident"), cview(m, "ones")
        conv_ps, tr_ps, lg_ps, pos_ps = (own.enter_context(nc.psum_tensor("s_" + k, [128, 512], F32))
                                         for k in ("conv_ps", "tr_ps", "lg_ps", "pos_ps"))
        out_ps = own.enter_context(nc.psum_tensor("s_out_ps", [128, 2, 512], F32))
        NK = 2 * TILES
        sl2 = [sb(f"s_slots{n}", [ROWS, NK], I32) for n in range(2)]; wt = sb("s_wts", [ROWS, NK])
        ga2 = [sb(f"s_gathered{n}", [ROWS, NK, HID]) for n in range(2)]; h = sb("s_h", [ROWS, TILES, HID])
        st, mv = sb("s_stats", [ROWS, TILES, 6]), sb("s_meanvar", [ROWS, TILES, 2])
        st2, mv2 = sb("s_stats2", [ROWS, TILES, 6]), sb("s_meanvar2", [ROWS, TILES, 2])
        vv, rs, nhalf = sb("s_var", [ROWS, 2, TILES]), sb("s_rstd", [ROWS, 2, TILES]), sb("s_nhalf", [ROWS, 2, TILES])
        vv2, rs2 = sb("s_var2", [ROWS, TILES]), sb("s_rstd2", [ROWS, TILES])
        hsc, hbi = sb("s_skip_scale", [ROWS, TILES]), sb("s_skip_bias", [ROWS, TILES])
        hs, xn = sb("s_skip", [ROWS, TILES, HID]), sb("s_xn", [ROWS, TILES, HID])
        wcol, biasc = sb("s_norm_w", [128, 1]), sb("s_bias_conv", [128, SEQP])
        y, y2, gl = sb("s_y", [128, COLS]), sb("s_y2", [128, COLS]), sb("s_gelu", [128, COLS])
        tg, h4 = sb("s_gate", [ROWS, TILES, HID]), sb("s_h4", [ROWS, TILES, HID])
        xg2 = [sb(f"s_xg{n}", [ROWS, TILES, HID]) for n in range(2)]
        xgT = sb("s_xgT", [128, COLS])
        lg = sb("s_logits", [ROWS, TILES, E2]); tv = sb("s_top", [ROWS, TILES, 8])
        ti = sb("s_top_i", [ROWS, TILES, 8], U32); idf = sb("s_top_f", [ROWS, 2, TILES])
        df, ex, wk = sb("s_diff", [ROWS, TILES]), sb("s_exp", [ROWS, TILES]), sb("s_w", [ROWS, 2, TILES])
        ohk = sb("s_chosen", [ROWS, 2, TILES, E2]); mk = sb("s_mask", [ROWS, TILES, E2], BF16)
        so = sb("s_slot_of", [ROWS, TILES, E2]); slf = sb("s_slot_f", [ROWS, NK]); sli = sb("s_slot_i", [ROWS, NK], I32)

        preset, comb, idx_in = sem("preset"), sem("comb"), sem("idx_in")
        gathered = [sem(f"gathered{n}") for n in range(2)]
        const_mm, const_ready = sem("const_mm"), sem("const_ready")
        var_ready, rs_ready, xn_ready = sem("var_ready"), sem("rs_ready"), sem("xn_ready")
        skip_ready, hs_ready, conv_mm, sq_ready = sem("skip_ready"), sem("hs_ready"), sem("conv_mm"), sem("sq_ready")
        y_ready, in_ready, tanh_ready, gl_ready = sem("y_ready"), sem("in_ready"), sem("tanh_ready"), sem("gl_ready")
        out_mm, gate_ready, h4_ready, kept = sem("out_mm"), sem("gate_ready"), sem("h4_ready"), sem("kept")
        var2_ready, rs2_ready = sem("var2_ready"), sem("rs2_ready")
        xg_ready, xgT_mm, xgT_ready, rt_mm = sem("xg_ready"), sem("xgT_mm"), sem("xgT_ready"), sem("rt_mm")
        lg_ready, df_ready, ex_ready, mk_ready = sem("lg_ready"), sem("df_ready"), sem("ex_ready"), sem("mk_ready")
        pos_mm, slot_ready, scattered, rows_sent = sem("pos_mm"), sem("slot_ready"), sem("scattered"), sem("rows_sent")
        own_x, own_y, own_r = sem("dve_next"), sem("dve_layer"), sem("dve_routing")
        wt_in = sem("wt_in")
        block = own.enter_context(nc.Block())
        STEPS_X, STEPS_Y, STEPS_R = 7, 7, 11
        C0, C1 = 0.7978845608028654, 0.7978845608028654 * 0.044715

        def passes(eng, body):
            body(1, following=True, last=False, turn=1)
            with eng.Fori(1, (PAIRS - 2) // 2 + 1) as i:
                for n in range(2):
                    body(2 * i + n, following=True, last=True, parity=n, turn=i + 1)
            body(PAIRS, following=False, last=True)

        @block.sync
        def _(sp):
            for s in (comb, idx_in, var_ready, rs_ready, xn_ready, skip_ready, hs_ready, conv_mm, sq_ready, y_ready,
                      in_ready, tanh_ready, gl_ready, out_mm, gate_ready, h4_ready, kept, var2_ready, rs2_ready,
                      xg_ready, xgT_mm, xgT_ready, rt_mm, lg_ready, df_ready, ex_ready, mk_ready, pos_mm,
                      slot_ready, wt_in):
                sp.sem_inc(s, 1)
            sp.sem_inc(rows_sent, 2)
            sp.sem_inc(own_x, STEPS_X)
            sp.sem_inc(own_y, STEPS_Y)
            sp.sem_inc(own_r, STEPS_R)

        @block.gpsimd
        def _(pool):
            nc.gpsimd.memset(nhalf[:, :, :], -0.5).then_inc(preset, 1)
            pool.wait_ge(preset, 1)

            def gather(f, p):
                sl, ga = sl2[p], ga2[p]
                nc.gpsimd.tensor_copy(sl[:, :], m.slots1[:, bass.ds(f - 1, 1), :].rearrange("p a n -> p (a n)")).then_inc(idx_in, 1)
                pool.wait_ge(idx_in, f + 1)
                pool.nop(nofuse=True)
                for n in range(NK):
                    nc.gpsimd.indirect_dma_start(
                        out=ga[:, n, :], out_offset=None, in_=d["y1"],
                        in_offset=bass.IndirectOffsetOnAxis(ap=sl[:, n:n + 1], axis=0)).then_inc(gathered[p], 16)

            def rstd(f):
                pool.wait_ge(var_ready, f + 1)
                nc.gpsimd.tensor_tensor(rs[:, :, :], vv[:, :, :], nhalf[:, :, :], ALU.pow).then_inc(rs_ready, 1)

            def rstd2(r):
                pool.wait_ge(var2_ready, r + 1)
                nc.gpsimd.tensor_tensor(rs2[:, :], vv2[:, :], nhalf[:, 0, :], ALU.pow).then_inc(rs2_ready, 1)

            def send_rows(s, xg):
                pool.wait_ge(slot_ready, s + 1)
                pool.nop(nofuse=True)
                for n in range(NK):
                    nc.gpsimd.indirect_dma_start(
                        out=d["buf2"], out_offset=bass.IndirectOffsetOnAxis(ap=sli[:, n:n + 1], axis=0),
                        in_=xg[:, n % TILES, :], in_offset=None,
                        bounds_check=SLOTS2 - 1, oob_is_err=False).then_inc(scattered, 16)

            def rows_gone(s):
                pool.wait_ge(scattered, s * (16 * NK))
                pool.sem_inc(rows_sent, 1)

            gather(1, 1)
            gather(2, 0)
            rstd(1)
            pool.wait_ge(comb, 1 + 1)
            gather(3, 1)
            rstd(2)
            rstd2(1)
            pool.wait_ge(comb, 2 + 1)
            gather(4, 0)
            rstd(3)
            send_rows(1, xg2[1])
            with pool.Fori(1, (PAIRS - 4) // 2 + 1) as i:
                for n in range(2):
                    r = 2 * i + (1 + n)
                    rstd2(r - 1)
                    pool.wait_ge(comb, r + 1)
                    gather(r + 2, 1 - n)
                    rows_gone(r - 2)
                    rstd(r + 1)
                    send_rows(r - 1, xg2[n])
            rstd2(PAIRS - 2)
            rows_gone(PAIRS - 3)
            rstd(PAIRS)
            send_rows(PAIRS - 2, xg2[(PAIRS - 2) % 2])
            rows_gone(PAIRS - 2)
            rstd2(PAIRS - 1)
            send_rows(PAIRS - 1, xg2[(PAIRS - 1) % 2])
            rows_gone(PAIRS - 1)
            rstd2(PAIRS)
            send_rows(PAIRS, xg2[PAIRS % 2])
            rows_gone(PAIRS)

        @block.tensor
        def _(pe):
            T = nc.tensor

            def over_time(ps, c, first, second):
                T.matmul(ps[:, c:c + SEQP], lhsT=first, rhs=m.toep[:, 0, :], start=True, stop=False)
                return T.matmul(ps[:, c + ROWS:c + SEQP], lhsT=second,
                                rhs=m.toep[0:ROWS - 1, 1, ROWS:], start=False, stop=True)

            over_time(tr_ps, 0, m.normb[:, :], m.normb[0:ROWS - 1, :])
            T.matmul(tr_ps[:, 256:257], lhsT=m.normw[0:1, :], rhs=ones[0:1, 0:1], start=True, stop=True).then_inc(const_mm, 1)
            pe.wait_ge(const_ready, 1)

            def layer(r):
                pe.wait_ge(xn_ready, r + 1)
                pe.wait_ge(y_ready, r)
                for b in range(2):
                    last = over_time(conv_ps, SEQP * b, xn[:, 2 * b, :], xn[0:ROWS - 1, 2 * b + 1, :])
                last.then_inc(conv_mm, 1)

            def router(s, xg):
                pe.wait_ge(xg_ready, s + 1)
                pe.wait_ge(xgT_ready, s)
                for j in range(TILES):
                    last = T.transpose(tr_ps[:, ROWS * j:ROWS * j + ROWS], xg[:, j, :], ident[0:ROWS, 0:ROWS])
                last.then_inc(xgT_mm, 1)
                pe.wait_ge(xgT_ready, s + 1)
                pe.wait_ge(lg_ready, s)
                for j in range(TILES):
                    last = T.matmul(lg_ps[0:ROWS, E2 * j:E2 * j + E2], lhsT=xgT[:, ROWS * j:ROWS * j + ROWS],
                                    rhs=m.rtw[:, :], start=True, stop=True)
                last.then_inc(rt_mm, 1)

            def project(r, tiles):
                if tiles[0] == 0:
                    pe.wait_ge(gl_ready, r + 1)
                    pe.wait_ge(h4_ready, r)
                for j in tiles:
                    o = out_ps[0:ROWS, j // 2, 256 * (j % 2):256 * (j % 2) + 256]
                    T.matmul(o, lhsT=gl[:, ROWS * j:ROWS * j + ROWS], rhs=m.outw[:, :], start=True, stop=False)
                    last = T.matmul(o, lhsT=ones[0:1, 0:ROWS], rhs=m.outb[:, :], start=False, stop=True)
                if tiles[-1] == TILES - 1:
                    last.then_inc(out_mm, 1)

            def positions(s):
                pe.wait_ge(mk_ready, s + 1)
                pe.wait_ge(slot_ready, s)
                out = pos_ps[0:ROWS, 0:TILES * E2].rearrange("p (j e) -> p j e", j=TILES)
                T.matmul(out, lhsT=m.tri_bf[:, :], rhs=mk[:, :, :], start=True, stop=False)
                for j in range(TILES - 1):
                    T.matmul(out[:, j + 1:, :], lhsT=m.ones_bf[:, :],
                             rhs=mk[:, j:j + 1, :].broadcast_to([ROWS, TILES - 1 - j, E2]), start=False, stop=False)
                T.matmul(out, lhsT=ones[0:1, 0:ROWS],
                         rhs=m.carry2[:, None, :].broadcast_to([1, TILES, E2]), start=False, stop=True)
                tot = pos_ps[0:1, TILES * E2:TILES * E2 + E2]
                for j in range(TILES):
                    T.matmul(tot, lhsT=m.ones_bf[:, 0:1], rhs=mk[:, j, :], start=(j == 0), stop=False)
                T.matmul(tot, lhsT=ones[0:1, 0:1], rhs=m.carry2[:, :], start=False, stop=True).then_inc(pos_mm, 1)

            def body(r, following, last, parity=None, turn=None):
                p = r % 2 if parity is None else parity
                layer(r)
                if last:
                    router(r - 1, xg2[1 - p])
                project(r, (0, 1))
                if last:
                    positions(r - 1)
                project(r, (2, 3))

            passes(pe, body)
            router(PAIRS, xg2[PAIRS % 2])
            positions(PAIRS)

        @block.scalar
        def _(act):
            A = nc.scalar

            def skip(f):
                act.wait_ge(skip_ready, f + 1)
                for j in range(TILES):
                    x = A.activation(hs[:, j, :], h[:, j, :], ACT.Identity, bias=hbi[:, j:j + 1], scale=hsc[:, j:j + 1])
                x.then_inc(hs_ready, 1)

            def transposed(s):
                act.wait_ge(xgT_mm, s + 1)
                A.activation(xgT[:, :], tr_ps[:, 0:COLS], ACT.Copy).then_inc(xgT_ready, 1)

            def logits(s):
                act.wait_ge(rt_mm, s + 1)
                A.activation(lg[:, :, :].rearrange("p j e -> p (j e)"), lg_ps[0:ROWS, 0:TILES * E2], ACT.Copy
                             ).then_inc(lg_ready, 1)

            def second_over_first(s):
                act.wait_ge(df_ready, s + 1)
                A.activation(ex[:, :], df[:, :], ACT.Exp).then_inc(ex_ready, 1)

            def body(r, following, last, parity=None, turn=None):
                act.wait_ge(y_ready, r + 1)
                A.activation(y2[:, :], y[:, :], ACT.Square).then_inc(sq_ready, 1)
                act.wait_ge(in_ready, r + 1)
                A.activation(y2[:, :], y2[:, :], ACT.Tanh).then_inc(tanh_ready, 1)
                if last:
                    transposed(r - 1)
                    logits(r - 1)
                    second_over_first(r - 1)
                act.wait_ge(out_mm, r + 1)
                z = out_ps[0:ROWS, :, :].rearrange("p a (j c) -> p (a j) c", j=2)
                A.activation(tg[:, :, :], z[:, :, HID:], ACT.Tanh, scale=0.5).then_inc(gate_ready, 1)
                act.wait_ge(h4_ready, r + 1)
                A.activation(m.hres[:, bass.ds(r - 1, 1), :, :].rearrange("p a j c -> p (a j c)"),
                             h4[:, :, :].rearrange("p j c -> p (j c)"), ACT.Copy).then_inc(kept, 1)
                if following:
                    skip(r + 1)

            skip(1)
            passes(act, body)
            transposed(PAIRS)
            logits(PAIRS)
            second_over_first(PAIRS)

        @block.vector
        def _(dve):
            V = nc.vector
            flat = lambda t: t[:, :, :].rearrange("p j c -> p (j c)")

            def variance(step, x, st, mv):
                for j in range(TILES):
                    ins = V.bn_stats(st[:, j, :], x[:, j, :])
                step(ins)
                V.tensor_tensor(mv[:, :, 0], st[:, :, 1], st[:, :, 4], ALU.add)
                step(V.tensor_tensor(mv[:, :, 1], st[:, :, 1], st[:, :, 4], ALU.subtract))
                V.tensor_scalar(mv[:, :, 0], mv[:, :, 0], 0.5, None, ALU.mult)
                step(V.scalar_tensor_tensor(out=mv[:, :, 1], in0=mv[:, :, 1], scalar=HID / 4.0, in1=mv[:, :, 1],
                                            op0=ALU.mult, op1=ALU.mult))
                step(V.tensor_tensor(mv[:, :, 1], mv[:, :, 1], st[:, :, 2], ALU.add))
                step(V.tensor_tensor(mv[:, :, 1], mv[:, :, 1], st[:, :, 5], ALU.add))

            def combine(step, f, k, p, turn):
                ga = ga2[p]
                if k == 0:
                    step(V.tensor_scalar(wt[:, :], m.wts1[:, bass.ds(f - 1, 1), :].rearrange("p a n -> p (a n)"), 1.0,
                                         None, ALU.mult), wt_in, f + 1)
                    dve.wait_ge(gathered[p], turn * (16 * NK))
                    dve.wait_ge(hs_ready, f)
                for j in range(TILES):
                    n = TILES * k + j
                    base = m.hres[:, bass.ds(f - 1, 1), j, :].rearrange("p a c -> p (a c)") if k == 0 else h[:, j, :]
                    x = V.scalar_tensor_tensor(out=h[:, j, :], in0=ga[:, n, :], scalar=wt[:, n:n + 1], in1=base,
                                               op0=ALU.mult, op1=ALU.add)
                if k == 0:
                    step(x)
                else:
                    step(x, comb, f + 1)

            def statistics(step, f):
                variance(step, h, st, mv)
                V.tensor_scalar(vv[:, 0, :], mv[:, :, 1], 1.0 / HID, EPS, ALU.mult, ALU.add)
                step(V.tensor_scalar(vv[:, 1, :], mv[:, :, 1], (1.0 + EPS) / HID, EPS * EPS, ALU.mult, ALU.add),
                     var_ready, f + 1)

            def normed(step, f):
                dve.wait_ge(rs_ready, f + 1)
                step(V.scalar_tensor_tensor(out=hbi[:, :], in0=mv[:, :, 0], scalar=-1.0, in1=rs[:, 0, :],
                                            op0=ALU.mult, op1=ALU.mult))
                step(V.tensor_scalar(hsc[:, :], rs[:, 0, :], 1.0, None, ALU.add), skip_ready, f + 1)
                dve.wait_ge(conv_mm, f)
                for j in range(TILES):
                    x = V.tensor_scalar(xn[:, j, :], h[:, j, :], mv[:, j, 0:1], rs[:, 1, j:j + 1],
                                        ALU.subtract, ALU.mult)
                step(x, xn_ready, f + 1)

            def layer_out(r):
                dve.wait_ge(conv_mm, r + 1)
                V.scalar_tensor_tensor(
                    out=y[:, :].rearrange("p (b t) -> p b t", b=2),
                    in0=conv_ps[:, 0:COLS].rearrange("p (b t) -> p b t", b=2), scalar=wcol[:, 0:1],
                    in1=biasc[:, None, :].broadcast_to([128, 2, SEQP]), op0=ALU.mult, op1=ALU.add).then_inc(y_ready, 1)

            def gelu_in(step, r):
                dve.wait_ge(sq_ready, r + 1)
                step(V.tensor_scalar(y2[:, :], y2[:, :], C1, C0, ALU.mult, ALU.add))
                step(V.tensor_tensor(y2[:, :], y2[:, :], y[:, :], ALU.mult), in_ready, r + 1)

            def gelu(step, r):
                dve.wait_ge(tanh_ready, r + 1)
                step(V.scalar_tensor_tensor(out=gl[:, :], in0=y2[:, :], scalar=1.0, in1=y[:, :],
                                            op0=ALU.add, op1=ALU.mult), gl_ready, r + 1)

            def gated(step, r):
                dve.wait_ge(gate_ready, r + 1)
                dve.wait_ge(hs_ready, r + 1)
                dve.wait_ge(kept, r)
                z = out_ps[0:ROWS, :, :].rearrange("p a (j c) -> p (a j) c", j=2)
                step(V.scalar_tensor_tensor(out=tg[:, :, :], in0=tg[:, :, :], scalar=1.0, in1=z[:, :, 0:HID],
                                            op0=ALU.add, op1=ALU.mult))
                step(V.scalar_tensor_tensor(out=flat(h4), in0=flat(tg), scalar=0.5, in1=flat(hs), op0=ALU.mult,
                                            op1=ALU.add), h4_ready, r + 1)
                variance(step, h4, st2, mv2)
                step(V.tensor_scalar(vv2[:, :], mv2[:, :, 1], 1.0 / HID, EPS, ALU.mult, ALU.add), var2_ready, r + 1)

            def normed2(step, r, xg):
                dve.wait_ge(rs2_ready, r + 1)
                dve.wait_ge(rows_sent, r)
                for j in range(TILES):
                    x = V.tensor_scalar(xg[:, j, :], h4[:, j, :], mv2[:, j, 0:1], rs2[:, j:j + 1],
                                        ALU.subtract, ALU.mult)
                step(x, xg_ready, r + 1)

            def best(step, s):
                dve.wait_ge(lg_ready, s + 1)
                dve.nop(nofuse=True)
                for j in range(TILES):
                    x = V.max(tv[:, j, :], lg[:, j, :])
                step(x)
                dve.nop(nofuse=True)
                for j in range(TILES):
                    x = V.max_index(ti[:, j, :], tv[:, j, :], lg[:, j, :])
                step(x)
                step(V.tensor_tensor(df[:, :], tv[:, :, 1], tv[:, :, 0], ALU.subtract), df_ready, s + 1)
                step(V.tensor_tensor(idf[:, :, :].rearrange("p k j -> p j k"), ti[:, :, 0:2],
                                     cview(m, "padbig", ROWS).rearrange("p (k j) -> p j k", k=2), ALU.add))
                step(V.tensor_tensor(
                    ohk[:, :, :, :].rearrange("p k j e -> p (k j) e"),
                    cview(m, "iota64", ROWS)[:, None, 0:E2].broadcast_to([ROWS, NK, E2]),
                    idf[:, :, :].rearrange("p k j -> p (k j)")[:, :, None].broadcast_to([ROWS, NK, E2]),
                    ALU.is_equal))
                step(V.tensor_tensor(mk[:, :, :], ohk[:, 0, :, :], ohk[:, 1, :, :], ALU.add), mk_ready, s + 1)

            def weights(step, s):
                dve.wait_ge(ex_ready, s + 1)
                step(V.tensor_scalar(wk[:, 1, :], ex[:, :], 1.0, None, ALU.add))
                step(V.reciprocal(wk[:, 0, :], wk[:, 1, :]))
                step(V.tensor_tensor(wk[:, 1, :], wk[:, 0, :], ex[:, :], ALU.mult))
                step(V.tensor_scalar(m.wts2[:, bass.ds(s - 1, 1), :].rearrange("p a n -> p (a n)"),
                                     wk[:, :, :].rearrange("p k j -> p (k j)"), 1.0, None, ALU.mult))

            def slots(step, s):
                dve.wait_ge(pos_mm, s + 1)
                pos = pos_ps[0:ROWS, 0:TILES * E2].rearrange("p (j e) -> p j e", j=TILES)
                V.tensor_copy(m.carry2[:, :], pos_ps[0:1, TILES * E2:TILES * E2 + E2])
                step(V.tensor_tensor(so[:, :, :], pos,
                                     cview(m, "eoff2", ROWS)[:, None, :].broadcast_to([ROWS, TILES, E2]), ALU.add))
                for k in range(2):
                    x = V.tensor_tensor(ohk[:, k, :, :], ohk[:, k, :, :], so[:, :, :], ALU.mult)
                step(x)
                step(V.tensor_reduce(slf[:, :], ohk[:, :, :, :].rearrange("p k j e -> p (k j) e"), AX_X, ALU.add))
                dve.wait_ge(rows_sent, s + 1)
                V.tensor_scalar(m.slots2[:, bass.ds(s - 1, 1), :].rearrange("p a n -> p (a n)"), slf[:, :],
                                float(SLOTS2), None, ALU.add)
                step(V.tensor_scalar(sli[:, :], slf[:, :], float(SLOTS2), None, ALU.add), slot_ready, s + 1)

            def body(r, following, last, parity=None, turn=None):
                p = r % 2 if parity is None else parity
                f, s = r + 1, r - 1
                next_step = Steps(dve, own_x, STEPS_X * f)
                step = Steps(dve, own_y, STEPS_Y * r)
                routing_step = Steps(dve, own_r, STEPS_R * s)
                layer_out(r)
                gelu_in(step, r)
                if last:
                    normed2(routing_step, s, xg2[1 - p])
                gelu(step, r)
                if following:
                    combine(next_step, f, 0, 1 - p, turn)
                if last:
                    best(routing_step, s)
                if following:
                    combine(next_step, f, 1, 1 - p, turn)
                    statistics(next_step, f)
                if last:
                    slots(routing_step, s)
                if following:
                    normed(next_step, f)
                if last:
                    weights(routing_step, s)
                gated(step, r)
                assert not following or next_step.n == STEPS_X, next_step.n
                assert step.n == STEPS_Y, step.n
                assert not last or routing_step.n == STEPS_R, routing_step.n

            dve.wait_ge(preset, 1)
            dve.wait_ge(const_mm, 1)
            V.tensor_copy(biasc[:, :], tr_ps[:, 0:SEQP])
            V.tensor_copy(wcol[:, :], tr_ps[:, 256:257]).then_inc(const_ready, 1)
            dve.wait_ge(const_ready, 1)
            step = Steps(dve, own_x, STEPS_X)
            combine(step, 1, 0, 1, 1)
            combine(step, 1, 1, 1, 1)
            statistics(step, 1)
            normed(step, 1)
            passes(dve, body)
            step = Steps(dve, own_r, STEPS_R * PAIRS)
            normed2(step, PAIRS, xg2[PAIRS % 2])
            best(step, PAIRS)
            slots(step, PAIRS)
            weights(step, PAIRS)


def mixture_phase(nc, m, d, ctx):
    with ExitStack() as own:
        def sb(name, shape, dt=F32):
            return own.enter_context(nc.sbuf_tensor(name, shape, dt))

        WAYS = 4
        ways = range(WAYS)

        def sem(name):
            return ctx.enter_context(nc.semaphore("t_" + name))

        def sems(name):
            return [sem(f"{name}{n}") for n in ways]

        ident = cview(m, "ident")
        nt, se, be, lo = sb("t_tiles", [1, E2]), sb("t_start", [1, E2]), sb("t_base", [1, E2]), sb("t_lower", [1, E2, E2])
        big, big2 = sb("t_big", [1, MT2, E2]), sb("t_big2", [1, MT2, E2])
        fe, fr, ff, fw = (sb(f"t_f{n}", [1, MT2]) for n in range(4))
        tabe, tabr = (sb(f"t_tab{n}", [1, MT2], I32) for n in range(2))
        mv, dl, dls = sb("t_firsts", [1, E2 + 1]), sb("t_moves", [1, E2 + 1]), sb("t_moves_all", [ROWS, E2 + 1])
        slf, acc, mov = (sb(f"t_slots{n}", [ROWS, PAIRS * 2 * TILES]) for n in range(3))
        zb, zi, zt = sb("t_tail_f", [1, E2]), sb("t_tail", [1, E2], I32), sb("t_zeros", [128, HID])
        xr = [sb(f"t_rows{n}", [128, HID]) for n in ways]; xT = [sb(f"t_xT{n}", [128, 128]) for n in ways]
        th = [sb(f"t_tanh{n}", [128, EH2]) for n in ways]; hh = [sb(f"t_hid{n}", [128, EH2]) for n in ways]
        hT = [sb(f"t_hidT{n}", [128, 2, 128]) for n in ways]; ys = sb("t_out", [128, WAYS, HID])
        gps = [own.enter_context(nc.psum_tensor(f"t_gu{n}", [128, 2, EH2], F32)) for n in ways]
        tps = [own.enter_context(nc.psum_tensor(f"t_tr{n}", [128, 4, 128], F32)) for n in ways]
        moves_mm, moves_ready, own_p = sem("moves_mm"), sem("moves_ready"), sem("pool")
        own_t, table_ready, zeroed, tails = sem("dve"), sem("table_ready"), sem("zeroed"), sem("tails")
        loaded, t_mm, xT_ready, gu_mm = sems("loaded"), sem("t_mm"), sem("xT_ready"), sem("gu_mm")
        th_ready, a_ready, h_ready, hT_mm = sem("th_ready"), sem("a_ready"), sem("h_ready"), sem("hT_mm")
        hT_ready, y_mm, y_ready, stored = sem("hT_ready"), sem("y_mm"), sem("y_ready"), sem("stored")
        hT1_ready = sem("hT1_ready")
        block = own.enter_context(nc.Block())
        N = MT2 // WAYS

        def hT_of(i, n):
            return (hT1_ready, 2 * i + n) if n in (1, 2) else (hT_ready, 2 * i + (1 if n == 0 else 2))

        @block.gpsimd
        def _(pool):
            nc.gpsimd.memset(zt[:, :], 0.0).then_inc(zeroed, 1)
            pool.wait_ge(moves_ready, 1)
            step = Steps(pool, own_p)
            all_slots = m.slots2[:, :, :].rearrange("p a n -> p (a n)")
            step(nc.gpsimd.tensor_copy(slf[:, :], all_slots))
            step(nc.gpsimd.tensor_scalar(acc[:, :], slf[:, :], dls[:, 0:1], None, ALU.add))
            for e in range(1, E2 + 1):
                step(nc.gpsimd.tensor_scalar(mov[:, :], slf[:, :], float(REG2 * e), dls[:, e:e + 1], ALU.is_ge, ALU.mult))
                step(nc.gpsimd.tensor_tensor(acc[:, :], acc[:, :], mov[:, :], ALU.add))
            step(nc.gpsimd.tensor_copy(all_slots, acc[:, :]))

        @block.sync
        def _(sp):
            for s in (t_mm, xT_ready, gu_mm, th_ready, a_ready, h_ready, hT_mm, y_mm, y_ready):
                sp.sem_inc(s, WAYS)
            for s in (hT_ready, hT1_ready):
                sp.sem_inc(s, 2)
            sp.sem_inc(stored, 16)
            sp.wait_ge(zeroed, 1)
            sp.wait_ge(table_ready, 1)
            for e in range(E2):
                at = sp.value_load(zi[0:1, e:e + 1], min_val=0, max_val=SLOTS2 - 128)
                sp.dma_start(d["buf2"][bass.ds(at, 128), :], zt[:, :]).then_inc(tails, 16)
            sp.wait_ge(tails, 16 * E2)

            def store(i):
                sp.wait_ge(y_ready, WAYS * i + WAYS)
                dst = d["y2"][bass.ds(i * (WAYS * 128) - WAYS * 128, WAYS * 128), :].rearrange("(n p) c -> p n c", p=128)
                sp.dma_start(dst, ys[:, :, :]).then_inc(stored, 16)

            def load(i):
                for n in ways:
                    sp.wait_ge(t_mm, WAYS * i + (n + 1 - WAYS))
                    at = sp.value_load(tabr[0:1, bass.ds(WAYS * i + (n - WAYS), 1)], min_val=0, max_val=SLOTS2)
                    sp.dma_start(xr[n][:, :], d["buf2"][bass.ds(at, 128), :]).then_inc(loaded[n], 16)

            load(1)
            load(2)
            with sp.Fori(3, N + 1) as i:
                load(i)
                store(i - 2)
            store(N - 1)
            store(N)
            sp.wait_ge(stored, 16 * (N + 1))

        @block.tensor
        def _(pe):
            T = nc.tensor
            pe.wait_ge(table_ready, 1)
            T.matmul(tps[0][0:ROWS, 0, 0:E2 + 1], lhsT=cview(m, "ones")[0:1, 0:ROWS], rhs=dl[:, :],
                     start=True, stop=True).then_inc(moves_mm, 1)
            pe.wait_ge(moves_ready, 1)

            def transpose_rows(i, n):
                pe.wait_ge(loaded[n], 16 * i)
                T.transpose(tps[n][:, 0, :], xr[n][:, :], ident).then_inc(t_mm, 1)

            def gate_up(i, n, expert):
                pe.wait_ge(xT_ready, WAYS * i + (n + 1))
                T.matmul(gps[n][:, :, :].rearrange("p a c -> p (a c)"), lhsT=xT[n][:, :],
                         rhs=m.tok[:, bass.ds(expert * (2 * EH2), 2 * EH2)],
                         start=True, stop=True).then_inc(gu_mm, 1)

            def transpose_hidden(i, n):
                pe.wait_ge(h_ready, WAYS * i + (n + 1))
                pe.wait_ge(y_ready, WAYS * i + (n + 1 - WAYS))
                for c in range(2):
                    last = T.transpose(tps[n][:, 1 + c, :], hh[n][:, 128 * c:128 * c + 128], ident)
                last.then_inc(hT_mm, 1)

            def down(i, n, expert):
                for c in range(2):
                    last = T.matmul(tps[n][:, 3, :], lhsT=hT[n][:, c, :],
                                    rhs=m.wd[:, bass.ds(expert, 1), c, :].rearrange("p a c -> p (a c)"),
                                    start=(c == 0), stop=(c == 1))
                last.then_inc(y_mm, 1)

            def expert_of(i, n):
                return pe.value_load(tabe[0:1, bass.ds(WAYS * i + (n - WAYS), 1)], min_val=0, max_val=E2 - 1)

            def batch(i, further, first=None, ahead=False):
                experts = [expert_of(i, 0) if first is None else first]
                following = None
                for n in ways:
                    if n > 0:
                        experts.append(expert_of(i, n))
                    if n == 3:
                        transpose_hidden(i, 0)
                    gate_up(i, n, experts[n])
                for n in (1, 2):
                    transpose_hidden(i, n)
                for n in range(3):
                    pe.wait_ge(*hT_of(i, n))
                    if further:
                        transpose_rows(i + 1, n)
                transpose_hidden(i, 3)
                for n in ways:
                    if n == 2:
                        pe.wait_ge(*hT_of(i, 3))
                        if further:
                            transpose_rows(i + 1, 3)
                    if further:
                        pe.wait_ge(xT_ready, WAYS * i + (n + 1 + WAYS))
                    if n == 1 and ahead:
                        following = expert_of(i + 1, 0)
                    down(i, n, experts[n])
                return following

            for n in ways:
                transpose_rows(1, n)
            assert N % 2 == 1
            with pe.Fori(1, N // 2 + 1) as k:
                following = batch(2 * k - 1, further=True, ahead=True)
                batch(2 * k, further=True, first=following)
            batch(N, further=False)

        @block.scalar
        def _(act):
            A = nc.scalar
            act.wait_ge(table_ready, 1)

            def rows_in(i, n):
                act.wait_ge(t_mm, WAYS * i + (n + 1))
                A.activation(xT[n][:, :], tps[n][:, 0, :], ACT.Copy).then_inc(xT_ready, 1)

            def gate(i, n):
                act.wait_ge(gu_mm, WAYS * i + (n + 1))
                A.activation(th[n][:, :], gps[n][:, 0, :], ACT.Tanh, scale=0.5).then_inc(th_ready, 1)

            def results(i, n):
                act.wait_ge(y_mm, WAYS * i + (n + 1))
                A.activation(ys[:, n, :], tps[n][:, 3, :], ACT.Copy).then_inc(y_ready, 1)

            def batch(i, further):
                for n in ways:
                    gate(i, n)
                for n in (1, 2):
                    act.wait_ge(hT_mm, WAYS * i + (n + 1))
                    A.activation(hT[n][:, :, :], tps[n][:, 1:3, :], ACT.Copy).then_inc(hT1_ready, 1)
                if further:
                    for n in range(3):
                        rows_in(i + 1, n)
                act.wait_ge(stored, 16 * i)
                for n in ways:
                    if n == 2 and further:
                        rows_in(i + 1, 3)
                    results(i, n)

            for n in ways:
                rows_in(1, n)
            with act.Fori(1, N) as i:
                batch(i, further=True)
            batch(N, further=False)

        @block.vector
        def _(dve):
            V = nc.vector
            step = Steps(dve, own_t)
            step(V.tensor_copy(lo[:, :, :], cview(m, "lower8", 1).rearrange("p (a b) -> p a b", a=E2)))
            step(V.tensor_scalar(nt[:, :], m.carry2[:, :], 1.0 / 128, 127.0 / 256, ALU.mult, ALU.add))
            step(V.tensor_scalar(nt[:, :], nt[:, :], ROUND, None, ALU.add))
            step(V.tensor_scalar(nt[:, :], nt[:, :], ROUND, None, ALU.subtract))
            step(V.tensor_tensor(lo[:, :, :], lo[:, :, :], nt[:, None, :].broadcast_to([1, E2, E2]), ALU.mult))
            step(V.tensor_reduce(se[:, :], lo[:, :, :], AX_X, ALU.add))
            step(V.scalar_tensor_tensor(out=be[:, :], in0=se[:, :], scalar=-128.0, in1=cview(m, "eoff2", 1),
                                        op0=ALU.mult, op1=ALU.add))
            step(V.tensor_tensor(nt[:, :], nt[:, :], se[:, :], ALU.add))
            index = cview(m, "tile_index", 1)
            wide = lambda t: t[:, :, None].broadcast_to([1, MT2, E2])
            each = lambda t: t[:, None, :].broadcast_to([1, MT2, E2])
            step(V.tensor_tensor(big[:, :, :], each(nt[:, :]), wide(index), ALU.is_le))
            step(V.tensor_reduce(fe[:, :], big[:, :, :], AX_X, ALU.add))
            step(V.tensor_tensor(big[:, :, :], each(cview(m, "iota64", 1)[:, 0:E2]), wide(fe[:, :]), ALU.is_equal))
            step(V.tensor_reduce(ff[:, :], big[:, :, :], AX_X, ALU.add))
            step(V.tensor_tensor(big2[:, :, :], big[:, :, :], each(be[:, :]), ALU.mult))
            step(V.tensor_reduce(fr[:, :], big2[:, :, :], AX_X, ALU.add))
            step(V.tensor_tensor(fw[:, :], ff[:, :], index, ALU.mult))
            step(V.scalar_tensor_tensor(out=fr[:, :], in0=fw[:, :], scalar=128.0, in1=fr[:, :], op0=ALU.mult, op1=ALU.add))
            step(V.tensor_scalar(tabr[:, :], fr[:, :], float(SLOTS2), None, ALU.add))
            step(V.tensor_scalar(mv[:, 0:E2], se[:, :], 128.0, None, ALU.mult))
            step(V.memset(mv[:, E2:E2 + 1], float(128 * MT2)))
            step(V.tensor_scalar(dl[:, 0:1], mv[:, 0:1], 1.0, None, ALU.mult))
            step(V.tensor_tensor(dl[:, 1:], mv[:, 1:], mv[:, 0:E2], ALU.subtract))
            step(V.tensor_scalar(dl[:, 1:], dl[:, 1:], float(-REG2), None, ALU.add))
            step(V.tensor_scalar(tabe[:, :], fe[:, :], float(E2 - 1), None, ALU.min))
            step(V.scalar_tensor_tensor(out=zb[:, :], in0=m.carry2[:, :], scalar=float(SLOTS2), in1=cview(m, "eoff2", 1),
                                        op0=ALU.add, op1=ALU.add))
            step(V.tensor_copy(zi[:, :], zb[:, :]), table_ready, 1)
            dve.wait_ge(moves_mm, 1)
            step(V.tensor_copy(dls[:, :], tps[0][0:ROWS, 0, 0:E2 + 1]), moves_ready, 1)

            def hidden(i, n):
                dve.wait_ge(th_ready, WAYS * i + (n + 1))
                V.scalar_tensor_tensor(out=th[n][:, :], in0=th[n][:, :], scalar=1.0, in1=gps[n][:, 0, :],
                                       op0=ALU.add, op1=ALU.mult).then_inc(a_ready, 1)
                dve.wait_ge(a_ready, WAYS * i + (n + 1))
                V.tensor_tensor(hh[n][:, :], th[n][:, :], gps[n][:, 1, :], ALU.mult).then_inc(h_ready, 1)

            def transposed(i, n):
                dve.wait_ge(hT_mm, WAYS * i + (n + 1))
                V.tensor_copy(hT[n][:, :, :], tps[n][:, 1:3, :]).then_inc(hT_ready, 1)

            with dve.Fori(1, N + 1) as i:
                for n in range(3):
                    hidden(i, n)
                transposed(i, 0)
                hidden(i, 3)
                transposed(i, 3)


def output_phase(nc, m, d, ctx):
    with ExitStack() as own:
        def sem(name):
            return ctx.enter_context(nc.semaphore("o_" + name))

        def sb(name, shape, dt=F32):
            return [own.enter_context(nc.sbuf_tensor(f"{name}{p}", shape, dt)) for p in two]

        two = range(2)
        NK = 2 * TILES
        sl, wt = sb("o_slots", [ROWS, NK], I32), sb("o_wts", [ROWS, NK])
        ga, o = sb("o_gathered", [ROWS, NK, HID]), sb("o_rows", [ROWS, TILES, HID])
        idx_in, comb, own_o, wt_in = (sem(n) for n in ("idx_in", "comb", "dve", "wt_in"))
        gathered, stored = [sem(f"gathered{p}") for p in two], [sem(f"stored{p}") for p in two]
        block = own.enter_context(nc.Block())

        @block.gpsimd
        def _(pool):
            with pool.Fori(1, PAIRS // 2 + 1) as i:
                for p in two:
                    r = 2 * i + (p - 1)
                    pool.wait_ge(comb, r)
                    nc.gpsimd.tensor_copy(sl[p][:, :], m.slots2[:, bass.ds(r - 1, 1), :].rearrange("p a n -> p (a n)")
                                          ).then_inc(idx_in, 1)
                    pool.wait_ge(idx_in, r)
                    pool.nop(nofuse=True)
                    for n in range(NK):
                        nc.gpsimd.indirect_dma_start(
                            out=ga[p][:, n, :], out_offset=None, in_=d["y2"],
                            in_offset=bass.IndirectOffsetOnAxis(ap=sl[p][:, n:n + 1], axis=0)).then_inc(gathered[p], 16)

        @block.vector
        def _(dve):
            V = nc.vector
            with dve.Fori(1, PAIRS // 2 + 1) as i:
                for p in two:
                    r = 2 * i + (p - 1)
                    step = Steps(dve, own_o, r - 1)
                    step(V.tensor_scalar(wt[p][:, :], m.wts2[:, bass.ds(r - 1, 1), :].rearrange("p a n -> p (a n)"), 1.0,
                                         None, ALU.mult), wt_in, r)
                    dve.wait_ge(gathered[p], i * (16 * NK))
                    dve.wait_ge(stored[p], 32 * i)
                    for n in range(NK):
                        j = n % TILES
                        base = m.hres[:, bass.ds(r - 1, 1), j, :].rearrange("p a c -> p (a c)") if n < TILES else o[p][:, j, :]
                        x = V.scalar_tensor_tensor(out=o[p][:, j, :], in0=ga[p][:, n, :], scalar=wt[p][:, n:n + 1],
                                                   in1=base, op0=ALU.mult, op1=ALU.add)
                        if n == TILES - 1:
                            step(x)
                    x.then_inc(comb, 1)

        @block.sync
        def _(sp):
            sp.sem_inc(comb, 2)
            for p in two:
                sp.sem_inc(stored[p], 32)
            with sp.Fori(1, PAIRS // 2 + 1) as i:
                for p in two:
                    sp.wait_ge(comb, 2 * i + (p + 1))
                    for t in range(2):
                        n = ROWS - t
                        dst = d["out"][bass.ds(4 * i + (2 * p - 4), 2), ROWS * t:ROWS * t + n, :].rearrange("b s c -> s b c")
                        sp.dma_start(dst, o[p][0:n, t::2, :]).then_inc(stored[p], 16)
            for p in two:
                sp.wait_ge(stored[p], 32 * (PAIRS // 2 + 1))


def program(nc, d):
    for k, shape in SCRATCH.items():
        d[k] = nc.dram_tensor("scratch_" + k, shape, F32).ap()
    with ExitStack() as ctx:
        m = memory(nc, ctx)
        for phase in (setup_phase, patch_phase, token_phase, expert_phase, ssm_phase, mixture_phase, output_phase):
            phase(nc, m, d, ctx)

def _layout(inputs):
    f = lambda k: np.asarray(inputs[k])
    a = {}
    x = f("x").reshape(BATCH, CHANS, GRID, PATCH, GRID, PATCH).transpose(0, 2, 4, 1, 3, 5)
    x = x.reshape(BATCH * NPATCH, PDIM)
    xp = np.zeros((BATCH * NPATCH, KCH * 128), x.dtype)
    xp[:, :PDIM] = x
    a["xpat"] = xp.reshape(2 * GROUPS, GB * NPATCH // 2, KCH, 128).transpose(0, 3, 2, 1)
    w = np.zeros((KCH * 128, HID), x.dtype)
    w[:PDIM] = f("L0_tok_W").T
    a["wtok"] = w.reshape(KCH, 128, HID).transpose(1, 0, 2)
    a["tokb"] = f("L0_tok_b")[:, None]
    a["cls"] = f("L0_tok_class_token").T
    a["posT"] = f("L0_tok_pos_embed").T
    a["ytxt"] = f("x_txt").reshape(PAIRS, 2 * NTEXT)
    a["emb"], a["cw"] = f("L0_txt_emb_weight"), f("L0_txt_conv_weight")[:, 0, :]

    def heads(ws, wp):
        ws, wp = ws.reshape(-1, HEADS, HD), wp.reshape(-1, HEADS, NPT)
        o = np.zeros((ws.shape[0], HEADS, 32), ws.dtype)
        o[:, :, 2:2 + HD], o[:, :, 2 + HD:2 + HD + NPT] = ws, wp
        return o.reshape(-1, 2, 128)

    a["wq"] = heads(f("L0_attn_wq"), f("L0_attn_wqp"))
    a["wk"] = heads(f("L0_attn_wk"), f("L0_attn_wkp"))
    a["brow"] = np.concatenate([heads(f("L0_attn_bq")[None], f("L0_attn_bqp")[None]).reshape(1, 256),
                                heads(f("L0_attn_bk")[None], f("L0_attn_bkp")[None]).reshape(1, 256)], axis=1)
    a["wv"], a["wo"] = f("L0_attn_wv"), f("L0_attn_wo")
    a["bv"], a["bo"] = f("L0_attn_bv")[None], f("L0_attn_bo")[None]
    a["lng"], a["lnb"] = f("L0_attn_ln_g")[:, None], f("L0_attn_ln_b")[:, None]
    a["pscale"] = f("L0_attn_pscale")[:, None]
    a["gatew"] = f("L0_ffn_gate_w").T
    a["sw13"] = np.concatenate([f("L0_ffn_sw1"), f("L0_ffn_sw3")], axis=1)
    a["sw2"] = f("L0_ffn_sw2")
    a["w13"] = np.concatenate([f("L0_ffn_w1"), f("L0_ffn_w3")], axis=2)
    a["w2"] = f("L0_ffn_w2")
    a["normw"], a["normb"] = f("L1_attn_norm_weight")[None], f("L1_attn_norm_bias")[None]
    a["ssm"] = np.stack([np.tile(f("L1_attn_" + k), 2) for k in ("lambda_re", "lambda_im", "p_re", "p_im")])[None]
    a["bc"] = np.stack([np.concatenate([f("L1_attn_b_re"), f("L1_attn_b_im")]),
                        np.concatenate([f("L1_attn_c_re"), f("L1_attn_c_im")])], axis=1)
    a["logstep"] = f("L1_attn_log_step").reshape(1, 1)
    a["dsc"] = f("L1_attn_d").reshape(1, 1)
    a["outw"] = np.concatenate([f("L1_attn_out_w").T, f("L1_attn_out2_w").T], axis=1)
    a["outb"] = np.concatenate([f("L1_attn_out_b"), f("L1_attn_out2_b")])[None]
    a["rtw"] = f("L1_ffn_router_w").T
    a["wgu"] = np.concatenate([f("L1_ffn_w_gate"), f("L1_ffn_w_up")], axis=2).transpose(1, 0, 2)
    a["wd"] = f("L1_ffn_w_down").reshape(E2, 2, 128, HID).transpose(2, 0, 1, 3)
    a["cst"] = CONSTS
    return {k: np.ascontiguousarray(v) for k, v in a.items()}


SCRATCH = {"buf1": [SLOTS1, HID], "y1": [SLOTS1 + 128, HID], "buf2": [SLOTS2 + 128, HID],
           "y2": [128 * MT2 + 128, HID], "kpad": [1, SEQ + SEQP]}


def kernel(**inputs):
    import concourse.bacc as bacc
    from concourse.bass_utils import run_bass_kernel_spmd

    nc = bacc.Bacc("TRN2", target_bir_lowering=False, num_devices=1)
    arrays = _layout(inputs)
    d = {k: nc.dram_tensor("in_" + k, v.shape, mybir.dt.from_np(v.dtype), kind="ExternalInput").ap()
         for k, v in arrays.items()}
    d["out"] = nc.dram_tensor("out", [BATCH, SEQ, HID], F32, kind="ExternalOutput").ap()
    program(nc, d)
    r = run_bass_kernel_spmd(nc, [{"in_" + k: v for k, v in arrays.items()}], core_ids=[0])
    return r.results[0]["out"]
```
